# Optimizing a Trainium2 kernel written in Bass

```python
import numpy as np
import jax
import jax.numpy as jnp

def _softmax(x, axis=-1):
    return jax.nn.softmax(x, axis=axis)

def _gelu(x):
    return jax.nn.gelu(x, approximate=True)

def _silu(x):
    return jax.nn.silu(x)

def _sigmoid(x):
    return jax.nn.sigmoid(x)

def _layernorm(x, axis=-1, eps=1e-05):
    m = jnp.mean(x, axis=axis, keepdims=True)
    v = jnp.var(x, axis=axis, keepdims=True)
    return (x - m) / jnp.sqrt(v + eps)

def _scatter_add(tgt, idx, src, axis=0):
    return tgt.at[idx].add(src)

def _segment_sum(src, seg, n):
    return jax.ops.segment_sum(src, seg, n)
kernel_name = 'mk_gps_d2_gnn_r32_aa2be9'

def setup_inputs(seed: int=0):
    np.random.seed(seed)
    _w = jnp.asarray

    def _rec_inputs():
        import jax
        import jax.numpy as jnp
        _gk = jax.random.key(seed)
        x = -0.0003713 + 1 * jax.random.normal(jax.random.fold_in(_gk, 1), (3125, 256), jnp.float32)
        src = jax.random.randint(jax.random.fold_in(_gk, 2), (50000,), 0, 3125, jnp.int32)
        dst = jax.random.randint(jax.random.fold_in(_gk, 3), (50000,), 0, 3125, jnp.int32)
        _o = jnp.argsort(dst, stable=True)
        src = src[_o]
        dst = dst[_o]
        edge_type_8 = jax.random.randint(jax.random.fold_in(_gk, 12), (50000,), 0, 8, jnp.int32)
        return (x, src, dst, edge_type_8)
    x, src, dst, edge_type_8 = _rec_inputs()

    def _L0_gnn_setup():
        import jax, jax.numpy as jnp
        import numpy as np
        N_NODES = 50000
        N_EDGES = 25000
        IN_FEAT = 256
        OUT_FEAT = 256
        NUM_RELS = 8
        ALPHA = 0.5
        key = jax.random.key(seed)
        k1, k2, k3, k4, k5, k6 = jax.random.split(key, 6)
        x = jax.random.normal(k1, (N_NODES, IN_FEAT), dtype=jnp.float32)
        edge_index = jax.random.randint(k2, (2, N_EDGES), 0, N_NODES, dtype=jnp.int64)
        edge_type = jax.random.randint(k3, (N_EDGES,), 0, NUM_RELS, dtype=jnp.int64)
        gain = float(np.sqrt(2.0))
        lim_w = gain * float(np.sqrt(6.0 / (IN_FEAT + OUT_FEAT)))
        weight = jax.random.uniform(k4, (NUM_RELS, IN_FEAT, OUT_FEAT), dtype=jnp.float32, minval=-lim_w, maxval=lim_w)
        loop_weight = jax.random.uniform(k5, (IN_FEAT, OUT_FEAT), dtype=jnp.float32, minval=-lim_w, maxval=lim_w)
        h_bias = jnp.zeros((OUT_FEAT,), dtype=jnp.float32)
        return {'edge_index': edge_index, 'x': x, 'edge_type': edge_type, 'weight': weight, 'h_bias': h_bias, 'loop_weight': loop_weight}
    _L0_gnn_all = _L0_gnn_setup()
    _L0_gnn_in = {k: v for k, v in _L0_gnn_all.items() if k in ('weight', 'h_bias', 'loop_weight')}
    del _L0_gnn_all

    def _L0_mix_setup():
        import jax, jax.numpy as jnp
        import numpy as np
        DIM = 256
        HEADS = 4
        DIM_HEAD = 32
        NUM_MEM = 4
        HIDDEN = HEADS * DIM_HEAD
        SCALE = DIM_HEAD ** (-0.5)

        def rmsnorm(x, g):
            n = jnp.linalg.norm(x, axis=-1, keepdims=True)
            return x / jnp.maximum(n, 1e-12) * g * x.shape[-1] ** 0.5
        key = jax.random.key(seed)
        ks = jax.random.split(key, 8)
        B, N = (4, 512)
        return {'x': jax.random.normal(ks[0], (B, N, DIM), jnp.float32), 't': jax.random.normal(ks[1], (B,), jnp.float32), 'w_qkv': jax.random.normal(ks[2], (DIM, 3 * HIDDEN), jnp.float32) * 0.02, 'mem_kv': jax.random.normal(ks[3], (2, HEADS, DIM_HEAD, NUM_MEM), jnp.float32), 'w_out': jax.random.normal(ks[4], (HIDDEN, DIM), jnp.float32) * 0.02, 'b_out': jnp.zeros((DIM,), jnp.float32), 'g_out': jnp.ones((DIM,), jnp.float32), 'g_pre': jnp.ones((DIM,), jnp.float32)}
    _L0_mix_all = _L0_mix_setup()
    _L0_mix_in = {k: v for k, v in _L0_mix_all.items() if k in ('t', 'w_qkv', 'mem_kv', 'w_out', 'b_out', 'g_out', 'g_pre')}
    del _L0_mix_all

    def _L0_ffn_setup():
        import jax, jax.numpy as jnp
        import numpy as np
        D_MODEL = 256
        EXPERT_DIM = 512
        NUM_EXPERTS = 8
        TOP_K = 2
        SEQ_LEN = 64
        BATCH = 2
        key = jax.random.key(seed)
        ks = jax.random.split(key, 8)
        s = 0.02
        x = jax.random.normal(ks[0], (SEQ_LEN, BATCH, D_MODEL), dtype=jnp.float32)
        Wg = jax.random.normal(ks[1], (D_MODEL, NUM_EXPERTS), dtype=jnp.float32) * s
        bg = jax.random.normal(ks[2], (NUM_EXPERTS,), dtype=jnp.float32) * s
        bias = jnp.zeros((NUM_EXPERTS,), dtype=jnp.float32)
        W1 = jax.random.normal(ks[3], (NUM_EXPERTS, D_MODEL, EXPERT_DIM), dtype=jnp.float32) * s
        b1 = jax.random.normal(ks[4], (NUM_EXPERTS, EXPERT_DIM), dtype=jnp.float32) * s
        W2 = jax.random.normal(ks[5], (NUM_EXPERTS, EXPERT_DIM, D_MODEL), dtype=jnp.float32) * s
        b2 = jax.random.normal(ks[6], (NUM_EXPERTS, D_MODEL), dtype=jnp.float32) * s
        return {'x': x, 'Wg': Wg, 'bg': bg, 'bias': bias, 'W1': W1, 'b1': b1, 'W2': W2, 'b2': b2}
    _L0_ffn_all = _L0_ffn_setup()
    _L0_ffn_in = {k: v for k, v in _L0_ffn_all.items() if k in ('Wg', 'bg', 'bias', 'W1', 'b1', 'W2', 'b2')}
    del _L0_ffn_all

    def _L1_gnn_setup():
        import jax, jax.numpy as jnp
        import numpy as np
        NUM_NODES = 1250
        NUM_REL = 8
        NUM_BASES = 4
        EMB = 256
        NUM_LAYERS = 3
        NUM_EDGES = 20000

        def _rgcn_layer(x, src, seg, inv_cnt, comp, basis, root, bias):
            N, D = x.shape
            R = comp.shape[0]
            W = jnp.einsum('rb,bio->rio', comp, basis)
            agg = jax.ops.segment_sum(x[src], seg, num_segments=R * N) * inv_cnt
            agg = agg.reshape(R, N, D)
            out = jnp.einsum('rni,rio->no', agg, W) + x @ root + bias
            return out
        key = jax.random.key(seed)
        ks = jax.random.split(key, 7)
        edge_index = jax.random.randint(ks[0], (2, NUM_EDGES), 0, NUM_NODES)
        edge_type = jax.random.randint(ks[1], (NUM_EDGES,), 0, NUM_REL)
        embeddings = jax.random.normal(ks[2], (NUM_NODES, EMB), dtype=jnp.float32)
        scale = 1.0 / np.sqrt(EMB)
        comps = jax.random.normal(ks[3], (NUM_LAYERS, NUM_REL, NUM_BASES), dtype=jnp.float32) * scale
        bases = jax.random.normal(ks[4], (NUM_LAYERS, NUM_BASES, EMB, EMB), dtype=jnp.float32) * scale
        roots = jax.random.normal(ks[5], (NUM_LAYERS, EMB, EMB), dtype=jnp.float32) * scale
        biases = jnp.zeros((NUM_LAYERS, EMB), dtype=jnp.float32)
        return {'edge_index': edge_index, 'edge_type': edge_type, 'embeddings': embeddings, 'comps': comps, 'bases': bases, 'roots': roots, 'biases': biases}
    _L1_gnn_all = _L1_gnn_setup()
    _L1_gnn_in = {k: v for k, v in _L1_gnn_all.items() if k in ('comps', 'bases', 'roots', 'biases')}
    del _L1_gnn_all

    def _L1_mix_setup():
        import jax, jax.numpy as jnp
        import numpy as np
        HEADS = 8
        DIM_HEAD = 64
        EPS = 1e-05

        def _inst_norm(t):
            mu = jnp.mean(t, axis=-1, keepdims=True)
            var = jnp.var(t, axis=-1, keepdims=True)
            return (t - mu) / jnp.sqrt(var + EPS)
        key = jax.random.key(seed)
        k1, k2, k3, k4 = jax.random.split(key, 4)
        b, n, dim = (4, 256, 256)
        inner = HEADS * DIM_HEAD
        x = jax.random.normal(k1, (b, n, dim), dtype=jnp.float32)
        w_qkv = jax.random.normal(k2, (dim, 3 * inner), dtype=jnp.float32) * (1.0 / DIM_HEAD)
        w_out = jax.random.normal(k3, (inner, dim), dtype=jnp.float32) * dim ** (-0.5)
        b_out = jax.random.normal(k4, (dim,), dtype=jnp.float32) * 0.01
        return {'x': x, 'w_qkv': w_qkv, 'w_out': w_out, 'b_out': b_out}
    _L1_mix_all = _L1_mix_setup()
    _L1_mix_in = {k: v for k, v in _L1_mix_all.items() if k in ('w_qkv', 'w_out', 'b_out')}
    del _L1_mix_all

    def _L1_ffn_setup():
        import jax, jax.numpy as jnp
        import numpy as np
        TOP_K = 2
        LN_EPS = 1e-05
        key = jax.random.key(seed)
        ks = jax.random.split(key, 8)
        B, S, D, E, H = (16, 1024, 256, 8, 1024)
        x = jax.random.normal(ks[0], (B, S, D), dtype=jnp.float32)
        Wr = jax.random.normal(ks[1], (D, E), dtype=jnp.float32) * 0.1
        br = jnp.zeros((E,), dtype=jnp.float32)
        ln_g = jnp.ones((E, D), dtype=jnp.float32)
        ln_b = jnp.zeros((E, D), dtype=jnp.float32)
        W1 = jax.random.normal(ks[2], (E, D, H), dtype=jnp.float32) * (1.0 / np.sqrt(D))
        b1 = jnp.zeros((E, H), dtype=jnp.float32)
        W2 = jax.random.normal(ks[3], (E, H, D), dtype=jnp.float32) * (1.0 / np.sqrt(H))
        b2 = jnp.zeros((E, D), dtype=jnp.float32)
        return {'x': x, 'Wr': Wr, 'br': br, 'ln_g': ln_g, 'ln_b': ln_b, 'W1': W1, 'b1': b1, 'W2': W2, 'b2': b2}
    _L1_ffn_all = _L1_ffn_setup()
    _L1_ffn_in = {k: v for k, v in _L1_ffn_all.items() if k in ('Wr', 'br', 'ln_g', 'ln_b', 'W1', 'b1', 'W2', 'b2')}
    del _L1_ffn_all
    return {'x': x, 'src': src, 'dst': dst, 'edge_type_8': edge_type_8, 'L0_gnn_weight': _L0_gnn_in['weight'], 'L0_gnn_h_bias': _L0_gnn_in['h_bias'], 'L0_gnn_loop_weight': _L0_gnn_in['loop_weight'], 'L0_mix_t': _L0_mix_in['t'], 'L0_mix_w_qkv': _L0_mix_in['w_qkv'], 'L0_mix_mem_kv': _L0_mix_in['mem_kv'], 'L0_mix_w_out': _L0_mix_in['w_out'], 'L0_mix_b_out': _L0_mix_in['b_out'], 'L0_mix_g_out': _L0_mix_in['g_out'], 'L0_mix_g_pre': _L0_mix_in['g_pre'], 'L0_ffn_Wg': _L0_ffn_in['Wg'], 'L0_ffn_bg': _L0_ffn_in['bg'], 'L0_ffn_bias': _L0_ffn_in['bias'], 'L0_ffn_W1': _L0_ffn_in['W1'], 'L0_ffn_b1': _L0_ffn_in['b1'], 'L0_ffn_W2': _L0_ffn_in['W2'], 'L0_ffn_b2': _L0_ffn_in['b2'], 'L1_gnn_comps': _L1_gnn_in['comps'], 'L1_gnn_bases': _L1_gnn_in['bases'], 'L1_gnn_roots': _L1_gnn_in['roots'], 'L1_gnn_biases': _L1_gnn_in['biases'], 'L1_mix_w_qkv': _L1_mix_in['w_qkv'], 'L1_mix_w_out': _L1_mix_in['w_out'], 'L1_mix_b_out': _L1_mix_in['b_out'], 'L1_ffn_Wr': _L1_ffn_in['Wr'], 'L1_ffn_br': _L1_ffn_in['br'], 'L1_ffn_ln_g': _L1_ffn_in['ln_g'], 'L1_ffn_ln_b': _L1_ffn_in['ln_b'], 'L1_ffn_W1': _L1_ffn_in['W1'], 'L1_ffn_b1': _L1_ffn_in['b1'], 'L1_ffn_W2': _L1_ffn_in['W2'], 'L1_ffn_b2': _L1_ffn_in['b2']}

def reference(x, src, dst, edge_type_8, L0_gnn_weight, L0_gnn_h_bias, L0_gnn_loop_weight, L0_mix_t, L0_mix_w_qkv, L0_mix_mem_kv, L0_mix_w_out, L0_mix_b_out, L0_mix_g_out, L0_mix_g_pre, L0_ffn_Wg, L0_ffn_bg, L0_ffn_bias, L0_ffn_W1, L0_ffn_b1, L0_ffn_W2, L0_ffn_b2, L1_gnn_comps, L1_gnn_bases, L1_gnn_roots, L1_gnn_biases, L1_mix_w_qkv, L1_mix_w_out, L1_mix_b_out, L1_ffn_Wr, L1_ffn_br, L1_ffn_ln_g, L1_ffn_ln_b, L1_ffn_W1, L1_ffn_b1, L1_ffn_W2, L1_ffn_b2):
    import jax
    import jax.numpy as jnp

    def _L0_gnn_ref(edge_index, x, edge_type, weight, h_bias, loop_weight):
        import jax, jax.numpy as jnp
        import numpy as np
        N_NODES = 50000
        N_EDGES = 25000
        IN_FEAT = 256
        OUT_FEAT = 256
        NUM_RELS = 8
        ALPHA = 0.5
        num_nodes = x.shape[0]
        src, dst = (edge_index[0], edge_index[1])
        hx = jnp.einsum('ni,rio->rno', x, weight)
        msg = hx[edge_type, src]
        agg = jax.ops.segment_sum(msg, dst, num_segments=num_nodes)
        node_repr = agg * jnp.asarray(ALPHA, x.dtype) ** 0.5
        node_repr = node_repr + h_bias
        loop_message = x @ loop_weight
        node_repr = node_repr + loop_message * jnp.asarray(1.0 - ALPHA, x.dtype) ** 0.5
        return node_repr

    def _L0_mix_ref(x, t, w_qkv, mem_kv, w_out, b_out, g_out, g_pre):
        import jax, jax.numpy as jnp
        import numpy as np
        DIM = 256
        HEADS = 4
        DIM_HEAD = 32
        NUM_MEM = 4
        HIDDEN = HEADS * DIM_HEAD
        SCALE = DIM_HEAD ** (-0.5)

        def rmsnorm(x, g):
            n = jnp.linalg.norm(x, axis=-1, keepdims=True)
            return x / jnp.maximum(n, 1e-12) * g * x.shape[-1] ** 0.5
        b, n, c = x.shape
        xn = rmsnorm(x, g_pre)
        qkv = xn @ w_qkv
        q, k, v = jnp.split(qkv, 3, axis=-1)

        def to_heads(z):
            return z.reshape(b, n, HEADS, DIM_HEAD).transpose(0, 2, 3, 1)
        q, k, v = map(to_heads, (q, k, v))
        mk = jnp.broadcast_to(mem_kv[0], (b, HEADS, DIM_HEAD, NUM_MEM))
        mv = jnp.broadcast_to(mem_kv[1], (b, HEADS, DIM_HEAD, NUM_MEM))
        k = jnp.concatenate([mk, k], axis=-1)
        v = jnp.concatenate([mv, v], axis=-1)
        q = jax.nn.softmax(q, axis=-2) * SCALE
        k = jax.nn.softmax(k, axis=-1)
        context = jnp.einsum('bhdn,bhen->bhde', k, v)
        out = jnp.einsum('bhde,bhdn->bhen', context, q)
        out = out.transpose(0, 3, 1, 2).reshape(b, n, HIDDEN)
        out = rmsnorm(out @ w_out + b_out, g_out)
        return out + x

    def _L0_ffn_ref(x, Wg, bg, bias, W1, b1, W2, b2):
        import jax, jax.numpy as jnp
        import numpy as np
        D_MODEL = 256
        EXPERT_DIM = 512
        NUM_EXPERTS = 8
        TOP_K = 2
        SEQ_LEN = 64
        BATCH = 2
        x_flat = x.reshape(-1, D_MODEL)
        gate_logits = x_flat @ Wg + bg + bias
        topk_vals, topk_idx = jax.lax.top_k(gate_logits, TOP_K)
        topk_w = jax.nn.softmax(topk_vals, axis=-1)
        combine = (jax.nn.one_hot(topk_idx, NUM_EXPERTS, dtype=x.dtype) * topk_w[..., None]).sum(axis=1)
        h = jax.nn.relu(jnp.einsum('td,edh->teh', x_flat, W1) + b1)
        y = jnp.einsum('teh,ehd->ted', h, W2) + b2
        out = jnp.einsum('ted,te->td', y, combine)
        return out.reshape(x.shape)

    def _L1_gnn_ref(edge_index, edge_type, embeddings, comps, bases, roots, biases):
        import jax, jax.numpy as jnp
        import numpy as np
        NUM_NODES = 1250
        NUM_REL = 8
        NUM_BASES = 4
        EMB = 256
        NUM_LAYERS = 3
        NUM_EDGES = 20000

        def _rgcn_layer(x, src, seg, inv_cnt, comp, basis, root, bias):
            N, D = x.shape
            R = comp.shape[0]
            W = jnp.einsum('rb,bio->rio', comp, basis)
            agg = jax.ops.segment_sum(x[src], seg, num_segments=R * N) * inv_cnt
            agg = agg.reshape(R, N, D)
            out = jnp.einsum('rni,rio->no', agg, W) + x @ root + bias
            return out
        src, dst = (edge_index[0], edge_index[1])
        N = embeddings.shape[0]
        R = comps.shape[1]
        seg = edge_type * N + dst
        cnt = jax.ops.segment_sum(jnp.ones_like(seg, dtype=embeddings.dtype), seg, num_segments=R * N)
        inv_cnt = (1.0 / jnp.maximum(cnt, 1.0))[:, None]
        x = _rgcn_layer(embeddings, src, seg, inv_cnt, comps[0], bases[0], roots[0], biases[0])
        for i in range(1, NUM_LAYERS - 1):
            x = _rgcn_layer(jax.nn.relu(x), src, seg, inv_cnt, comps[i], bases[i], roots[i], biases[i])
        return x

    def _L1_mix_ref(x, w_qkv, w_out, b_out):
        import jax, jax.numpy as jnp
        import numpy as np
        HEADS = 8
        DIM_HEAD = 64
        EPS = 1e-05

        def _inst_norm(t):
            mu = jnp.mean(t, axis=-1, keepdims=True)
            var = jnp.var(t, axis=-1, keepdims=True)
            return (t - mu) / jnp.sqrt(var + EPS)
        b, n, dim = x.shape
        qkv = x @ w_qkv
        q, k, v = jnp.split(qkv, 3, axis=-1)
        to_heads = lambda t: t.reshape(b, n, HEADS, DIM_HEAD).transpose(0, 2, 1, 3)
        q, k, v = (to_heads(q), to_heads(k), to_heads(v))
        k = _inst_norm(k)
        v = _inst_norm(v)
        dots = jnp.einsum('bhnd,bhne->bhde', k, v)
        out = jnp.einsum('bhnd,bhde->bhne', q, dots) * (1.0 / n)
        out = out.transpose(0, 2, 1, 3).reshape(b, n, HEADS * DIM_HEAD)
        return out @ w_out + b_out

    def _L1_ffn_ref(x, Wr, br, ln_g, ln_b, W1, b1, W2, b2):
        import jax, jax.numpy as jnp
        import numpy as np
        TOP_K = 2
        LN_EPS = 1e-05
        B, S, D = x.shape
        N = B * S
        xt = x.reshape(N, D)
        logits = xt @ Wr + br
        probs = jax.nn.softmax(logits, axis=-1)
        top_p, top_idx = jax.lax.top_k(probs, TOP_K)
        weights = top_p / top_p.sum(axis=-1, keepdims=True)
        mu = xt.mean(axis=-1, keepdims=True)
        var = ((xt - mu) ** 2).mean(axis=-1, keepdims=True)
        xn = (xt - mu) * jax.lax.rsqrt(var + LN_EPS)
        xe = xn[None, :, :] * ln_g[:, None, :] + ln_b[:, None, :]
        h = jax.nn.gelu(jnp.einsum('end,edh->enh', xe, W1) + b1[:, None, :], approximate=False)
        y = jnp.einsum('enh,ehd->end', h, W2) + b2[:, None, :]
        y_tok = jnp.transpose(y, (1, 0, 2))
        sel = jnp.take_along_axis(y_tok, top_idx[:, :, None], axis=1)
        out = (weights[:, :, None] * sel).sum(axis=1)
        return out.reshape(B, S, D)
    edge_index = jnp.stack([src, dst])
    xn = _layernorm(x, axis=-1)
    x = x + _L0_gnn_ref(edge_index, xn, edge_type_8, L0_gnn_weight, L0_gnn_h_bias, L0_gnn_loop_weight) + _L0_mix_ref(xn[None], L0_mix_t, L0_mix_w_qkv, L0_mix_mem_kv, L0_mix_w_out, L0_mix_b_out, L0_mix_g_out, L0_mix_g_pre)[0]
    x = x + _L0_ffn_ref(_layernorm(x, axis=-1)[None], L0_ffn_Wg, L0_ffn_bg, L0_ffn_bias, L0_ffn_W1, L0_ffn_b1, L0_ffn_W2, L0_ffn_b2)[0]
    xn = _layernorm(x, axis=-1)
    x = x + _L1_gnn_ref(edge_index, edge_type_8, xn, L1_gnn_comps, L1_gnn_bases, L1_gnn_roots, L1_gnn_biases) + _L1_mix_ref(xn[None], L1_mix_w_qkv, L1_mix_w_out, L1_mix_b_out)[0]
    x = x + _L1_ffn_ref(_layernorm(x, axis=-1)[None], L1_ffn_Wr, L1_ffn_br, L1_ffn_ln_g, L1_ffn_ln_b, L1_ffn_W1, L1_ffn_b1, L1_ffn_W2, L1_ffn_b2)[0]
    return x

_drawn_inputs = setup_inputs


def setup_inputs(seed=0):
    import zlib

    import numpy as np

    out = dict(_drawn_inputs(seed))
    spreads = {'L0_gnn_h_bias': (0.0, 0.314),
     'L0_mix_b_out': (0.0, 0.1),
     'L0_mix_g_out': (1.0, 0.2),
     'L0_mix_g_pre': (1.0, 0.6),
     'L0_ffn_bias': (0.0, 0.64),
     'L1_gnn_biases': (0.0, 0.27),
     'L1_ffn_br': (0.0, 0.465),
     'L1_ffn_ln_g': (1.0, 0.6),
     'L1_ffn_ln_b': (0.0, 0.691),
     'L1_ffn_b1': (0.0, 0.719),
     'L1_ffn_b2': (0.0, 0.493)}
    factors = {'L0_mix_w_qkv': 8.0,
     'L0_mix_mem_kv': 8.0,
     'L0_mix_w_out': 8.0,
     'L0_ffn_Wg': 3.729,
     'L0_ffn_bg': 8.0,
     'L0_ffn_W1': 3.871,
     'L0_ffn_b1': 8.0,
     'L0_ffn_W2': 3.209,
     'L0_ffn_b2': 8.0,
     'L1_mix_b_out': 26.083}
    for name, (base, spread) in spreads.items():
        noise = np.random.default_rng([zlib.crc32(name.encode()), seed]).standard_normal(out[name].shape)
        drawn = base * np.exp(spread * noise) if base else spread * noise
        out[name] = jnp.asarray(drawn.astype(out[name].dtype))
    for name, factor in factors.items():
        out[name] = (out[name] * factor).astype(out[name].dtype)
    return out
```

```python
import concourse.bass as bass
from concourse import mybir
from contextlib import ExitStack

F32 = mybir.dt.float32
I32 = mybir.dt.int32
ALU = mybir.AluOpType
ACT = mybir.ActivationFunctionType
X = mybir.AxisListType.X

NODES, D = 3125, 256
P = 125
T = NODES // P
U = 5
TI = T // U
KC = D // 128
R = 8
EDGES = 50000
EC = EDGES // P
GROUP = 256
GROUPS = (EDGES + T * (GROUP - 1)) // GROUP
GU = 4
GROUPS = -(-GROUPS // GU) * GU
CH = GROUP // 128
COLS = GROUPS * CH
PADC = GU * CH
NE = 8
SLOT = 256
SLOTS = (2 * NODES + NE * (SLOT - 1)) // SLOT
SLOTS += SLOTS % 2
EPS = 1e-5
SCU = 8


class Chain:

    def __init__(self, eng, sem):
        self.eng, self.sem, self.n, self.base = eng, sem, 0, 0

    def __call__(self, ins):
        self.step(ins)
        self.wait()

    def step(self, ins):
        ins.then_inc(self.sem, 1)
        self.n += 1

    def wait(self):
        self.eng.wait_ge(self.sem, self.n)

    def loop(self, i, steps):
        self.base = self.n
        self.n = self.base + i * steps

    def end(self, rounds, steps):
        self.n = self.base + rounds * steps


def gps_block(nc, x_in, src, dst, etype, w0, hb0, wl0, t0, wqkv0, memkv, wout0, bout0, gout0, gpre0,
              f0_wg, f0_bg, f0_bias, f0_w1, f0_b1, f0_w2, f0_b2, comps, bases, roots, biases,
              wqkv1, wout1, bout1, f1_wr, f1_br, f1_g, f1_b, f1_w1, f1_b1, f1_w2, f1_b2, out):
    ctx = ExitStack()
    with ctx:
        def sb(name, shape, dt=F32):
            return ctx.enter_context(nc.sbuf_tensor(name, shape, dt))

        def sem(name):
            return ctx.enter_context(nc.semaphore(name))

        def dram(name, shape, dt=F32):
            return nc.dram_tensor(name, shape, dt, kind="Internal").ap()

        hx_d = dram("hx_d", [R * NODES, D])
        rec_d = dram("rec_d", [128 * COLS, 4], I32)
        inv_d = dram("inv_d", [NODES * R, 1])
        xs_d = dram("xs_d", [SLOTS * SLOT, D])
        ys_d = dram("ys_d", [SLOTS * SLOT, D])

        x = sb("x", [P, T, D])
        xn = sb("xn", [P, T, D])
        accb = sb("accb", [128, T * D])
        tmpb = sb("tmpb", [128, T * D])
        acc = accb[0:P, :].rearrange("p (t d) -> p t d", d=D)
        tmp = tmpb[0:P, :].rearrange("p (t d) -> p t d", d=D)
        wcat = sb("wcat", [128, KC, (R + 1) * D])
        hst = sb("hst", [P, 2, R, D])
        stage = sb("stage", [P, U, D])
        xT = sb("xT", [128, U, KC, P])
        G = sb("G", [128, GU, CH, D])
        wq0 = G[:, 0:KC, :, :].rearrange("p k c d -> p k (c d)")[:, :, 0:384]
        oh = sb("oh", [128, GU, CH, P])
        moe = sb("moe", [128, 5 * EC + T * 129])
        hT = moe[:, 0:2048].rearrange("p (j s) -> p j s", s=SLOT)
        xsr = [moe[:, 2048 + 512 * a:2560 + 512 * a].rearrange("p (a d) -> p a d", d=D) for a in range(2)]
        xsT = [moe[:, 3072 + 512 * a:3584 + 512 * a].rearrange("p (k s) -> p k s", s=SLOT) for a in range(2)]
        ysb = [moe[:, 4096 + 512 * a:4608 + 512 * a].rearrange("p (a d) -> p a d", d=D) for a in range(2)]
        b2c = sb("b2c", [128, 2, D])
        par = sb("par", [12, 2, 128])
        parT = sb("parT", [128, 2, 12])
        vv = moe[0:P, 5 * EC:5 * EC + T * 129].rearrange("p (t n) -> p t n", n=129)
        rec = moe[0:P, 0:4 * EC].bitcast(I32).rearrange("p (c f) -> p c f", f=4)
        posi = moe[0:P, 4 * EC:5 * EC].bitcast(I32)
        SA = [accb[0:P, EC * n:EC * (n + 1)] for n in range(9)]
        recs = moe[:, 0:4 * COLS].bitcast(I32).rearrange("p (c f) -> p c f", f=4)
        unused = tmpb[:, 8 * D:8 * D + 4 * COLS].bitcast(I32).rearrange("p (c f) -> p c f", f=4)
        gid = sb("gid", [128, COLS], I32)
        seg = sb("seg", [128, COLS], I32)
        dstl = sb("dstl", [128, COLS + PADC])
        inv = sb("inv", [128, COLS + PADC])
        toh = tmpb[:, 0:COLS * R].rearrange("p (c r) -> p c r", r=R)
        cnt = sb("cnt", [P, T, R])
        gixs = sb("gixs", [128, GU, CH], I32)
        scix = sb("scix", [P, 2, SCU], I32)
        scrc = sb("scrc", [P, 2, SCU, 4], I32)
        mix = sb("mix", [P, 2, U], I32)
        binr = sb("binr", [1, GROUPS + GU], I32)
        eidr = sb("eidr", [1, 2, SLOTS], I32)
        ident = sb("ident", [128, 128])
        ones = sb("ones", [128, 128])
        tri = sb("tri", [128, 128])
        iota = sb("iota", [128, GROUPS + 4])
        bmask = sb("bmask", [128, 128])
        bmask1 = sb("bmask1", [128, 128])
        ltm = sb("ltm", [P, NE, NE])
        bc = sb("bc", [128, 6, D])
        compb = sb("compb", [128, 2, 32])
        gatb = sb("gatb", [P, 4, NE])
        gpre = sb("gpre", [128, KC])
        memk = sb("memk", [4, 128])
        memv = sb("memv", [4, 129])
        wo0 = sb("wo0", [128, D])
        wg = sb("wg", [128, 2, KC, NE])
        sm = sb("sm", [128, 1160])
        lg = sb("lg", [P, T, NE])
        stf = stage[:, :, :].rearrange("p u d -> p (u d)")
        rk = stf[:, 0:T * NE].rearrange("p (t e) -> p t e", e=NE)
        scn = stf[:, T * NE:2 * T * NE].rearrange("p (t e) -> p t e", e=NE)
        sel = stf[:, 2 * T * NE:5 * T * NE].rearrange("p (m t e) -> p m t e", e=NE, t=T)
        pw = sb("pw", [P, 2, T])
        pwi = sb("pwi", [P, 2, T], I32)
        yg = hst[:, 0, :, :].rearrange("p (a b) d -> p a b d", a=4)
        big = tmpb[0:P, 0:T * NE * NE].rearrange("p (t e j) -> p t e j", e=NE, j=NE)
        big2 = tmpb[0:P, T * NE * NE:2 * T * NE * NE].rearrange("p (t e j) -> p t e j", e=NE, j=NE)
        mu = sm[0:P, 0:T]
        va = sm[0:P, 32:32 + T]
        r0 = sm[0:P, 64:64 + T]
        tot = sm[0:P, 96:96 + T]
        off = sm[0:P, 128:128 + T]
        tt = sm[0:P, 160:160 + T]
        tti = sm[0:P, 192:192 + T].bitcast(I32)
        bs = sm[0:P, 224:224 + T]
        onec = ones[0:P, 0:1]
        var = sm[0:P, 356:372]
        rkv = sm[0:P, 372:380]
        qs = sm[0:P, 256:356]
        kmx = sm[0:P, 384:512]
        mcol = sm[:, 512:513]
        rden = sm[:, 513:514]
        dg = sm[:, 520:648]
        ctxs = sm[:, 648:776]
        ctxT = sm[:, 776:904]
        M0 = sm[:, 904:1160]

        ivs = sb("ivs", [128, GU * CH])
        dT = moe[:, 3584:4096].rearrange("p (j c) -> p j c", j=4)
        zer = moe[:, 5 * EC:5 * EC + 512]
        kt = hst[:, 0, 0:4, :].rearrange("p (z a) d -> p z (a d)", z=2)
        vt = hst[:, 0, 4:8, :].rearrange("p (z a) d -> p z (a d)", z=2)
        sqv = hst[:, 1, 0:4, :].rearrange("p a d -> p (a d)")
        M1 = moe[:, 0:1024].rearrange("p (j d) -> p j d", d=D)
        wqT = moe[:, 1024:2048].rearrange("p (k j c) -> p k j c", k=KC, j=4)

        pb = [ctx.enter_context(nc.psum_tensor(f"pb{i}", [128, 512], F32)) for i in range(8)]

        s_vec = sem("s_vec")
        s_act = sem("s_act")
        s_pool = sem("s_pool")
        s_xin = sem("s_xin")
        s_edge = sem("s_edge")
        s_par = sem("s_par")
        s_w0 = sem("s_w0")
        s_const = sem("s_const")
        s_zero = sem("s_zero")
        s_zd = sem("s_zd")
        s_lnc = sem("s_lnc")
        s_sq = sem("s_sq")
        s_ln = sem("s_ln")
        s_stg = sem("s_stg")
        s_trn = sem("s_trn")
        s_xT = sem("s_xT")
        s_blk = sem("s_blk")
        s_eva = [sem(f"s_ev{j}") for j in range(6)]
        s_hst = [sem(f"s_hst{j}") for j in range(2)]
        s_pos = sem("s_pos")
        s_cst = sem("s_cst")
        s_sct = [sem(f"s_sct{j}") for j in range(2)]
        s_recl = sem("s_recl")
        s_srt = sem("s_srt")
        s_gix = sem("s_gix")
        s_G = [sem(f"s_G{j}") for j in range(GU)]
        s_oh = [sem(f"s_oh{j}") for j in range(GU)]
        s_sg = [sem(f"s_sg{j}") for j in range(GU)]
        s_acc = sem("s_acc")
        s_inv = sem("s_inv")
        s_ivd = sem("s_ivd")
        s_ivg = sem("s_ivg")
        s_q = sem("s_q")
        s_v2p = sem("s_v2p")
        s_v2a = sem("s_v2a")
        s_a2v = sem("s_a2v")
        s_dot = sem("s_dot")
        s_w1l = sem("s_w1l")
        s_wm = sem("s_wm")
        s_cmb = sem("s_cmb")
        s_rt = sem("s_rt")
        s_dsp = sem("s_dsp")
        s_dix = sem("s_dix")
        s_dst = [sem(f"s_dst{j}") for j in range(U)]
        s_mw = [sem(f"s_mw{j}") for j in range(2)]
        s_mt = sem("s_mt")
        s_mx = sem("s_mx")
        s_mh = sem("s_mh")
        s_ma = sem("s_ma")
        s_my = [sem(f"s_my{j}") for j in range(2)]
        s_mo = [sem(f"s_mo{j}") for j in range(2)]
        s_ys = [sem(f"s_ys{j}") for j in range(2)]
        s_cix = sem("s_cix")
        s_cg = [sem(f"s_cg{j}") for j in range(2)]
        s_cmbd = sem("s_cmbd")
        s_out = sem("s_out")
        s_ivc = sem("s_ivc")
        s_rsv = sem("s_rsv")
        s_rsa = sem("s_rsa")
        s_turn = sem("s_turn")
        s_turn_sp = sem("s_turn_sp")
        s_dt = sem("s_dt")
        s_sqf = sem("s_sqf")
        s_sqk = sem("s_sqk")
        s_vw = sem("s_vw")
        s_mp = sem("s_mp")
        s_cm1 = sem("s_cm1")

        def row(ap, n=128):
            return ap.partition_broadcast(n)

        hx_v = hx_d.rearrange("(r t p) d -> t p r d", r=R, p=P)
        rec_v = rec_d.rearrange("(p c) f -> p c f", p=128)
        xs_z = xs_d.rearrange("(n p a) d -> n p (a d)", n=SLOTS // 4, p=128)
        x_v = x_in.rearrange("(t p) d -> p t d", p=P)
        out_v = out.rearrange("(t p) d -> p t d", p=P)
        NEV = [0, 0, 0, 0, 0, 0]

        w_hx = [(wcat[:, :, 512 * j:512 * (j + 1)], "av"[j % 2]) for j in range(4)]
        w_loop = [(wcat[:, :, R * D:(R + 1) * D], "v")]
        wkv = wcat[:, :, 0:1024]
        PASSES = {}

        def tile_pass(name, nk, blocks):
            k = len(PASSES)
            inst = dict(k=k, nk=nk, blocks=blocks, ev=[NEV[j] for j in range(len(blocks))],
                        blk=sum(len(q["blocks"]) * T for q in PASSES.values()))
            for j in range(len(blocks)):
                NEV[j] += T
            PASSES[name] = inst

        M0v = M0.rearrange("p (k n) -> p k n", k=1)
        P1v = moe[:, 3072:3584].rearrange("p (k d) -> p k d", d=D)
        tile_pass("gnn0", KC, w_hx + w_loop + [(wq0[:, :, :], "v")])
        tile_pass("mix0", 1, [(M0v, "v")])
        tile_pass("gate0", KC, [(wg[:, 0, :, :], "v")])
        tile_pass("gnn1", KC, w_hx + w_loop)
        tile_pass("kv1", KC, [(wkv[:, :, 0:512], "v"), (wkv[:, :, 512:1024], "a")])
        tile_pass("mix1", KC, [(P1v[:, :, :], "v")])
        tile_pass("gnn2", KC, w_hx + w_loop)
        tile_pass("gate1", KC, [(wg[:, 1, :, :], "v")])
        HSTN = {"gnn0": 0, "gnn1": 1, "gnn2": 2}

        def pass_act(act, name, source, evac=None):
            q = PASSES[name]
            k0, nk, nb = q["k"] * T, q["nk"], len(q["blocks"])
            with act.Fori(0, TI) as i:
                act.wait_ge(s_trn, k0 + i * U)
                for s in range(U):
                    nc.scalar.activation(stage[:, s, 0:nk * 128], source(i * U + s), ACT.Copy).then_inc(s_stg, 1)
                for s in range(U):
                    t = i * U + s
                    act.wait_ge(s_trn, k0 + t + 1)
                    act.wait_ge(s_blk, q["blk"] + nb * U * i)
                    nc.scalar.activation(xT[:, s, 0:nk, :], pb[6 + s % 2][:, 0:nk * P].rearrange(
                        "p (k n) -> p k n", n=P), ACT.Copy).then_inc(s_xT, 1)
                    for j, (_, e) in enumerate(q["blocks"]):
                        if e == "a":
                            act.wait_ge(s_blk, q["blk"] + nb * t + j + 1)
                            evac(act, i, s, j)

        def pass_pe(pe, name, more=None):
            q = PASSES[name]
            k0, nk, nb = q["k"] * T, q["nk"], len(q["blocks"])

            def transposes(i, s):
                t = i * U + s
                pe.wait_ge(s_stg, k0 + t + 1)
                if s >= 2:
                    pe.wait_ge(s_xT, k0 + t - 1)
                else:
                    pe.wait_ge(s_xT, k0 + i * U)
                for k in range(nk):
                    last = nc.tensor.transpose(pb[6 + s % 2][:, P * k:P * (k + 1)],
                                               stage[:, s, 128 * k:128 * (k + 1)], ident[0:P, 0:P])
                last.then_inc(s_trn, 1)

            with pe.Fori(0, TI) as i:
                transposes(i, 0)
                for s in range(U):
                    if s + 1 < U:
                        transposes(i, s + 1)
                    t = i * U + s
                    pe.wait_ge(s_xT, k0 + t + 1)
                    for j, (w, _) in enumerate(q["blocks"]):
                        pe.wait_ge(s_eva[j], q["ev"][j] + t)
                        n = w.shape[2]
                        for k in range(nk):
                            last = nc.tensor.matmul(pb[j][0:P, 0:n], xT[:, s, k, :], w[:, k, :],
                                                    start=(k == 0), stop=(k == nk - 1))
                        last.then_inc(s_blk, 1)
                    if more:
                        more(i, s)

        def pass_dve(dve, name, evac):
            q = PASSES[name]
            nb = len(q["blocks"])
            with dve.Fori(0, TI) as i:
                for s in range(U):
                    t = i * U + s
                    for j, (_, e) in enumerate(q["blocks"]):
                        if e == "v":
                            dve.wait_ge(s_blk, q["blk"] + nb * t + j + 1)
                            evac(dve, i, s, j)

        def hx_free(eng, name, i, s):
            n = HSTN[name]
            per = (3, 2)[s % 2]
            eng.wait_ge(s_hst[s % 2], 16 * (n * per * TI + per * i + s // 2))

        def hx_copy(eng, name, copy):
            def evac(e, i, s, j):
                hx_free(e, name, i, s)
                copy(hst[:, s % 2, 2 * j:2 * j + 2, :], pb[j][0:P, :].rearrange("p (a d) -> p a d", d=D))\
                    .then_inc(s_eva[j], 1)
            return evac

        def hx_store(sp, name):
            q = PASSES[name]
            with sp.Fori(0, TI) as i:
                for s in range(U):
                    for j in range(4):
                        sp.wait_ge(s_eva[j], q["ev"][j] + i * U + s + 1)
                        sp.sem_inc(s_turn_sp, 1)
                    sp.dma_start(hx_v[bass.ds(i * U + s, 1), :, :, :].rearrange("a p r d -> (a p) r d"),
                                 hst[:, s % 2, :, :]).then_inc(s_hst[s % 2], 16)

        def hx_done(eng, name):
            n = HSTN[name] + 1
            for z, per in enumerate((3, 2)):
                eng.wait_ge(s_hst[z], 16 * n * per * TI)

        GR = GROUPS // GU

        H = [f0_w1.shape[2], f1_w1.shape[2]]
        MW = [(f0_w1, f0_b1, f0_w2, f0_b2, None, None), (f1_w1, f1_b1, f1_w2, f1_b2, f1_g, f1_b)]
        wreg = [tmpb, accb]
        NLOAD = [5, 7]

        def gnn_weights_sp(sp, n):
            for k in range(KC):
                sp.dma_start(tmpb[:, 1024 * k:1024 * (k + 1)].rearrange("p (b n) -> p b n", b=4),
                             bases[n].rearrange("b (k p) n -> k p b n", p=128)[k]).then_inc(s_w1l, 16)
                sp.dma_start(wcat[:, k, R * D:], roots[n].rearrange("(k p) n -> k p n", p=128)[k]).then_inc(s_w1l, 16)

        def mw1(n, z):
            return wreg[z][:, 0:2 * H[n]].rearrange("p (k h) -> p k h", k=KC)

        def mw2(n, z):
            return wreg[z][:, 2048:2048 + 2 * H[n]].rearrange("p (j d) -> p j d", d=D)

        def moe_sp(sp, n):
            w1, b1, w2, b2, g, b = MW[n]
            HC = H[n] // 128
            base = SLOTS // 2 * 16 * (0, NLOAD[0])[n]
            sp.wait_ge(s_rt, (1, 4)[n])
            for s in range(U):
                sp.wait_ge(s_dst[s], 32 * TI * (n + 1))

            def store(i, z):
                sp.wait_ge(s_mo[z], n * SLOTS // 2 + i + 1)
                sp.dma_start(ys_d.rearrange("(m a p) d -> m p a d", p=128, a=2)[bass.ds(2 * i + z, 1)]
                             .rearrange("m p a d -> (m p) a d"), ysb[z]).then_inc(s_ys[z], 16)

            def load(i, z):
                e = sp.value_load(eidr[0:1, n, bass.ds(2 * i + z, 1)], min_val=0, max_val=NE - 1)
                sm_ = s_mw[z]
                sp.dma_start(xsr[z], xs_d.rearrange("(m a p) d -> m p a d", p=128, a=2)[bass.ds(2 * i + z, 1)]
                             .rearrange("m p a d -> (m p) a d")).then_inc(sm_, 16)
                sp.dma_start(mw1(n, z), w1[bass.ds(e, 1)].rearrange("a (k p) h -> (a p) k h", p=128)).then_inc(sm_, 16)
                sp.dma_start(mw2(n, z), w2[bass.ds(e, 1)].rearrange("a (j p) d -> (a p) j d", p=128)).then_inc(sm_, 16)
                sp.dma_start(par[0:HC, z, :], b1[bass.ds(e, 1)].rearrange("a (j p) -> (a j) p", p=128)).then_inc(sm_, 16)
                sp.dma_start(b2c[:, z, :], b2[bass.ds(e, 1)].rearrange("a d -> (a d)").partition_broadcast(128))\
                    .then_inc(sm_, 16)
                if g is not None:
                    for m, v in enumerate((g, b)):
                        sp.dma_start(par[HC + 2 * m:HC + 2 * m + 2, z, :],
                                     v[bass.ds(e, 1)].rearrange("a (j p) -> (a j) p", p=128)).then_inc(sm_, 16)

            for z in range(2):
                load(0, z)
            with sp.Fori(0, SLOTS // 2 - 1) as i:
                for z in range(2):
                    store(i, z)
                    load(i + 1, z)
            for z in range(2):
                store(SLOTS // 2 - 1, z)

        def gather_pool(pool, n):
            g = nc.gpsimd
            with pool.Fori(0, GR) as i:
                for u in range(GU):
                    pool.wait_ge(s_sg[u], n * GR + i)
                    g.tensor_copy(gixs[:, u, :], gid[:, bass.ds(i * GU * CH + u * CH, CH)]).then_inc(s_gix, 1)
                    pool.wait_ge(s_gix, (0, 2 * GROUPS, 3 * GROUPS)[n] + i * GU + u + 1)
                    pool.sem_inc(s_turn, 1)
                    for c in range(CH):
                        g.indirect_dma_start(G[:, u, c, :], None, hx_d,
                                             bass.IndirectOffsetOnAxis(gixs[:, u, c:c + 1], axis=0))\
                            .then_inc(s_G[u], 16)

        def dispatch_pool(pool, n):
            g = nc.gpsimd
            pool.wait_ge(s_rt, (1, 4)[n])
            with pool.Fori(0, TI) as i:
                for s in range(U):
                    pool.wait_ge(s_dst[s], 32 * (n * TI + i))
                for m in range(2):
                    g.tensor_copy(mix[:, m, :], pwi[:, m, bass.ds(i * U, U)]).then_inc(s_dix, 1)
                pool.wait_ge(s_dix, 2 * (n * TI + i) + 2)
                for s in range(U):
                    pool.wait_ge(s_dsp, n * T + i * U + s + 1)
                    pool.sem_inc(s_turn, 1)
                    for m in range(2):
                        g.indirect_dma_start(xs_d, bass.IndirectOffsetOnAxis(mix[:, m, s:s + 1], axis=0),
                                             stage[:, s, :], None).then_inc(s_dst[s], 16)

        def combine_pool(pool, n):
            g = nc.gpsimd
            for z in range(2):
                pool.wait_ge(s_ys[z], 16 * SLOTS // 2 * (n + 1))
            with pool.Fori(0, TI) as i:
                pool.wait_ge(s_cmbd, n * T + i * U)
                for m in range(2):
                    g.tensor_copy(mix[:, m, :], pwi[:, m, bass.ds(i * U, U)]).then_inc(s_cix, 1)
                pool.wait_ge(s_cix, 2 * (n * TI + i) + 2)
                for s in range(U):
                    if s >= 2:
                        pool.wait_ge(s_cmbd, n * T + i * U + s - 1)
                    pool.sem_inc(s_turn, 1)
                    for m in range(2):
                        g.indirect_dma_start(yg[:, s % 2, m, :], None, ys_d,
                                             bass.IndirectOffsetOnAxis(mix[:, m, s:s + 1], axis=0))\
                            .then_inc(s_cg[s % 2], 16)

        def prefix_pe(pe, n, operand):
            pe.wait_ge(s_v2p, operand)
            nc.tensor.matmul(pb[7][0:P, 0:n], tri[0:P, 0:P], tot[:, 0:n], start=True, stop=True)
            nc.tensor.matmul(pb[6][0:P, 0:n], ones[0:P, 0:P], tot[:, 0:n], start=True, stop=True).then_inc(s_q, 1)

        def gather_pe(pe, n):
            with pe.Fori(0, GR) as i:
                for u in range(GU):
                    pe.wait_ge(s_G[u], 16 * CH * (n * GR + i + 1))
                    pe.wait_ge(s_oh[u], n * (GR + 1) + i + 1)
                    if u == 0:
                        pe.wait_ge(s_acc, n * GROUPS + i * GU)
                    for c in range(CH):
                        last = nc.tensor.matmul(pb[u][0:P, 0:D], oh[:, u, c, :], G[:, u, c, :],
                                                start=(c == 0), stop=(c == CH - 1))
                    if n == 0:
                        for c in range(CH):
                            last = nc.tensor.matmul(pb[4 + u][0:P, 0:R], oh[:, u, c, :],
                                                    toh[:, bass.ds(i * GU * CH + u * CH + c, 1), :]
                                                    .rearrange("p a r -> p (a r)"),
                                                    start=(c == 0), stop=(c == CH - 1))
                    last.then_inc(s_sg[u], 1)

        def moe_pe(pe, n):
            HC = H[n] // 128
            NL = 16 * NLOAD[n]
            b0 = (0, 16 * NLOAD[0] * (SLOTS // 2))[n]
            hb = (0, SLOTS * (H[0] // 128))[n]
            np_ = HC + (4 if n else 0)

            def transposes(i, z):
                pe.wait_ge(s_mw[z], b0 + NL * (i + 1))
                pe.wait_ge(s_mx, n * SLOTS + 2 * i + z)
                for k in range(KC):
                    for a in range(2):
                        nc.tensor.transpose(pb[7][:, 256 * k + 128 * a:256 * k + 128 * (a + 1)],
                                            xsr[z][:, a, 128 * k:128 * (k + 1)], ident[:, :])
                nc.tensor.transpose(pb[6][:, 0:np_], par[0:np_, z, :], ident[0:np_, 0:np_]).then_inc(s_mt, 1)

            def tile(i, z, ahead):
                pe.wait_ge(s_mx, n * SLOTS + 2 * i + z + 1)
                for j in range(HC):
                    h0 = hb + HC * (2 * i + z) + j
                    pe.wait_ge(s_ma, h0 - 3 if j >= 4 else h0 - j)
                    for k in range(KC):
                        last = nc.tensor.matmul(pb[j % 4][:, 0:SLOT], mw1(n, z)[:, k, 128 * j:128 * (j + 1)],
                                                xsT[z][:, k, :], start=(k == 0), stop=(k == KC - 1))
                    last.then_inc(s_mh, 1)
                if ahead:
                    transposes(*ahead)
                pe.wait_ge(s_mo[z], n * SLOTS // 2 + i)
                for a in range(2):
                    for j in range(HC):
                        if a == 0:
                            pe.wait_ge(s_ma, hb + HC * (2 * i + z) + j + 1)
                        last = nc.tensor.matmul(pb[4 + z][:, D * a:D * (a + 1)],
                                                hT[:, j, 128 * a:128 * (a + 1)], mw2(n, z)[:, j, :],
                                                start=(j == 0), stop=(j == HC - 1))
                last.then_inc(s_my[z], 1)

            transposes(0, 0)
            with pe.Fori(0, SLOTS // 2 - 1) as i:
                tile(i, 0, (i, 1))
                tile(i, 1, (i + 1, 0))
            tile(SLOTS // 2 - 1, 0, (SLOTS // 2 - 1, 1))
            tile(SLOTS // 2 - 1, 1, None)

        def moe_act(act, n):
            HC = H[n] // 128
            hb = (0, SLOTS * (H[0] // 128))[n]
            ac = nc.scalar
            act.wait_ge(s_v2a, (5, 6)[n])
            ac.activation(pw[:, 1, :], pw[:, 1, :], ACT.Exp).then_inc(s_a2v, 1)
            act.wait_ge(s_rt, (1, 4)[n])
            with act.Fori(0, TI) as i:
                for s in range(U):
                    act.wait_ge(s_dst[s], 32 * (n * TI + i))
                    ac.activation(stage[:, s, :], xn[:, bass.ds(i * U + s, 1), :].rearrange("p a d -> p (a d)"),
                                  ACT.Copy).then_inc(s_dsp, 1)
            with act.Fori(0, SLOTS // 2) as i:
                for z in range(2):
                    for j in range(HC):
                        h0 = hb + HC * (2 * i + z) + j
                        act.wait_ge(s_mh, h0 + 1)
                        act.wait_ge(s_my[1 - z], n * SLOTS // 2 + i + z)
                        ac.activation(hT[:, j, :], pb[j % 4][:, 0:SLOT], (ACT.Relu, ACT.Gelu)[n],
                                      bias=parT[:, z, j:j + 1]).then_inc(s_ma, 1)

        def NEVQ(name):
            return PASSES[name]["ev"][0] + T

        def relation_weights(dve, ch, n):
            v = nc.vector
            dve.wait_ge(s_w1l, 32 * KC * (n + 1))
            for r in range(R):
                for b in range(4):
                    c = compb[:, n, 4 * r + b:4 * r + b + 1]
                    o = wcat[:, :, D * r:D * (r + 1)]
                    i = tmpb[:, 0:2048].rearrange("p (k b n) -> p k b n", k=KC, b=4)[:, :, b, :]
                    if b == 0:
                        ch(v.tensor_scalar(o, i, c, None, ALU.mult))
                    else:
                        ch(v.scalar_tensor_tensor(o, i, c, o, ALU.mult, ALU.add))
            dve.sem_inc(s_cmb, 1)

        def prefix(dve, ch, n, size, shift, q):
            v = nc.vector
            dve.sem_inc(s_v2p, 1)
            dve.wait_ge(s_q, q)
            ch(v.tensor_scalar(tti[:, 0:n], pb[6][0:P, 0:n], float(size - 1), None, ALU.add))
            ch(v.tensor_scalar(tti[:, 0:n], tti[:, 0:n], shift, None, ALU.arith_shift_right))
            ch(v.tensor_copy(tt[:, 0:n], tti[:, 0:n]))
            ch(v.tensor_tensor_scan(bs[:, 0:n], ones[0:P, 0:n], tt[:, 0:n], 0.0, ALU.mult, ALU.add))
            ch(v.tensor_tensor(bs[:, 0:n], bs[:, 0:n], tt[:, 0:n], ALU.subtract))
            ch(v.scalar_tensor_tensor(off[:, 0:n], bs[:, 0:n], float(size), pb[7][0:P, 0:n], ALU.mult, ALU.add))

        def gather_dve(dve, n):
            v = nc.vector

            def onehots(i, u):
                for c in range(CH):
                    col = i * GU * CH + u * CH + c
                    if n:
                        last = v.tensor_scalar(oh[:, u, c, :], iota[:, 0:P], dstl[:, bass.ds(col, 1)],
                                               inv[:, bass.ds(col, 1)], ALU.is_equal, ALU.mult)
                    else:
                        last = v.tensor_scalar(oh[:, u, c, :], iota[:, 0:P], dstl[:, bass.ds(col, 1)], None, ALU.is_equal)
                last.then_inc(s_oh[u], 1)
            for u in range(GU):
                onehots(0, u)
            with dve.Fori(0, GR) as i:
                for u in range(GU):
                    b = dve.value_load(binr[0:1, bass.ds(i * GU + u, 1)], min_val=0, max_val=T - 1)
                    dve.wait_ge(s_sg[u], n * GR + i + 1)
                    dve.wait_ge(s_acc, n * GROUPS + i * GU + u)
                    at = acc[:, bass.ds(b, 1), :].rearrange("p a d -> p (a d)")
                    if n == 0:
                        ct = cnt[:, bass.ds(b, 1), :].rearrange("p a d -> p (a d)")
                        v.tensor_tensor(ct, ct, pb[4 + u][0:P, 0:R], ALU.add)
                    v.tensor_tensor(at, at, pb[u][0:P, 0:D], ALU.add).then_inc(s_acc, 1)
                    onehots(i + 1, u)

        def moe_dve(dve, ch, n):
            v = nc.vector
            name = ("gate0", "gate1")[n]
            HC = H[n] // 128

            gb = gatb[:, 3, :]
            if n == 0:
                ch(v.tensor_tensor(gb, gatb[:, 0, :], gatb[:, 1, :], ALU.add))
            else:
                ch(v.tensor_copy(gb, gatb[:, 2, :]))

            def evac(e, i, s, j):
                v.tensor_tensor(lg[:, bass.ds(i * U + s, 1), :].rearrange("p a e -> p (a e)"), pb[0][0:P, 0:NE], gb,
                                ALU.add).then_inc(s_eva[0], 1)
            pass_dve(dve, name, evac)
            dve.wait_ge(s_eva[0], NEVQ(name))
            lj = lg[:, :, :].unsqueeze(2).to_broadcast([P, T, NE, NE])
            le = lg[:, :, :].unsqueeze(3).to_broadcast([P, T, NE, NE])
            ch.step(v.tensor_tensor(big, lj, le, ALU.is_gt))
            ch(v.tensor_tensor(big2, lj, le, ALU.is_equal))
            ch(v.tensor_tensor(big2, big2, ltm[:, :, :].unsqueeze(1).to_broadcast([P, T, NE, NE]), ALU.mult))
            ch(v.tensor_tensor(big, big, big2, ALU.add))
            ch(v.tensor_reduce(rk[:, :, :], big, X, ALU.add))
            for m in range(2):
                ch(v.tensor_scalar(sel[:, m], rk[:, :, :], float(m), None, ALU.is_equal))
            ch(v.tensor_tensor(sel[:, 2], sel[:, 0], sel[:, 1], ALU.add))
            for m in range(2):
                ch(v.tensor_tensor(rk[:, :, :], sel[:, m], lg[:, :, :], ALU.mult))
                ch(v.tensor_reduce(pw[:, m, :], rk[:, :, :], X, ALU.add))
            v.tensor_tensor(pw[:, 1, :], pw[:, 1, :], pw[:, 0, :], ALU.subtract).then_inc(s_v2a, 1)
            dve.wait_ge(s_a2v, 3 + n)
            ch(v.tensor_scalar(pw[:, 0, :], pw[:, 1, :], 1.0, None, ALU.add))
            ch(v.reciprocal(pw[:, 0, :], pw[:, 0, :]))
            ch(v.tensor_tensor(pw[:, 1, :], pw[:, 1, :], pw[:, 0, :], ALU.mult))
            for e in range(NE):
                ch(v.tensor_tensor_scan(scn[:, :, e], ones[0:P, 0:T], sel[:, 2, :, e], 0.0, ALU.mult, ALU.add))
            ch(v.tensor_copy(tot[:, 0:NE], scn[:, T - 1, :]))
            prefix(dve, ch, NE, SLOT, 8, (7, 16)[n])
            ch(v.tensor_tensor(scn[:, :, :], scn[:, :, :], off[:, 0:NE].unsqueeze(1).to_broadcast([P, T, NE]), ALU.add))
            ch(v.tensor_scalar(scn[:, :, :], scn[:, :, :], -1.0, None, ALU.add))
            for m in range(2):
                ch(v.tensor_tensor(rk[:, :, :], sel[:, m], scn[:, :, :], ALU.mult))
                ch(v.tensor_reduce(mu, rk[:, :, :], X, ALU.add))
                ch(v.tensor_copy(pwi[:, m, :], mu))
            sl = sel[0:1, 0, 0:8, :].rearrange("p a b -> p (a b)")[:, 0:SLOTS]
            s2 = sel[0:1, 1, 0:8, :].rearrange("p a b -> p (a b)")[:, 0:SLOTS]
            ch(v.memset(sl, 0.0))
            for e in range(1, NE):
                ch(v.tensor_scalar(s2, iota[0:1, 0:SLOTS], bs[0:1, e:e + 1], None, ALU.is_ge))
                ch(v.tensor_tensor(sl, sl, s2, ALU.add))
            ch(v.tensor_copy(eidr[:, n, :], sl))
            dve.sem_inc(s_rt, 1)
            def operands(i, z):
                t = n * SLOTS + 2 * i + z
                dve.wait_ge(s_mt, t + 1)
                np_ = HC + (4 if n else 0)
                v.tensor_copy(parT[:, z, 0:np_], pb[6][:, 0:np_]).then_inc(s_mp, 1)
                dve.wait_ge(s_mp, t + 1)
                for k in range(KC):
                    tp = pb[7][:, SLOT * k:SLOT * (k + 1)]
                    if n:
                        last = v.tensor_scalar(xsT[z][:, k, :], tp, parT[:, z, HC + k:HC + k + 1],
                                               parT[:, z, HC + 2 + k:HC + 3 + k], ALU.mult, ALU.add)
                    else:
                        last = v.tensor_copy(xsT[z][:, k, :], tp)
                last.then_inc(s_mx, 1)

            def outputs(i, z):
                dve.wait_ge(s_my[z], n * SLOTS // 2 + i + 1)
                dve.wait_ge(s_ys[z], 16 * (n * SLOTS // 2 + i))
                v.tensor_tensor(ysb[z], pb[4 + z][:, :].rearrange("p (a d) -> p a d", d=D),
                                b2c[:, z, :].unsqueeze(1).to_broadcast([128, 2, D]), ALU.add).then_inc(s_mo[z], 1)

            operands(0, 0)
            with dve.Fori(0, SLOTS // 2 - 1) as i:
                operands(i, 1)
                outputs(i, 0)
                operands(i + 1, 0)
                outputs(i, 1)
            operands(SLOTS // 2 - 1, 1)
            for z in range(2):
                outputs(SLOTS // 2 - 1, z)
            with dve.Fori(0, TI) as i:
                for s in range(U):
                    t = i * U + s
                    per = (3, 2)[s % 2]
                    dve.wait_ge(s_cg[s % 2], 32 * (n * TI * per + per * i + s // 2 + 1))
                    xt = x[:, bass.ds(t, 1), :].rearrange("p a d -> p (a d)")
                    v.scalar_tensor_tensor(xt, yg[:, s % 2, 0, :], pw[:, 0, bass.ds(t, 1)], xt, ALU.mult, ALU.add)\
                        .then_inc(s_cm1, 1)
                    dve.wait_ge(s_cm1, n * T + t + 1)
                    v.scalar_tensor_tensor(xt, yg[:, s % 2, 1, :], pw[:, 1, bass.ds(t, 1)], xt, ALU.mult, ALU.add)\
                        .then_inc(s_cmbd, 1)
            dve.wait_ge(s_cmbd, (n + 1) * T)



        block = ctx.enter_context(nc.Block())

        @block.sync
        def _(sp):
            sp.dma_start(x[:, :, :], x_v).then_inc(s_xin, 16)
            for n, a in enumerate((src, dst, etype)):
                sp.dma_start(SA[n].bitcast(I32), a.rearrange("(p c) -> p c", p=P)).then_inc(s_edge, 16)
            for k in range(KC):
                sp.dma_start(wcat[:, k, 0:R * D].rearrange("p (r n) -> p r n", r=R),
                             w0.rearrange("r (k p) n -> k p r n", p=128)[k]).then_inc(s_w0, 16)
                sp.dma_start(wcat[:, k, R * D:], wl0.rearrange("(k p) n -> k p n", p=128)[k]).then_inc(s_w0, 16)
                sp.dma_start(wq0[:, k, :], wqkv0.rearrange("(k p) n -> k p n", p=128)[k]).then_inc(s_w0, 16)
                sp.dma_start(wg[:, 0, k, :], f0_wg.rearrange("(k p) n -> k p n", p=128)[k]).then_inc(s_par, 16)
                sp.dma_start(wg[:, 1, k, :], f1_wr.rearrange("(k p) n -> k p n", p=128)[k]).then_inc(s_par, 16)
            sp.dma_start(gpre[:, :], gpre0.rearrange("(k p) -> p k", p=128), allow_slow_non_contiguous=True).then_inc(s_par, 16)
            for h in range(4):
                sp.dma_start(memk[:, 32 * h:32 * h + 32], memkv[0, h].rearrange("d m -> m d"), allow_slow_non_contiguous=True).then_inc(s_par, 16)
                sp.dma_start(memv[:, 32 * h:32 * h + 32], memkv[1, h].rearrange("d m -> m d"), allow_slow_non_contiguous=True).then_inc(s_par, 16)
            sp.dma_start(wo0[:, :], wout0).then_inc(s_par, 16)
            for n, a in enumerate((hb0, bout0, gout0, biases[0], biases[1], bout1)):
                sp.dma_start(bc[:, n, :], row(a)).then_inc(s_par, 16)
            for n in range(2):
                sp.dma_start(compb[:, n, :], row(comps[n].rearrange("r b -> (r b)"))).then_inc(s_par, 16)
            for n, a in enumerate((f0_bg, f0_bias, f1_br)):
                sp.dma_start(gatb[:, n, :], row(a, P)).then_inc(s_par, 16)
            sp.wait_ge(s_zero, 2)
            for n in range(SLOTS // 4):
                sp.dma_start(xs_z[n], tmpb[:, 0:8 * D]).then_inc(s_zd, 16)
            sp.dma_start(rec_v, unused).then_inc(s_zd, 16)

            hx_store(sp, "gnn0")
            for z in range(2):
                sp.wait_ge(s_sct[z], 16 * SCU * (EC // (2 * SCU)))
            sp.dma_start(recs[:, :, :], rec_v).then_inc(s_recl, 16)
            sp.wait_ge(s_inv, 1)
            sp.dma_start(inv_d.rearrange("(t p r) a -> p t (r a)", p=P, r=R), cnt[:, :, :]).then_inc(s_ivd, 16)
            moe_sp(sp, 0)
            sp.wait_ge(s_ln, 3)
            gnn_weights_sp(sp, 0)
            hx_store(sp, "gnn1")
            sp.wait_ge(s_blk, PASSES["kv1"]["blk"])
            for k in range(KC):
                sp.dma_start(wkv[:, k, :], wqkv1.rearrange("(k p) n -> k p n", p=128)[k][:, 512:1536]).then_inc(s_wm, 16)
            sp.wait_ge(s_dot, 2)
            for k in range(KC):
                sp.dma_start(tmpb[:, 512 * k:512 * k + 512], wqkv1.rearrange("(k p) n -> k p n", p=128)[k][:, 0:512])\
                    .then_inc(s_wm, 16)
            sp.dma_start(tmpb[:, 1024:2048].rearrange("p (j n) -> p j n", j=4),
                         wout1.rearrange("(j p) n -> p j n", p=128)).then_inc(s_wm, 16)
            sp.wait_ge(s_rt, 3)
            gnn_weights_sp(sp, 1)
            hx_store(sp, "gnn2")
            moe_sp(sp, 1)
            for n in range(TI):
                sp.wait_ge(s_cmbd, T + U * (n + 1))
                sp.dma_start(out_v[:, U * n:U * (n + 1), :], x[:, U * n:U * (n + 1), :]).then_inc(s_out, 16)
            sp.wait_ge(s_out, 16 * TI)


        @block.gpsimd
        def _(pool):
            ch = Chain(pool, s_pool)
            g = nc.gpsimd
            ch(g.memset(tmpb[:, 0:8 * D], 0.0))
            ch.step(g.memset(unused, 0))
            ch.wait()
            ch.step(g.memset(unused[:, :, 1:2].bitcast(F32), -1.0))
            ch.step(g.memset(unused[:, :, 3:4].bitcast(F32), -1.0))
            ch.wait()
            g.memset(ident[:, :], 0.0).then_inc(s_zero, 2)
            ch.step(g.memset(ones[:, :], 1.0))
            ch.step(g.memset(tri[:, :], 1.0))
            ch.step(g.memset(bmask[:, :], 32 ** -0.5))
            ch.step(g.memset(bmask1[:, :], 1.0 / NODES))
            ch.step(g.memset(ltm[:, :, :], 1.0))
            ch.step(g.memset(memv[:, 128:129], 1.0))
            ch.step(g.memset(vv[:, :, 128:129], 1.0))
            ch.wait()
            pool.wait_ge(s_zero, 2)
            ch.step(g.affine_select(out=ident[:, :], in_=ident[:, :], compare_op=ALU.not_equal, fill=1.0,
                                    base=0, pattern=[[-1, 128]], channel_multiplier=1))
            ch.step(g.affine_select(out=tri[:, :], in_=tri[:, :], compare_op=ALU.is_gt, fill=0.0,
                                    base=0, pattern=[[1, 128]], channel_multiplier=-1))
            ch.step(g.affine_select(out=ltm[:, :, :], in_=ltm[:, :, :], compare_op=ALU.is_gt, fill=0.0,
                                    base=0, pattern=[[1, NE], [-1, NE]], channel_multiplier=0))
            for m, b in ((bmask, 32), (bmask1, 64)):
                v = m[:, :].rearrange("p (a c) -> p a c", c=b)
                ch(g.affine_select(out=v, in_=v, compare_op=ALU.is_ge, fill=0.0, base=0,
                                   pattern=[[-b, 128 // b], [0, b]], channel_multiplier=1))
                ch(g.affine_select(out=v, in_=v, compare_op=ALU.is_ge, fill=0.0, base=b - 1,
                                   pattern=[[b, 128 // b], [0, b]], channel_multiplier=-1))
            ch.step(g.iota(iota[:, :], [[1, GROUPS + 4]], base=0, channel_multiplier=0,
                           allow_small_or_imprecise_dtypes=True))
            ch.wait()
            g.memset(dstl[:, COLS:], -1.0).then_inc(s_const, 1)
            g.memset(inv[:, COLS:], 0.0).then_inc(s_const, 1)
            pool.wait_ge(s_pos, 1)
            pool.wait_ge(s_zd, 16 * (SLOTS // 4 + 1))
            with pool.Fori(0, EC // (2 * SCU)) as i:
                for z in range(2):
                    c = i * 2 * SCU + z * SCU
                    pool.wait_ge(s_sct[z], 16 * SCU * i)
                    g.tensor_copy(scix[:, z, :], posi[:, bass.ds(c, SCU)]).then_inc(s_cst, 1)
                    g.tensor_copy(scrc[:, z, :, :], rec[:, bass.ds(c, SCU), :]).then_inc(s_cst, 1)
                    pool.wait_ge(s_cst, 4 * i + 2 * z + 2)
                    pool.sem_inc(s_turn, 1)
                    for m in range(SCU):
                        g.indirect_dma_start(rec_d, bass.IndirectOffsetOnAxis(scix[:, z, m:m + 1], axis=0),
                                             scrc[:, z, m, :], None).then_inc(s_sct[z], 16)
            pool.wait_ge(s_srt, 1)
            hx_done(pool, "gnn0")
            gather_pool(pool, 0)
            dispatch_pool(pool, 0)
            pool.wait_ge(s_ivd, 16)
            with pool.Fori(0, GR) as i:
                pool.wait_ge(s_ivg, 16 * GU * CH * i)
                pool.wait_ge(s_ivc, i)
                g.tensor_copy(gixs[:, :, :], seg[:, bass.ds(i * GU * CH, GU * CH)]
                              .rearrange("p (a b) -> p a b", b=CH)).then_inc(s_gix, GU)
                pool.wait_ge(s_gix, GROUPS + GU * i + GU)
                pool.sem_inc(s_turn, 1)
                for m in range(GU * CH):
                    g.indirect_dma_start(ivs[:, m:m + 1], None, inv_d,
                                         bass.IndirectOffsetOnAxis(gixs[:, m // CH, m % CH:m % CH + 1], axis=0))\
                        .then_inc(s_ivg, 16)
                pool.wait_ge(s_ivg, 16 * GU * CH * i + 16 * GU * CH)
                g.tensor_copy(inv[:, bass.ds(i * GU * CH, GU * CH)], ivs[:, :]).then_inc(s_ivc, 1)
            combine_pool(pool, 0)
            hx_done(pool, "gnn1")
            gather_pool(pool, 1)
            hx_done(pool, "gnn2")
            gather_pool(pool, 2)
            dispatch_pool(pool, 1)
            combine_pool(pool, 1)


        @block.tensor
        def _(pe):
            pe.wait_ge(s_const, 2)
            q = [0]

            def done(ins):
                ins.then_inc(s_q, 1)

            prefix_pe(pe, T, 2)
            pe.wait_ge(s_w0, 16 * 3 * KC)
            pe.wait_ge(s_pos, 1)
            pass_pe(pe, "gnn0")
            pe.wait_ge(s_v2p, 3)
            nc.tensor.transpose(pb[7][:, 0:P], kmx, ident[0:P, 0:P])
            done(nc.tensor.transpose(pb[7][:, P:P + 4], memk[:, :], ident[0:4, 0:4]))
            pe.wait_ge(s_v2p, 4)
            done(nc.tensor.matmul(pb[6][:, 0:128], ones[:, :], dg, start=True, stop=True))
            pe.wait_ge(s_a2v, 2)
            for t in range(T):
                nc.tensor.matmul(pb[7][:, 0:129], tmp[:, t, 128:256], vv[:, t, :], start=(t == 0), stop=False)
            done(nc.tensor.matmul(pb[7][:, 0:129], memk[:, :], memv[:, :], start=False, stop=True))
            pe.wait_ge(s_v2p, 5)
            done(nc.tensor.transpose(pb[6][:, 0:128], ctxs, ident[:, :]))
            pe.wait_ge(s_v2p, 6)
            done(nc.tensor.matmul(pb[6][:, 0:D], ctxT, wo0[:, :], start=True, stop=True))
            pe.wait_ge(s_v2p, 7)
            pass_pe(pe, "mix0")
            gather_pe(pe, 0)
            pe.wait_ge(s_ln, 2)
            pass_pe(pe, "gate0")
            prefix_pe(pe, NE, 8)
            moe_pe(pe, 0)
            pe.wait_ge(s_cmb, 1)
            pass_pe(pe, "gnn1")
            pe.wait_ge(s_v2p, 9)
            nc.tensor.matmul(pb[5][:, :], zer[:, 0:128], zer[:, :], start=True, stop=True, skip_group_check=True)\
                .then_inc(s_dot, 1)

            def dots(i, s):
                t = i * U + s
                for j in range(2):
                    pe.wait_ge(s_eva[j], PASSES["kv1"]["ev"][j] + t + 1)
                for h in range(4):
                    last = nc.tensor.matmul(pb[5][:, 128 * h:128 * (h + 1)], vt[:, s % 2, 128 * h:128 * (h + 1)],
                                            kt[:, s % 2, 128 * h:128 * (h + 1)], start=False, stop=False,
                                            skip_group_check=True)
                last.then_inc(s_dt, 1)
            pass_pe(pe, "kv1", dots)
            pe.wait_ge(s_dt, T)
            nc.tensor.matmul(pb[4][:, 0:8], zer[:, 0:128], zer[:, 0:8], start=True, stop=True).then_inc(s_dot, 1)
            pe.wait_ge(s_v2p, 10)
            pe.wait_ge(s_wm, 16 * (2 * KC + 1))
            for j in range(4):
                done(nc.tensor.matmul(pb[j // 2][:, D * (j % 2):D * (j % 2 + 1)], dT[:, j, :],
                                      tmpb[:, 1024 + D * j:1024 + D * (j + 1)], start=True, stop=True))
            for k in range(KC):
                for j in range(4):
                    last = nc.tensor.transpose(pb[2 + k][:, 128 * j:128 * (j + 1)],
                                               tmpb[:, 512 * k + 128 * j:512 * k + 128 * (j + 1)], ident[:, :])
                done(last)
            pe.wait_ge(s_v2p, 11)
            for k in range(KC):
                for j in range(4):
                    last = nc.tensor.matmul(pb[4][:, D * k:D * (k + 1)], wqT[:, k, j, :], M1[:, j, :],
                                            start=(j == 0), stop=(j == 3))
                done(last)
            pe.wait_ge(s_v2p, 12)
            pass_pe(pe, "mix1")
            gather_pe(pe, 1)
            pe.wait_ge(s_cmb, 2)
            pass_pe(pe, "gnn2")
            gather_pe(pe, 2)
            pe.wait_ge(s_ln, 4)
            pass_pe(pe, "gate1")
            prefix_pe(pe, NE, 13)
            moe_pe(pe, 1)


        @block.scalar
        def _(act):
            ac = nc.scalar

            def square(src_, dst_):
                ac.activation(dst_, src_, ACT.Square).then_inc(s_sq, 1)

            RA = [0]

            def root(o, count=None):
                act.wait_ge(s_rsv, (RA[0] if count is None else count) + 1)
                ac.activation(o, o, ACT.Sqrt).then_inc(s_rsa, 1)
                if count is None:
                    RA[0] += 1

            def ln_act(n):
                act.wait_ge(s_lnc, n + 1)
                square(tmp, xn[:, :, :])
                root(va)

            def tsrc(a):
                return lambda t: a[:, bass.ds(t, 1), :].rearrange("p a d -> p (a d)")

            ln_act(0)
            act.wait_ge(s_ln, 1)
            square(xn[:, :, :], tmp)
            root(r0)
            pass_act(act, "gnn0", tsrc(xn), hx_copy(act, "gnn0", lambda o, i: ac.activation(o, i, ACT.Copy)))
            act.wait_ge(s_v2a, 1)
            ac.activation(tmp[:, :, 0:128], tmp[:, :, 0:128], ACT.Exp).then_inc(s_a2v, 1)
            act.wait_ge(s_v2a, 2)
            ac.activation(memk[:, :], memk[:, :], ACT.Exp)
            ac.activation(tmp[:, :, 128:256], tmp[:, :, 128:256], ACT.Exp).then_inc(s_a2v, 1)
            act.wait_ge(s_v2p, 7)
            act.wait_ge(s_v2a, 3)
            pass_act(act, "mix0", lambda t: tmp[:, bass.ds(t, 1), 0:128].rearrange("p a d -> p (a d)"))
            act.wait_ge(s_v2a, 4)
            square(tmp, xn[:, :, :])
            root(va)
            ln_act(1)
            act.wait_ge(s_ln, 2)
            pass_act(act, "gate0", tsrc(xn))
            moe_act(act, 0)
            ln_act(2)
            act.wait_ge(s_ln, 3)
            pass_act(act, "gnn1", tsrc(xn), hx_copy(act, "gnn1", lambda o, i: ac.activation(o, i, ACT.Copy)))

            hx_done(act, "gnn1")
            k0 = PASSES["kv1"]["ev"]

            def kv_evac(e, i, s, j):
                t = i * U + s
                act.wait_ge(s_sqf, t)
                ac.activation(sqv[:, 0:512], pb[0][0:P, :], ACT.Square)
                ac.activation(sqv[:, 512:1024], pb[1][0:P, :], ACT.Square).then_inc(s_sqk, 1)
                if s >= 2:
                    act.wait_ge(s_dt, t - 1)
                else:
                    act.wait_ge(s_dt, i * U)
                ac.activation(vt[:, s % 2, :], pb[1][0:P, :], ACT.Copy).then_inc(s_eva[1], 1)
                root(var, RA[0] + t)
            act.wait_ge(s_v2p, 9)
            pass_act(act, "kv1", tsrc(xn), kv_evac)
            RA[0] += T
            act.wait_ge(s_v2p, 12)
            pass_act(act, "mix1", tsrc(xn))
            act.wait_ge(s_cmb, 2)
            pass_act(act, "gnn2", tsrc(xn), hx_copy(act, "gnn2", lambda o, i: ac.activation(o, i, ACT.Copy)))
            ln_act(3)
            act.wait_ge(s_ln, 4)
            pass_act(act, "gate1", tsrc(xn))
            moe_act(act, 1)


        @block.vector
        def _(dve):
            ch = Chain(dve, s_vec)
            v = nc.vector
            AX = X

            def bt(a, n):
                return a.unsqueeze(2).to_broadcast([a.shape[0], a.shape[1], n])

            def btm(a, n):
                return a.unsqueeze(1).to_broadcast([a.shape[0], n, a.shape[1]])

            RS = [0]

            def rsq(o, scale, eps, lo=None, mul=1.0, count=None):
                k = RS[0] if count is None else count
                if lo is None:
                    v.tensor_scalar(o, o, scale, eps, ALU.mult, ALU.add).then_inc(s_rsv, 1)
                else:
                    v.tensor_scalar(o, o, lo, None, ALU.max).then_inc(s_rsv, 1)
                dve.wait_ge(s_rsa, k + 1)
                ch(v.reciprocal(o, o))
                if mul != 1.0:
                    ch(v.tensor_scalar(o, o, mul, None, ALU.mult))
                if count is None:
                    RS[0] += 1

            def ln(n):
                ch(v.tensor_reduce(mu, x[:, :, :], AX, ALU.add))
                ch(v.tensor_scalar(mu, mu, 1.0 / D, None, ALU.mult))
                v.tensor_tensor(tmp, x[:, :, :], bt(mu, D), ALU.subtract).then_inc(s_lnc, 1)
                dve.wait_ge(s_sq, SQ[n])
                ch(v.tensor_reduce(va, xn[:, :, :], AX, ALU.add))
                rsq(va, 1.0 / D, EPS)
                v.tensor_tensor(xn[:, :, :], tmp, bt(va, D), ALU.mult).then_inc(s_ln, 1)
                dve.wait_ge(s_ln, n + 1)

            SQ = [1, 4, 5, 6]
            dve.wait_ge(s_xin, 16)
            dve.wait_ge(s_zd, 16 * (SLOTS // 4 + 1))
            ln(0)

            dve.wait_ge(s_par, 16 * 25)
            dve.wait_ge(s_w0, 16 * 3 * KC)
            for k in range(KC):
                last = v.tensor_scalar(wq0[:, k, :], wq0[:, k, :], gpre[:, k:k + 1], None, ALU.mult)
                last.then_inc(s_vw, 1)
            dve.wait_ge(s_sq, 2)
            ch(v.tensor_reduce(r0, tmp, AX, ALU.add))
            rsq(r0, 1.0, 0.0, 1e-24, D ** 0.5)
            dve.wait_ge(s_vw, KC)
            dve.sem_inc(s_v2p, 1)

            dve.wait_ge(s_edge, 48)
            dve.wait_ge(s_const, 2)
            dst_f, typ_f, bin_f, posf, t1, t2, gof = SA[3], SA[4], SA[5], SA[6], SA[7], SA[8], SA[1]
            ch.step(v.tensor_copy(dst_f, SA[1].bitcast(I32)))
            ch.step(v.tensor_copy(typ_f, SA[2].bitcast(I32)))
            ch(v.tensor_copy(t2, SA[0].bitcast(I32)))
            ch(v.tensor_scalar(t1.bitcast(I32), dst_f, 4195.0, None, ALU.mult))
            ch(v.tensor_scalar(t1.bitcast(I32), t1.bitcast(I32), 19, None, ALU.arith_shift_right))
            ch(v.tensor_copy(bin_f, t1.bitcast(I32)))
            ch.step(v.scalar_tensor_tensor(rec[:, :, 0], typ_f, float(NODES), t2, ALU.mult, ALU.add))
            ch.step(v.scalar_tensor_tensor(rec[:, :, 1].bitcast(F32), bin_f, -float(P), dst_f, ALU.mult, ALU.add))
            ch.step(v.scalar_tensor_tensor(rec[:, :, 2], dst_f, float(R), typ_f, ALU.mult, ALU.add))
            ch.step(v.tensor_copy(rec[:, :, 3].bitcast(F32), typ_f))
            ch(v.memset(posf, -1.0))
            one_c = t2
            ch(v.memset(one_c, 1.0))
            S0, S1 = SA[0], SA[1]
            with dve.Fori(0, T) as b:
                ch.loop(b, 5)
                ch(v.tensor_scalar(S0, bin_f, iota[0:P, bass.ds(b, 1)], None, ALU.is_equal))
                ch(v.tensor_tensor_scan(S1, one_c, S0, 0.0, ALU.mult, ALU.add))
                ch.step(v.tensor_tensor(t1, S1, S0, ALU.mult))
                ch(v.tensor_tensor(tot[:, bass.ds(b, 1)], S1[:, EC - 1:EC], onec, ALU.mult))
                ch(v.tensor_tensor(posf, posf, t1, ALU.add))
            ch.end(T, 5)
            prefix(dve, ch, T, GROUP, 8, 1)
            with dve.Fori(0, T) as b:
                ch.loop(b, 2)
                ch(v.tensor_scalar(t1, bin_f, iota[0:P, bass.ds(b, 1)], off[:, bass.ds(b, 1)], ALU.is_equal, ALU.mult))
                ch(v.tensor_tensor(posf, posf, t1, ALU.add))
            ch.end(T, 2)
            ch(v.tensor_copy(posi, posf))
            ch(v.tensor_scalar(S0.bitcast(I32), posi, 7, None, ALU.arith_shift_right))
            ch(v.tensor_copy(S1, S0.bitcast(I32)))
            ch(v.scalar_tensor_tensor(posf, S1, -128.0, posf, ALU.mult, ALU.add))
            ch(v.scalar_tensor_tensor(posf, posf, float(COLS), S1, ALU.mult, ALU.add))
            ch(v.tensor_copy(posi, posf))
            g0, g1 = S0[0:1, 0:GROUPS + GU], S1[0:1, 0:GROUPS + GU]
            ch(v.memset(g0, 0.0))
            for b in range(1, T):
                ch(v.tensor_scalar(g1, iota[0:1, 0:GROUPS + GU], bs[0:1, b:b + 1], None, ALU.is_ge))
                ch(v.tensor_tensor(g0, g0, g1, ALU.add))
            ch(v.tensor_copy(binr[:, :], g0))
            dve.sem_inc(s_pos, 1)

            def gnn_evac(name, bias=None, qkv=False):
                hx = hx_copy(dve, name, v.tensor_copy)
                n = HSTN[name]

                def evac(e, i, s, j):
                    t = i * U + s
                    if j < 4:
                        return hx(e, i, s, j)
                    at = acc[:, bass.ds(t, 1), :].rearrange("p a d -> p (a d)")
                    if j == 4:
                        b = bc[0:P, bias, :] if bias is not None else None
                        if b is None:
                            v.tensor_scalar(at, pb[4][0:P, 0:D], 1.0, None, ALU.mult).then_inc(s_eva[4], 1)
                        else:
                            v.tensor_tensor(at, pb[4][0:P, 0:D], b, ALU.add).then_inc(s_eva[4], 1)
                        return
                    v.tensor_scalar(tmp[:, bass.ds(t, 1), :].rearrange("p a d -> p (a d)"), pb[5][0:P, 0:D],
                                    r0[:, bass.ds(t, 1)], None, ALU.mult)
                    v.tensor_scalar(vv[:, bass.ds(t, 1), 0:128].rearrange("p a d -> p (a d)"), pb[5][0:P, D:384],
                                    r0[:, bass.ds(t, 1)], None, ALU.mult).then_inc(s_eva[5], 1)
                return evac

            pass_dve(dve, "gnn0", gnn_evac("gnn0"))
            dve.wait_ge(s_eva[5], T)
            qv = tmp[:, :, 0:128].rearrange("p t (h d) -> p t h d", d=32)
            kv = tmp[:, :, 128:256]
            q4 = qs.rearrange("p (t h) -> p t h", h=4)
            q4b = q4.unsqueeze(3).to_broadcast([P, T, 4, 32])
            v.tensor_reduce(kmx, kv.rearrange("p t c -> p c t"), AX, ALU.max).then_inc(s_v2p, 1)
            ch(v.tensor_reduce(q4, qv, AX, ALU.max))
            v.tensor_tensor(qv, qv, q4b, ALU.subtract).then_inc(s_v2a, 1)
            dve.wait_ge(s_q, 2)
            ch(v.tensor_reduce(mcol, pb[7][:, 0:P + 4], AX, ALU.max))
            v.tensor_scalar(dg, ident[:, :], mcol, None, ALU.mult).then_inc(s_v2p, 1)
            dve.wait_ge(s_q, 3)
            v.tensor_tensor(memk[:, :], memk[:, :], pb[6][0:4, 0:128], ALU.subtract)
            v.tensor_tensor(kv, kv, btm(pb[6][0:P, 0:128], T), ALU.subtract).then_inc(s_v2a, 1)
            dve.wait_ge(s_a2v, 1)
            ch(v.tensor_reduce(q4, qv, AX, ALU.add))
            ch(v.reciprocal(qs, qs))
            v.tensor_tensor(qv, qv, q4b, ALU.mult).then_inc(s_v2a, 1)
            dve.wait_ge(s_q, 4)
            ch(v.reciprocal(rden, pb[7][:, 128:129]))
            v.scalar_tensor_tensor(ctxs, pb[7][:, 0:128], rden, bmask[:, :], ALU.mult, ALU.mult).then_inc(s_v2p, 1)
            dve.wait_ge(s_q, 5)
            v.tensor_copy(ctxT, pb[6][:, 0:128]).then_inc(s_v2p, 1)
            dve.wait_ge(s_q, 6)
            v.tensor_copy(M0, pb[6][:, 0:D]).then_inc(s_v2p, 1)

            def mix0_evac(e, i, s, j):
                v.tensor_tensor(tmp[:, bass.ds(i * U + s, 1), :].rearrange("p a d -> p (a d)"), pb[0][0:P, 0:D],
                                bc[0:P, 1, :], ALU.add).then_inc(s_eva[0], 1)
            ch(v.tensor_tensor(x[:, :, :], x[:, :, :], xn[:, :, :], ALU.add))
            pass_dve(dve, "mix0", mix0_evac)
            dve.wait_ge(s_eva[0], NEVQ("mix0"))
            dve.sem_inc(s_v2a, 1)
            dve.wait_ge(s_sq, 3)
            ch(v.tensor_reduce(va, xn[:, :, :], AX, ALU.add))
            rsq(va, 1.0, 0.0, 1e-24, D ** 0.5)
            ch(v.tensor_tensor(tmp, tmp, bt(va, D), ALU.mult))
            ch(v.tensor_tensor(tmp, tmp, btm(bc[0:P, 2, :], T), ALU.mult))
            ch(v.tensor_tensor(x[:, :, :], x[:, :, :], tmp, ALU.add))
            dve.wait_ge(s_recl, 16)
            ch.step(v.tensor_copy(gid[:, :], recs[:, :, 0]))
            ch.step(v.tensor_copy(seg[:, :], recs[:, :, 2]))
            ch.step(v.tensor_copy(dstl[:, 0:COLS], recs[:, :, 1].bitcast(F32)))
            ch.step(v.tensor_tensor(toh, recs[:, :, 3:4].bitcast(F32).to_broadcast([128, COLS, R]),
                                    btm(iota[:, 0:R], COLS), ALU.is_equal))
            ch.wait()
            v.memset(cnt[:, :, :], 0.0).then_inc(s_srt, 1)
            gather_dve(dve, 0)
            dve.wait_ge(s_acc, GROUPS)
            ch(v.scalar_tensor_tensor(x[:, :, :], acc, 0.5 ** 0.5, x[:, :, :], ALU.mult, ALU.add))
            ch(v.tensor_tensor(x[:, :, :], x[:, :, :], btm(bc[0:P, 0, :], T), ALU.add))
            ch(v.tensor_scalar(cnt[:, :, :], cnt[:, :, :], 1.0, None, ALU.max))
            v.reciprocal(cnt[:, :, :], cnt[:, :, :]).then_inc(s_inv, 1)
            ln(1)
            moe_dve(dve, ch, 0)
            ln(2)
            relation_weights(dve, ch, 0)
            pass_dve(dve, "gnn1", gnn_evac("gnn1", bias=3))
            dve.wait_ge(s_eva[4], PASSES["gnn2"]["ev"][4])
            dve.wait_ge(s_wm, 16 * KC)
            ch(v.memset(zer, 0.0))
            wv = wkv.rearrange("p k (h d) -> p k h d", d=64)
            mh = sm[:, 256:256 + 32].rearrange("p (k h) -> p k h", k=KC)
            for k in range(KC):
                ch(v.tensor_reduce(mh[:, k, :], wv[:, k], AX, ALU.add))
                ch(v.tensor_scalar(mh[:, k, :], mh[:, k, :], 1.0 / 64, None, ALU.mult))
                ch(v.tensor_tensor(wv[:, k], wv[:, k], mh[:, k, :].unsqueeze(2).to_broadcast([128, 16, 64]), ALU.subtract))
            ch(v.tensor_tensor(x[:, :, :], x[:, :, :], btm(bc[0:P, 5, :], T), ALU.add))
            dve.sem_inc(s_v2p, 1)
            CK = 2

            def kv_evac(e, i, s, j):
                t = i * U + s
                ch.n = ch.base + (i * U + s) * CK
                dve.wait_ge(s_sqk, t + 1)
                v.tensor_reduce(var, sqv.rearrange("p (h d) -> p h d", d=64), AX, ALU.add).then_inc(s_sqf, 1)
                dve.wait_ge(s_sqf, t + 1)
                rsq(var, 1.0 / 64, EPS, count=RS[0] + t)
                ch(v.tensor_tensor(rkv, var[:, 0:8], var[:, 8:16], ALU.mult))
                dve.wait_ge(s_dt, t - 1 if s >= 2 else i * U)
                v.tensor_tensor(kt[:, s % 2, :].rearrange("p (h d) -> p h d", d=64),
                                pb[0][0:P, :].rearrange("p (h d) -> p h d", d=64),
                                rkv.unsqueeze(2).to_broadcast([P, 8, 64]), ALU.mult).then_inc(s_eva[0], 1)
            ch.base = ch.n
            pass_dve(dve, "kv1", kv_evac)
            ch.n = ch.base + T * CK
            RS[0] += T
            dve.wait_ge(s_dot, 2)
            v.tensor_tensor(dT[:, :, :], pb[5][:, :].rearrange("p (j c) -> p j c", j=4), btm(bmask1[:, :], 4), ALU.mult)\
                .then_inc(s_v2p, 1)
            dve.wait_ge(s_q, 7 + 6)
            for j in range(2):
                ch.step(v.tensor_copy(M1[:, 2 * j:2 * j + 2, :], pb[j][:, :].rearrange("p (a d) -> p a d", d=D)))
            ch.step(v.tensor_copy(wqT[:, 0], pb[2][:, :].rearrange("p (j c) -> p j c", j=4)))
            ch.wait()
            v.tensor_copy(wqT[:, 1], pb[3][:, :].rearrange("p (j c) -> p j c", j=4)).then_inc(s_v2p, 1)
            dve.wait_ge(s_q, 7 + 8)
            v.tensor_copy(P1v[:, :, :], pb[4][:, :].rearrange("p (k d) -> p k d", d=D)).then_inc(s_v2p, 1)

            def mix1_evac(e, i, s, j):
                xt = x[:, bass.ds(i * U + s, 1), :].rearrange("p a d -> p (a d)")
                v.tensor_tensor(xt, pb[0][0:P, 0:D], xt, ALU.add).then_inc(s_eva[0], 1)
            pass_dve(dve, "mix1", mix1_evac)
            dve.wait_ge(s_eva[0], NEVQ("mix1"))
            dve.sem_inc(s_rt, 2)
            dve.wait_ge(s_ivc, GR)
            gather_dve(dve, 1)
            dve.wait_ge(s_acc, 2 * GROUPS)
            ch(v.tensor_scalar(xn[:, :, :], acc, 0.0, None, ALU.max))
            relation_weights(dve, ch, 1)
            pass_dve(dve, "gnn2", gnn_evac("gnn2", bias=4))
            dve.wait_ge(s_eva[4], NEV[4])
            gather_dve(dve, 2)
            dve.wait_ge(s_acc, 3 * GROUPS)
            ch(v.tensor_tensor(x[:, :, :], x[:, :, :], acc, ALU.add))
            ln(3)
            moe_dve(dve, ch, 1)


_INS = ['x', 'src', 'dst', 'edge_type_8', 'L0_gnn_weight', 'L0_gnn_h_bias', 'L0_gnn_loop_weight', 'L0_mix_t',
        'L0_mix_w_qkv', 'L0_mix_mem_kv', 'L0_mix_w_out', 'L0_mix_b_out', 'L0_mix_g_out', 'L0_mix_g_pre',
        'L0_ffn_Wg', 'L0_ffn_bg', 'L0_ffn_bias', 'L0_ffn_W1', 'L0_ffn_b1', 'L0_ffn_W2', 'L0_ffn_b2',
        'L1_gnn_comps', 'L1_gnn_bases', 'L1_gnn_roots', 'L1_gnn_biases', 'L1_mix_w_qkv', 'L1_mix_w_out',
        'L1_mix_b_out', 'L1_ffn_Wr', 'L1_ffn_br', 'L1_ffn_ln_g', 'L1_ffn_ln_b', 'L1_ffn_W1', 'L1_ffn_b1',
        'L1_ffn_W2', 'L1_ffn_b2']


def kernel(**inputs):
    import numpy as _np
    import concourse.bacc as _bacc
    from concourse import mybir as _mybir
    from concourse.bass_utils import run_bass_kernel_spmd as _run

    nc = _bacc.Bacc("TRN2", target_bir_lowering=False, num_devices=1)
    arrays, args = {}, []
    for name in _INS:
        a = _np.ascontiguousarray(inputs[name])
        arrays[f"in_{name}_dram"] = a
        args.append(nc.dram_tensor(f"in_{name}_dram", a.shape, _mybir.dt.from_np(a.dtype), kind="ExternalInput").ap())
    args.append(nc.dram_tensor("out_dram", (3125, 256), _mybir.dt.float32, kind="ExternalOutput").ap())
    gps_block(nc, *args)
    r = _run(nc, [arrays], core_ids=[0])
    return r.results[0]["out_dram"]
```

```python
import concourse.bass as bass
from concourse import mybir
from contextlib import ExitStack

F32 = mybir.dt.float32
I32 = mybir.dt.int32
ALU = mybir.AluOpType
ACT = mybir.ActivationFunctionType
X = mybir.AxisListType.X

NODES, D = 3125, 256
P = 125
T = NODES // P
U = 5
TI = T // U
KC = D // 128
R = 8
EDGES = 50000
EC = EDGES // P
GROUP = 256
GROUPS = (EDGES + T * (GROUP - 1)) // GROUP
GS = 4
GROUPS = -(-GROUPS // GS) * GS
GU = 8
GR = GROUPS // GU
CH = GROUP // 128
COLS = GROUPS * CH
OS = 8
OL = 7
PADC = 3 * OS * CH
NE = 8
SLOT = 256
SLOTS = (2 * NODES + NE * (SLOT - 1)) // SLOT
SLOTS += SLOTS % 2
EPS = 1e-5
SCU = 8
HEAD = 8
HEAD_DMA = 16


class Chain:

    def __init__(self, eng, sem):
        self.eng, self.sem, self.n, self.base = eng, sem, 0, 0

    def __call__(self, ins):
        self.step(ins)
        self.wait()

    def step(self, ins):
        ins.then_inc(self.sem, 1)
        self.n += 1

    def wait(self):
        self.eng.wait_ge(self.sem, self.n)

    def loop(self, i, steps):
        self.base = self.n
        self.n = self.base + i * steps

    def end(self, rounds, steps):
        self.n = self.base + rounds * steps


def gps_block(nc, x_in, src, dst, etype, w0, hb0, wl0, t0, wqkv0, memkv, wout0, bout0, gout0, gpre0,
              f0_wg, f0_bg, f0_bias, f0_w1, f0_b1, f0_w2, f0_b2, comps, bases, roots, biases,
              wqkv1, wout1, bout1, f1_wr, f1_br, f1_g, f1_b, f1_w1, f1_b1, f1_w2, f1_b2, out):
    ctx = ExitStack()
    with ctx:
        def sb(name, shape, dt=F32):
            return ctx.enter_context(nc.sbuf_tensor(name, shape, dt))

        def sem(name):
            return ctx.enter_context(nc.semaphore(name))

        def dram(name, shape, dt=F32):
            return nc.dram_tensor(name, shape, dt, kind="Internal").ap()

        hx_d = dram("hx_d", [R * NODES, D])
        rec_d = dram("rec_d", [128 * COLS, 4], I32)
        xs_d = dram("xs_d", [SLOTS * SLOT, D])
        ys_d = dram("ys_d", [SLOTS * SLOT, D])

        x = sb("x", [P, T, D])
        xn = sb("xn", [P, T, D])
        accb = sb("accb", [128, T * D])
        tmpb = sb("tmpb", [128, T * D])
        acc = accb[0:P, :].rearrange("p (t d) -> p t d", d=D)
        tmp = tmpb[0:P, :].rearrange("p (t d) -> p t d", d=D)
        wcat = sb("wcat", [128, KC, (R + 1) * D])
        hst = sb("hst", [P, 2, R, D])
        stage = sb("stage", [P, U, D])
        xT = sb("xT", [128, U, KC, P])
        G = sb("G", [128, GS, CH, D])
        wq0 = G[:, 0:KC, :, :].rearrange("p k c d -> p k (c d)")[:, :, 0:384]
        oh = sb("oh", [128, GS, CH, P])
        ohs = [oh[:, q, :, :] for q in range(GS)] + [xT[:, 1 + q, :, :] for q in range(OS - GS)]
        ohb = [0, GROUPS + GS, GROUPS + GS + OL]
        moe = sb("moe", [128, 5 * EC + T * 129])
        hT = moe[:, 0:2048].rearrange("p (j s) -> p j s", s=SLOT)
        xsr = [moe[:, 2048 + 512 * a:2560 + 512 * a].rearrange("p (a d) -> p a d", d=D) for a in range(2)]
        xsT = [moe[:, 3072 + 512 * a:3584 + 512 * a].rearrange("p (k s) -> p k s", s=SLOT) for a in range(2)]
        ysb = [moe[:, 4096 + 512 * a:4608 + 512 * a].rearrange("p (a d) -> p a d", d=D) for a in range(2)]
        ohT = moe[0:P, 4096:4608].rearrange("p (z c n) -> p z c n", z=2, n=128)
        b2c = sb("b2c", [128, 2, D])
        par = sb("par", [12, 2, 128])
        parT = sb("parT", [128, 2, 12])
        vv = moe[0:P, 5 * EC:5 * EC + T * 129].rearrange("p (t n) -> p t n", n=129)
        rec = moe[0:P, 0:4 * EC].bitcast(I32).rearrange("p (c f) -> p c f", f=4)
        posi = moe[0:P, 4 * EC:5 * EC].bitcast(I32)
        SA = [accb[0:P, EC * n:EC * (n + 1)] for n in range(9)]
        recs = moe[:, 0:4 * COLS].bitcast(I32).rearrange("p (c f) -> p c f", f=4)
        zeros = moe[:, 5 * EC:5 * EC + 8 * D]
        wq1 = tmpb[:, 2048:3072].rearrange("p (k n) -> p k n", k=KC)
        wo1 = tmpb[:, 3072:4096].rearrange("p (j n) -> p j n", j=4)
        unused = tmpb[:, 8 * D:8 * D + 4 * COLS].bitcast(I32).rearrange("p (c f) -> p c f", f=4)
        gid = sb("gid", [128, COLS], I32)
        typ = sb("typ", [128, COLS + PADC])
        dstl = sb("dstl", [128, COLS + PADC])
        inv = sb("inv", [128, COLS + PADC])
        toh = tmpb[:, 0:COLS * R].rearrange("p (c r) -> p c r", r=R)
        cnt = sb("cnt", [P, T, R])
        gixs = sb("gixs", [128, 2, GS, CH], I32)
        scix = sb("scix", [P, 2, SCU], I32)
        scrc = sb("scrc", [P, 2, SCU, 4], I32)
        mix = sb("mix", [P, 2, U], I32)
        binr = sb("binr", [1, GROUPS + GU], I32)
        eidr = sb("eidr", [1, 2, SLOTS], I32)
        ident = sb("ident", [128, 128])
        ones = sb("ones", [128, 128])
        tri = sb("tri", [128, 128])
        iota = sb("iota", [128, GROUPS + GU])
        bmask = sb("bmask", [128, 128])
        bmask1 = sb("bmask1", [128, 128])
        ltm = sb("ltm", [P, NE, NE])
        bc = sb("bc", [128, 6, D])
        compb = sb("compb", [128, 2, 32])
        gatb = sb("gatb", [P, 4, NE])
        gpre = sb("gpre", [128, KC])
        memk = sb("memk", [4, 128])
        memv = sb("memv", [4, 129])
        wo0 = sb("wo0", [128, D])
        wg = sb("wg", [128, 2, KC, NE])
        sm = sb("sm", [128, 1160])
        stf = stage[:, :, :].rearrange("p u d -> p (u d)")
        rk = stf[:, 0:T * NE].rearrange("p (t e) -> p t e", e=NE)
        scn = stf[:, T * NE:2 * T * NE].rearrange("p (t e) -> p t e", e=NE)
        sel = stf[:, 2 * T * NE:5 * T * NE].rearrange("p (m t e) -> p m t e", e=NE, t=T)
        pw = sb("pw", [P, 2, T])
        pwi = sb("pwi", [P, 2, T], I32)
        yg = hst[:, 0, :, :].rearrange("p (a b) d -> p a b d", a=4)
        big = tmpb[0:P, 0:T * NE * NE].rearrange("p (t e j) -> p t e j", e=NE, j=NE)
        big2 = tmpb[0:P, T * NE * NE:2 * T * NE * NE].rearrange("p (t e j) -> p t e j", e=NE, j=NE)
        lg = tmpb[0:P, 2 * T * NE * NE:2 * T * NE * NE + T * NE].rearrange("p (t e) -> p t e", e=NE)
        mu = sm[0:P, 0:T]
        va = sm[0:P, 32:32 + T]
        r0 = sm[0:P, 64:64 + T]
        tot = sm[0:P, 96:96 + T]
        off = sm[0:P, 128:128 + T]
        tt = sm[0:P, 160:160 + T]
        tti = sm[0:P, 192:192 + T].bitcast(I32)
        bs = sm[0:P, 224:224 + T]
        onec = ones[0:P, 0:1]
        var = sm[0:P, 356:372]
        rkv = sm[0:P, 372:380]
        qs = sm[0:P, 256:356]
        kmx = sm[0:P, 384:512]
        mcol = sm[:, 512:513]
        rden = sm[:, 513:514]
        dg = sm[:, 520:648]
        ctxs = sm[:, 648:776]
        ctxT = sm[:, 776:904]
        M0 = sm[:, 904:1160]

        tq = sb("tq", [128, CH, R])
        dsts = sb("dsts", [128, GU * CH])
        typs = sb("typs", [128, GU * CH])
        invs = sb("invs", [128, GU * CH])
        dT = moe[:, 3584:4096].rearrange("p (j c) -> p j c", j=4)
        zer = moe[:, 5 * EC:5 * EC + 512]
        kt = hst[:, 0, 0:2, :].rearrange("p a d -> p (a d)")
        vt = hst[:, 0, 2:4, :].rearrange("p a d -> p (a d)")
        sqv = hst[:, 1, 0:4, :].rearrange("p a d -> p (a d)")
        M1 = moe[:, 0:1024].rearrange("p (j d) -> p j d", d=D)
        wqT = moe[:, 1024:2048].rearrange("p (k j c) -> p k j c", k=KC, j=4)

        pb = [ctx.enter_context(nc.psum_tensor(f"pb{i}", [128, 512], F32)) for i in range(8)]

        s_vec = sem("s_vec")
        s_act = sem("s_act")
        s_pool = sem("s_pool")
        s_xin = sem("s_xin")
        s_edge = sem("s_edge")
        s_par = sem("s_par")
        s_w0 = sem("s_w0")
        s_const = sem("s_const")
        s_zero = sem("s_zero")
        s_zr = sem("s_zr")
        s_zd = sem("s_zd")
        s_lnc = sem("s_lnc")
        s_sq = sem("s_sq")
        s_ln = sem("s_ln")
        s_stg = sem("s_stg")
        s_trn = sem("s_trn")
        s_xT = sem("s_xT")
        s_blk = sem("s_blk")
        s_eva = [sem(f"s_ev{j}") for j in range(6)]
        s_hst = [sem(f"s_hst{j}") for j in range(2)]
        s_pos = sem("s_pos")
        s_cst = sem("s_cst")
        s_sct = [sem(f"s_sct{j}") for j in range(2)]
        s_recl = sem("s_recl")
        s_srt = sem("s_srt")
        s_gix = sem("s_gix")
        s_G = [sem(f"s_G{j}") for j in range(GS)]
        s_oh = sem("s_oh")
        s_oT = sem("s_oT")
        s_oC = sem("s_oC")
        s_iP = sem("s_iP")
        s_iv = sem("s_iv")
        s_col = sem("s_col")
        s_sg = sem("s_sg")
        s_acc = sem("s_acc")
        s_kst = sem("s_kst")
        s_ktr = sem("s_ktr")
        s_kxT = sem("s_kxT")
        s_kmm = sem("s_kmm")
        s_kev = sem("s_kev")
        s_kss = sem("s_kss")
        s_krt = sem("s_krt")
        s_krc = sem("s_krc")
        s_kkk = sem("s_kkk")
        s_q = sem("s_q")
        s_v2p = sem("s_v2p")
        s_v2a = sem("s_v2a")
        s_a2v = sem("s_a2v")
        s_dot = sem("s_dot")
        s_w1l = sem("s_w1l")
        s_wm = sem("s_wm")
        s_cmb = sem("s_cmb")
        s_rt = sem("s_rt")
        s_dsp = sem("s_dsp")
        s_dix = sem("s_dix")
        s_dst = [sem(f"s_dst{j}") for j in range(U)]
        s_dfr = sem("s_dfr")
        s_ml = [sem(f"s_ml{j}") for j in range(2)]
        s_mw1 = [sem(f"s_mw1{j}") for j in range(2)]
        s_mw2 = [sem(f"s_mw2{j}") for j in range(2)]
        s_mt = sem("s_mt")
        s_mx = sem("s_mx")
        s_mh = sem("s_mh")
        s_ma = sem("s_ma")
        s_my = [sem(f"s_my{j}") for j in range(2)]
        s_mo = [sem(f"s_mo{j}") for j in range(2)]
        s_ys = [sem(f"s_ys{j}") for j in range(2)]
        s_cix = sem("s_cix")
        s_cg = [sem(f"s_cg{j}") for j in range(2)]
        s_cmbd = sem("s_cmbd")
        s_out = sem("s_out")
        s_rsv = sem("s_rsv")
        s_rsa = sem("s_rsa")
        s_turn = sem("s_turn")
        s_turn_sp = sem("s_turn_sp")
        s_turn_dve = sem("s_turn_dve")
        s_dt = sem("s_dt")
        s_sqk = sem("s_sqk")
        s_vw = sem("s_vw")
        s_mp = sem("s_mp")
        s_cm1 = sem("s_cm1")

        def row(ap, n=128):
            return ap.partition_broadcast(n)

        hx_v = hx_d.rearrange("(r t p) d -> t p r d", r=R, p=P)
        rec_v = rec_d.rearrange("(p c) f -> p c f", p=128)
        xs_z = xs_d.rearrange("(n p a) d -> n p (a d)", n=SLOTS // 4, p=128)
        x_v = x_in.rearrange("(t p) d -> p t d", p=P)
        out_v = out.rearrange("(t p) d -> p t d", p=P)
        NEV = [0, 0, 0, 0, 0, 0]

        w_hx = [(wcat[:, :, 512 * j:512 * (j + 1)], "av"[j % 2]) for j in range(4)]
        w_loop = [(wcat[:, :, R * D:(R + 1) * D], "v")]
        wkv = wcat[:, :, 0:1024]
        PASSES = {}

        def tile_pass(name, nk, blocks):
            k = len(PASSES)
            inst = dict(k=k, nk=nk, blocks=blocks, ev=[NEV[j] for j in range(len(blocks))],
                        blk=sum(len(q["blocks"]) * T for q in PASSES.values()))
            for j in range(len(blocks)):
                NEV[j] += T
            PASSES[name] = inst

        M0v = M0.rearrange("p (k n) -> p k n", k=1)
        P1v = moe[:, 3072:3584].rearrange("p (k d) -> p k d", d=D)
        tile_pass("gnn0", KC, w_hx + w_loop + [(wq0[:, :, :], "v")])
        tile_pass("mix0", 1, [(M0v, "v")])
        tile_pass("gate0", KC, [(wg[:, 0, :, :], "v")])
        tile_pass("gnn1", KC, w_hx + w_loop)
        tile_pass("gnn2", KC, w_hx + w_loop)
        tile_pass("gate1", KC, [(wg[:, 1, :, :], "v")])
        HSTN = {"gnn0": 0, "gnn1": 1, "gnn2": 2}

        def pass_act(act, name, source, evac=None, func=ACT.Copy):
            q = PASSES[name]
            k0, nk, nb = q["k"] * T, q["nk"], len(q["blocks"])
            with act.Fori(0, TI) as i:
                act.wait_ge(s_trn, HEAD + k0 + i * U)
                for s in range(U):
                    nc.scalar.activation(stage[:, s, 0:nk * 128], source(i * U + s), func).then_inc(s_stg, 1)
                for s in range(U):
                    t = i * U + s
                    act.wait_ge(s_trn, HEAD + k0 + t + 1)
                    act.wait_ge(s_blk, HEAD + q["blk"] + nb * U * i)
                    nc.scalar.activation(xT[:, s, 0:nk, :], pb[6 + s % 2][:, 0:nk * P].rearrange(
                        "p (k n) -> p k n", n=P), ACT.Copy).then_inc(s_xT, 1)
                    for j, (_, e) in enumerate(q["blocks"]):
                        if e == "a":
                            act.wait_ge(s_blk, HEAD + q["blk"] + nb * t + j + 1)
                            evac(act, i, s, j)

        def pass_pe(pe, name, more=None):
            q = PASSES[name]
            k0, nk, nb = q["k"] * T, q["nk"], len(q["blocks"])

            def transposes(i, s):
                t = i * U + s
                pe.wait_ge(s_stg, k0 + t + 1)
                if s >= 2:
                    pe.wait_ge(s_xT, HEAD + k0 + t - 1)
                else:
                    pe.wait_ge(s_xT, HEAD + k0 + i * U)
                for k in range(nk):
                    last = nc.tensor.transpose(pb[6 + s % 2][:, P * k:P * (k + 1)],
                                               stage[:, s, 128 * k:128 * (k + 1)], ident[0:P, 0:P])
                last.then_inc(s_trn, 1)

            with pe.Fori(0, TI) as i:
                transposes(i, 0)
                for s in range(U):
                    if s + 1 < U:
                        transposes(i, s + 1)
                    t = i * U + s
                    pe.wait_ge(s_xT, HEAD + k0 + t + 1)
                    for j, (w, _) in enumerate(q["blocks"]):
                        pe.wait_ge(s_eva[j], HEAD + q["ev"][j] + t)
                        n = w.shape[2]
                        for k in range(nk):
                            last = nc.tensor.matmul(pb[j][0:P, 0:n], xT[:, s, k, :], w[:, k, :],
                                                    start=(k == 0), stop=(k == nk - 1))
                        last.then_inc(s_blk, 1)
                    if more:
                        more(i, s)

        def pass_dve(dve, name, evac):
            q = PASSES[name]
            nb = len(q["blocks"])
            with dve.Fori(0, TI) as i:
                for s in range(U):
                    t = i * U + s
                    for j, (_, e) in enumerate(q["blocks"]):
                        if e == "v":
                            dve.wait_ge(s_blk, HEAD + q["blk"] + nb * t + j + 1)
                            evac(dve, i, s, j)

        def hx_free(eng, name, i, s):
            n = HSTN[name]
            per = (3, 2)[s % 2]
            eng.wait_ge(s_hst[s % 2], HEAD_DMA + 16 * (n * per * TI + per * i + s // 2))

        def hx_copy(eng, name, copy):
            def evac(e, i, s, j):
                hx_free(e, name, i, s)
                copy(hst[:, s % 2, 2 * j:2 * j + 2, :], pb[j][0:P, :].rearrange("p (a d) -> p a d", d=D))\
                    .then_inc(s_eva[j], 1)
            return evac

        def hx_store(sp, name):
            q = PASSES[name]
            with sp.Fori(0, TI) as i:
                for s in range(U):
                    for j in range(4):
                        sp.wait_ge(s_eva[j], HEAD + q["ev"][j] + i * U + s + 1)
                        sp.sem_inc(s_turn_sp, 1)
                    sp.dma_start(hx_v[bass.ds(i * U + s, 1), :, :, :].rearrange("a p r d -> (a p) r d"),
                                 hst[:, s % 2, :, :]).then_inc(s_hst[s % 2], 16)

        def hx_done(eng, name):
            n = HSTN[name] + 1
            for z, per in enumerate((3, 2)):
                eng.wait_ge(s_hst[z], HEAD_DMA + 16 * n * per * TI)

        H = [f0_w1.shape[2], f1_w1.shape[2]]
        MW = [(f0_w1, f0_b1, f0_w2, f0_b2, None, None), (f1_w1, f1_b1, f1_w2, f1_b2, f1_g, f1_b)]
        wreg = [tmpb, accb]
        NLOAD = [2, 4]

        def gnn_weights_sp(sp, n):
            for k in range(KC):
                sp.dma_start(tmpb[:, 1024 * k:1024 * (k + 1)].rearrange("p (b n) -> p b n", b=4),
                             bases[n].rearrange("b (k p) n -> k p b n", p=128)[k]).then_inc(s_w1l, 16)
                sp.dma_start(wcat[:, k, R * D:], roots[n].rearrange("(k p) n -> k p n", p=128)[k]).then_inc(s_w1l, 16)

        def mw1(n, z):
            return wreg[z][:, 0:2 * H[n]].rearrange("p (k h) -> p k h", k=KC)

        def mw2(n, z):
            return wreg[z][:, 2048:2048 + 2 * H[n]].rearrange("p (j d) -> p j d", d=D)

        def moe_sp(sp, n):
            w1, b1, w2, b2, g, b = MW[n]
            HC = H[n] // 128
            sp.wait_ge(s_rt, n + 1)
            for s in range(U):
                sp.wait_ge(s_dst[s], 32 * TI * (n + 1))

            def store(i, z):
                sp.wait_ge(s_mo[z], HEAD + n * SLOTS // 2 + i + 1)
                sp.dma_start(ys_d.rearrange("(m a p) d -> m p a d", p=128, a=2)[bass.ds(2 * i + z, 1)]
                             .rearrange("m p a d -> (m p) a d"), ysb[z]).then_inc(s_ys[z], 16)

            def load_rows(i, z):
                e = sp.value_load(eidr[0:1, n, bass.ds(2 * i + z, 1)], min_val=0, max_val=NE - 1)
                sp.dma_start(xsr[z], xs_d.rearrange("(m a p) d -> m p a d", p=128, a=2)[bass.ds(2 * i + z, 1)]
                             .rearrange("m p a d -> (m p) a d")).then_inc(s_ml[z], 16)
                sp.dma_start(par[0:HC, z, :], b1[bass.ds(e, 1)].rearrange("a (j p) -> (a j) p", p=128)).then_inc(s_ml[z], 16)
                if g is not None:
                    for m, v in enumerate((g, b)):
                        sp.dma_start(par[HC + 2 * m:HC + 2 * m + 2, z, :],
                                     v[bass.ds(e, 1)].rearrange("a (j p) -> (a j) p", p=128)).then_inc(s_ml[z], 16)
                sp.dma_start(mw1(n, z), w1[bass.ds(e, 1)].rearrange("a (k p) h -> (a p) k h", p=128)).then_inc(s_mw1[z], 16)

            def load_second(i, z):
                e = sp.value_load(eidr[0:1, n, bass.ds(2 * i + z, 1)], min_val=0, max_val=NE - 1)
                sp.dma_start(mw2(n, z), w2[bass.ds(e, 1)].rearrange("a (j p) d -> (a p) j d", p=128)).then_inc(s_mw2[z], 16)
                sp.dma_start(b2c[:, z, :], b2[bass.ds(e, 1)].rearrange("a d -> (a d)").partition_broadcast(128))\
                    .then_inc(s_mw2[z], 16)

            for z in range(2):
                load_rows(0, z)
                load_second(0, z)
            with sp.Fori(0, SLOTS // 2 - 1) as i:
                for z in range(2):
                    sp.wait_ge(s_mh, HEAD + (0, SLOTS * (H[0] // 128))[n] + HC * (2 * i + z + 1))
                    load_rows(i + 1, z)
                    store(i, z)
                    load_second(i + 1, z)
            for z in range(2):
                store(SLOTS // 2 - 1, z)

        def bins(engine, first):
            return nc.values_load_multi_w_load_instructions(binr[0:1, bass.ds(first, GU)], [engine],
                                                            min_val=0, max_val=T - 1,
                                                            skip_runtime_bounds_check_because="a count of the T - 1 "
                                                            "tiles after the first")[1]

        def groups(eng, body, first=0):
            with eng.Fori(first, GR) as i:
                for u in range(GU):
                    body(i, u)
            for u in range(GROUPS % GU):
                body(GR, u)

        def groups_beside(eng, n, body, beside):
            for u in range(GU):
                body(0, u)
                beside(0, u, True, False)
            with eng.Fori(1, T) as i:
                for u in range(GU):
                    body(i, u)
                    beside(i, u, True, n == 1)
            if n == 1:
                for u in range(GU):
                    beside(T, u, False, True)
            groups(eng, body, T)

        def gather_pool(pool, n):
            g = nc.gpsimd

            def rows(i, u):
                q, half = u % GS, u // GS
                at = n * GROUPS + i * GU + u
                if q == 0:
                    pool.wait_ge(s_sg, HEAD + at - GS)
                    g.tensor_copy(gixs[:, half, :, :], gid[:, bass.ds((i * GU + u) * CH, GS * CH)]
                                  .rearrange("p (a b) -> p a b", b=CH)).then_inc(s_gix, 1)
                    pool.wait_ge(s_gix, n * (GROUPS // GS) + i * 2 + half + 1)
                pool.wait_ge(s_sg, HEAD + at - GS + 1)
                pool.sem_inc(s_turn, 1)
                for c in range(CH):
                    g.indirect_dma_start(G[:, q, c, :], None, hx_d,
                                         bass.IndirectOffsetOnAxis(gixs[:, half, q, c:c + 1], axis=0)).then_inc(s_G[q], 16)
            groups(pool, rows)

        def dispatch_pool(pool, n):
            g = nc.gpsimd
            pool.wait_ge(s_rt, n + 1)
            with pool.Fori(0, TI) as i:
                for m in range(2):
                    g.tensor_copy(mix[:, m, :], pwi[:, m, bass.ds(i * U, U)]).then_inc(s_dix, 1)
                pool.wait_ge(s_dix, 2 * (n * TI + i) + 2)
                for s in range(U):
                    pool.wait_ge(s_dsp, n * T + i * U + s + 1)
                    pool.sem_inc(s_turn, 1)
                    for m in range(2):
                        g.indirect_dma_start(xs_d, bass.IndirectOffsetOnAxis(mix[:, m, s:s + 1], axis=0),
                                             stage[:, s, :], None).then_inc(s_dst[s], 16)
                for s in range(U):
                    pool.wait_ge(s_dst[s], 32 * (n * TI + i + 1))
                    pool.sem_inc(s_dfr, 1)

        def combine_pool(pool, n):
            g = nc.gpsimd
            for z in range(2):
                pool.wait_ge(s_ys[z], HEAD_DMA + 16 * SLOTS // 2 * (n + 1))
            with pool.Fori(0, TI) as i:
                pool.wait_ge(s_cmbd, HEAD + n * T + i * U)
                for m in range(2):
                    g.tensor_copy(mix[:, m, :], pwi[:, m, bass.ds(i * U, U)]).then_inc(s_cix, 1)
                pool.wait_ge(s_cix, 2 * (n * TI + i) + 2)
                for s in range(U):
                    if s >= 2:
                        pool.wait_ge(s_cmbd, HEAD + n * T + i * U + s - 1)
                    pool.sem_inc(s_turn, 1)
                    for m in range(2):
                        g.indirect_dma_start(yg[:, s % 2, m, :], None, ys_d,
                                             bass.IndirectOffsetOnAxis(mix[:, m, s:s + 1], axis=0))\
                            .then_inc(s_cg[s % 2], 16)

        def prefix_pe(pe, n, operand):
            pe.wait_ge(s_v2p, operand)
            nc.tensor.matmul(pb[7][0:P, 0:n], tri[0:P, 0:P], tot[:, 0:n], start=True, stop=True)
            nc.tensor.matmul(pb[6][0:P, 0:n], ones[0:P, 0:P], tot[:, 0:n], start=True, stop=True).then_inc(s_q, 1)

        def gather_pe(pe, n):
            banks = 4 if n == 0 else 2

            def invert_t(g, q):
                if not isinstance(g, int) or g > 0:
                    pe.wait_ge(s_oC, g)
                for c in range(CH):
                    last = nc.tensor.transpose(pb[2][0:P, 128 * c:128 * (c + 1)], ohs[q][:, c, :], ident[:, :])
                last.then_inc(s_oT, 1)

            tiles = []

            def invert_m(g, z, b, first=False):
                if not first:
                    pe.wait_ge(s_iv, g)
                for c in range(CH):
                    last = nc.tensor.matmul(pb[3][:, R * c:R * (c + 1)], ohT[:, z, c, :],
                                            cnt[:, bass.ds(b, 1), :].rearrange("p a r -> p (a r)"), start=True, stop=True)
                last.then_inc(s_iP, 1)

            def sums(i, u):
                g = i * GU + u
                at = n * GROUPS + g
                q = u % GS
                if n == 1:
                    if u == 0:
                        tiles[:] = bins(mybir.EngineType.PE, g + 3)
                    invert_m(g + 3, (u + 3) % 2, tiles[u])
                else:
                    pe.wait_ge(s_oh, ohb[n] + g + 1)
                pe.wait_ge(s_G[q], 16 * CH * (n * (GROUPS // GS) + i * 2 + u // GS + 1))
                pe.wait_ge(s_acc, HEAD + at - banks + 1)
                for c in range(CH):
                    last = nc.tensor.matmul(pb[u % banks][0:P, 0:D], ohs[u if n == 1 else q][:, c, :], G[:, q, c, :],
                                            start=(c == 0), stop=(c == CH - 1))
                if n == 0:
                    for c in range(CH):
                        last = nc.tensor.matmul(pb[4 + u % banks][0:P, 0:R], oh[:, q, c, :],
                                                toh[:, bass.ds(g * CH + c, 1), :].rearrange("p a r -> p (a r)"),
                                                start=(c == 0), stop=(c == CH - 1))
                last.then_inc(s_sg, 1)
                if n == 1:
                    invert_t(g + 5, (u + 5) % OS)

            if n == 1:
                tiles[:] = bins(mybir.EngineType.PE, 0)
                pe.wait_ge(s_oh, ohb[1] + OL)
                invert_t(0, 0)
                invert_t(1, 1)
                for q in range(3):
                    invert_m(q, q % 2, tiles[q], q == 0)
                    invert_t(q + 2, q + 2)
            if n == 0:
                groups(pe, sums)
                return

            def beside(i, u, now, late):
                k = (n - 1) * T + i
                if now and u == 1:
                    pe.wait_ge(s_kst, k + 1)
                    for c in range(KC):
                        last = nc.tensor.transpose(pb[7][:, P * c:P * (c + 1)], stage[:, 0, 128 * c:128 * (c + 1)],
                                                   ident[0:P, 0:P])
                    last.then_inc(s_ktr, 1)
                if late and u in (3, 4):
                    pe.wait_ge(s_kkk, HEAD + i)
                    pe.wait_ge(s_kev, HEAD + i)
                    for h in (2 * (u - 3), 2 * (u - 3) + 1):
                        last = nc.tensor.matmul(pb[6][:, 128 * h:128 * (h + 1)], vt[:, 128 * h:128 * (h + 1)],
                                                kt[:, 128 * h:128 * (h + 1)], start=False, stop=False,
                                                skip_group_check=True)
                    if u == 4:
                        last.then_inc(s_dt, 1)
                if now and n == 1 and u in (3, 4, 5, 6):
                    if u == 3:
                        pe.wait_ge(s_kxT, k + 1)
                    pe.wait_ge((s_kkk, s_kev)[(u - 3) // 2], HEAD + i)
                    c, kv = (u - 3) % 2, (u - 3) // 2
                    last = nc.tensor.matmul(pb[4 + kv][0:P, :], xT[:, 0, c, :], wkv[:, c, 512 * kv:512 * (kv + 1)],
                                            start=(c == 0), stop=(c == KC - 1))
                    if c == KC - 1:
                        last.then_inc(s_kmm, 1)
                if now and n == 2 and u == 3:
                    pe.wait_ge(s_kxT, k + 1)
                    pe.wait_ge(s_kev, HEAD + k)
                    for c in range(KC):
                        last = nc.tensor.matmul(pb[3][0:P, 0:D], xT[:, 0, c, :], P1v[:, c, :],
                                                start=(c == 0), stop=(c == KC - 1))
                    last.then_inc(s_kmm, 1)

            groups_beside(pe, n, sums, beside)

        def moe_pe(pe, n):
            HC = H[n] // 128
            NL = 16 * NLOAD[n]
            b0 = (0, 16 * NLOAD[0] * (SLOTS // 2))[n]
            hb = (0, SLOTS * (H[0] // 128))[n]
            np_ = HC + (4 if n else 0)

            def transposes(i, z):
                pe.wait_ge(s_ml[z], b0 + NL * (i + 1))
                pe.wait_ge(s_mx, HEAD + n * SLOTS + 2 * i + z)
                for k in range(KC):
                    for a in range(2):
                        nc.tensor.transpose(pb[7][:, 256 * k + 128 * a:256 * k + 128 * (a + 1)],
                                            xsr[z][:, a, 128 * k:128 * (k + 1)], ident[:, :])
                nc.tensor.transpose(pb[6][:, 0:np_], par[0:np_, z, :], ident[0:np_, 0:np_]).then_inc(s_mt, 1)

            def tile(i, z, ahead):
                pe.wait_ge(s_mx, HEAD + n * SLOTS + 2 * i + z + 1)
                pe.wait_ge(s_mw1[z], 16 * (n * SLOTS // 2 + i + 1))
                for j in range(HC):
                    h0 = hb + HC * (2 * i + z) + j
                    pe.wait_ge(s_ma, HEAD + (h0 - 3 if j >= 4 else h0 - j))
                    for k in range(KC):
                        last = nc.tensor.matmul(pb[j % 4][:, 0:SLOT], mw1(n, z)[:, k, 128 * j:128 * (j + 1)],
                                                xsT[z][:, k, :], start=(k == 0), stop=(k == KC - 1))
                    last.then_inc(s_mh, 1)
                if ahead:
                    transposes(*ahead)
                pe.wait_ge(s_mo[z], HEAD + n * SLOTS // 2 + i)
                pe.wait_ge(s_mw2[z], 32 * (n * SLOTS // 2 + i + 1))
                for a in range(2):
                    for j in range(HC):
                        if a == 0:
                            pe.wait_ge(s_ma, HEAD + hb + HC * (2 * i + z) + j + 1)
                        last = nc.tensor.matmul(pb[4 + z][:, D * a:D * (a + 1)],
                                                hT[:, j, 128 * a:128 * (a + 1)], mw2(n, z)[:, j, :],
                                                start=(j == 0), stop=(j == HC - 1))
                last.then_inc(s_my[z], 1)

            transposes(0, 0)
            with pe.Fori(0, SLOTS // 2 - 1) as i:
                tile(i, 0, (i, 1))
                tile(i, 1, (i + 1, 0))
            tile(SLOTS // 2 - 1, 0, (SLOTS // 2 - 1, 1))
            tile(SLOTS // 2 - 1, 1, None)

        def moe_act(act, n):
            HC = H[n] // 128
            hb = (0, SLOTS * (H[0] // 128))[n]
            ac = nc.scalar
            act.wait_ge(s_v2a, (5, 6)[n])
            ac.activation(pw[:, 1, :], pw[:, 1, :], ACT.Exp).then_inc(s_a2v, 1)
            act.wait_ge(s_rt, n + 1)
            with act.Fori(0, TI) as i:
                for s in range(U):
                    act.wait_ge(s_dfr, HEAD + n * T + U * i)
                    ac.activation(stage[:, s, :], xn[:, bass.ds(i * U + s, 1), :].rearrange("p a d -> p (a d)"),
                                  ACT.Copy).then_inc(s_dsp, 1)
            with act.Fori(0, SLOTS // 2) as i:
                for z in range(2):
                    for j in range(HC):
                        h0 = hb + HC * (2 * i + z) + j
                        act.wait_ge(s_mh, HEAD + h0 + 1)
                        act.wait_ge(s_my[1 - z], HEAD + n * SLOTS // 2 + i + z)
                        ac.activation(hT[:, j, :], pb[j % 4][:, 0:SLOT], (ACT.Relu, ACT.Gelu)[n],
                                      bias=parT[:, z, j:j + 1]).then_inc(s_ma, 1)

        def NEVQ(name, j=0):
            return PASSES[name]["ev"][j] + T

        def relation_weights(dve, ch, n):
            v = nc.vector
            dve.wait_ge(s_w1l, 32 * KC * (n + 1))
            for r in range(R):
                for b in range(4):
                    c = compb[:, n, 4 * r + b:4 * r + b + 1]
                    o = wcat[:, :, D * r:D * (r + 1)]
                    i = tmpb[:, 0:2048].rearrange("p (k b n) -> p k b n", k=KC, b=4)[:, :, b, :]
                    if b == 0:
                        ch(v.tensor_scalar(o, i, c, None, ALU.mult))
                    else:
                        ch(v.scalar_tensor_tensor(o, i, c, o, ALU.mult, ALU.add))
            dve.sem_inc(s_cmb, 1)

        def prefix(dve, ch, n, size, shift, q):
            v = nc.vector
            dve.sem_inc(s_v2p, 1)
            dve.wait_ge(s_q, q)
            ch(v.tensor_scalar(tti[:, 0:n], pb[6][0:P, 0:n], float(size - 1), None, ALU.add))
            ch(v.tensor_scalar(tti[:, 0:n], tti[:, 0:n], shift, None, ALU.arith_shift_right))
            ch(v.tensor_copy(tt[:, 0:n], tti[:, 0:n]))
            ch(v.tensor_tensor_scan(bs[:, 0:n], ones[0:P, 0:n], tt[:, 0:n], 0.0, ALU.mult, ALU.add))
            ch(v.tensor_tensor(bs[:, 0:n], bs[:, 0:n], tt[:, 0:n], ALU.subtract))
            ch(v.scalar_tensor_tensor(off[:, 0:n], bs[:, 0:n], float(size), pb[7][0:P, 0:n], ALU.mult, ALU.add))

        def gather_dve(dve, n):
            v = nc.vector
            banks = 4 if n == 0 else 2

            def onehots(g, q, sem_=None):
                for c in range(CH):
                    if n == 1:
                        last = v.tensor_scalar(ohs[q][:, c, :], iota[:, 0:P], dsts[:, q * CH + c:q * CH + c + 1], None,
                                               ALU.is_equal)
                        continue
                    col = g * CH + c
                    if n == 2:
                        last = v.tensor_scalar(oh[:, q, c, :], iota[:, 0:P], dstl[:, bass.ds(col, 1)],
                                               inv[:, bass.ds(col, 1)], ALU.is_equal, ALU.mult)
                    else:
                        last = v.tensor_scalar(oh[:, q, c, :], iota[:, 0:P], dstl[:, bass.ds(col, 1)], None, ALU.is_equal)
                last.then_inc(sem_ or s_oh, 1)

            def stage_round(to, array, i, count):
                v.tensor_copy(to[:, :], array[:, bass.ds(i * GU * CH, GU * CH)]).then_inc(s_col, 1)
                dve.wait_ge(s_col, count)

            def invert(g, q):
                dve.wait_ge(s_iP, HEAD + g + 1)
                for c in range(CH):
                    k = q * CH + c
                    last = v.scalar_tensor_tensor(tq[:, c, :], iota[:, 0:R], typs[:, k:k + 1], pb[3][:, R * c:R * (c + 1)],
                                                  ALU.is_equal, ALU.mult, accum_out=invs[:, k:k + 1])
                last.then_inc(s_iv, 1)

            def keep(i):
                v.tensor_copy(inv[:, bass.ds(i * GU * CH, GU * CH)], invs[:, :])

            tiles = []

            def add(i, u):
                g = i * GU + u
                if n == 1:
                    if u == 5:
                        stage_round(typs, typ, i + 1, 2 + 2 * i + 2)
                    invert(g + 3, (u + 3) % GU)
                    if u == 4:
                        dve.wait_ge(s_iv, g + 4)
                        keep(i)
                if u == 0:
                    tiles[:] = bins(mybir.EngineType.DVE, g)
                b = tiles[u]
                dve.wait_ge(s_acc, HEAD + n * GROUPS + g)
                dve.wait_ge(s_sg, HEAD + n * GROUPS + g + 1)
                at = acc[:, bass.ds(b, 1), :].rearrange("p a d -> p (a d)")
                if n == 0:
                    ct = cnt[:, bass.ds(b, 1), :].rearrange("p a d -> p (a d)")
                    v.tensor_tensor(ct, ct, pb[4 + u % banks][0:P, 0:R], ALU.add)
                last = v.tensor_tensor(at, at, pb[u % banks][0:P, 0:D], ALU.add)
                if n == 1:
                    if u == GU - OL:
                        stage_round(dsts, dstl, i + 1, 2 + 2 * i + 1)
                    onehots(g + OL, (u + OL) % OS, s_acc)
                else:
                    last.then_inc(s_acc, 1)
                    onehots(g + GS, u % GS)

            if n == 1:
                stage_round(dsts, dstl, 0, 1)
                stage_round(typs, typ, 0, 2)
            for q in range(OL if n == 1 else GS):
                onehots(q, q)
            if n == 1:
                for q in range(3):
                    invert(q, q)
            if n == 0:
                groups(dve, add)
                return

            def beside(i, u, now, late):
                k = (n - 1) * T + i
                if now and n == 2 and u == 4:
                    dve.wait_ge(s_kmm, HEAD + 2 * T + i + 1)
                    xt = x[:, bass.ds(i, 1), :].rearrange("p a d -> p (a d)")
                    v.tensor_tensor(xt, pb[3][0:P, 0:D], xt, ALU.add).then_inc(s_kev, 1)
                if late and u == 0:
                    dve.wait_ge(s_sqk, 2 * i)
                    v.tensor_reduce(var[:, 8:16], sqv[:, 512:1024].rearrange("p (h d) -> p h d", d=64), X, ALU.add)\
                        .then_inc(s_kss, 1)
                    dve.wait_ge(s_kss, HEAD + 3 * i - 1)
                    v.tensor_scalar(var, var, 1.0 / 64, EPS, ALU.mult, ALU.add).then_inc(s_kss, 1)
                if late and u == 1:
                    dve.wait_ge(s_krt, i)
                    v.reciprocal(var, var).then_inc(s_krc, 1)
                    dve.wait_ge(s_krc, 2 * i - 1)
                    v.tensor_tensor(rkv, var[:, 0:8], var[:, 8:16], ALU.mult).then_inc(s_krc, 1)
                    dve.wait_ge(s_krc, 2 * i)
                    dve.wait_ge(s_dt, HEAD + i - 1)
                    v.tensor_tensor(kt.rearrange("p (h d) -> p h d", d=64),
                                    pb[4][0:P, :].rearrange("p (h d) -> p h d", d=64),
                                    rkv.unsqueeze(2).to_broadcast([P, 8, 64]), ALU.mult).then_inc(s_kkk, 1)
                if now and n == 1 and u == 6:
                    dve.wait_ge(s_sqk, 2 * i + 1)
                    v.tensor_reduce(var[:, 0:8], sqv[:, 0:512].rearrange("p (h d) -> p h d", d=64), X, ALU.add)\
                        .then_inc(s_kss, 1)

            groups_beside(dve, n, add, beside)
            if n == 1 and GROUPS % GU:
                dve.wait_ge(s_iv, GROUPS + 3)
                keep(GR)

        def gather_act(act, n):
            ac = nc.scalar

            def ahead(g, u):
                act.wait_ge(s_oT, g + 6)
                last = ac.activation(ohT[:, (u + 1) % 2, :, :], pb[2][0:P, 0:CH * 128].rearrange("p (c e) -> p c e", e=128),
                                     ACT.Copy)
                if not isinstance(g, int) or -2 <= g < GROUPS - 2:
                    q = (u + 2) % OS
                    for c in range(CH):
                        last = ac.activation(ohs[q][:, c, :], ohs[q][:, c, :], ACT.Copy,
                                             scale=invs[:, q * CH + c:q * CH + c + 1])
                last.then_inc(s_oC, 1)

            def beside(i, u, now, late):
                k = (n - 1) * T + i
                if late and u == 0:
                    act.wait_ge(s_kmm, HEAD + 2 * i)
                    act.wait_ge(s_dt, HEAD + i - 1)
                    ac.activation(vt, pb[5][0:P, :], ACT.Copy).then_inc(s_kev, 1)
                if now and u == 0:
                    act.wait_ge(s_ktr, HEAD + k)
                    ac.activation(stage[:, 0, :], xn[:, bass.ds(i, 1), :].rearrange("p a d -> p (a d)"), ACT.Copy)\
                        .then_inc(s_kst, 1)
                if late and u == 1:
                    act.wait_ge(s_kss, HEAD + 3 * i)
                    ac.activation(var, var, ACT.Sqrt).then_inc(s_krt, 1)
                if now and u == 2:
                    act.wait_ge(s_ktr, HEAD + k + 1)
                    act.wait_ge(s_kmm, HEAD + (2 * i if n == 1 else 2 * T + i))
                    ac.activation(xT[:, 0, :, :], pb[7][:, 0:KC * P].rearrange("p (k n) -> p k n", n=P), ACT.Copy)\
                        .then_inc(s_kxT, 1)
                if now and n == 1 and u in (5, 7):
                    kv = (u - 5) // 2
                    act.wait_ge(s_kmm, HEAD + 2 * i + kv + 1)
                    act.wait_ge(s_kss, HEAD + 3 * i)
                    ac.activation(sqv[:, 512 * kv:512 * (kv + 1)], pb[4 + kv][0:P, :], ACT.Square).then_inc(s_sqk, 1)

            if n == 1:
                for g in range(-5, 0):
                    ahead(g, g)
                groups_beside(act, n, lambda i, u: ahead(i * GU + u, u), beside)
            else:
                with act.Fori(0, T) as i:
                    for u in range(GU):
                        beside(i, u, True, False)

        def moe_dve(dve, ch, n):
            v = nc.vector
            name = ("gate0", "gate1")[n]
            HC = H[n] // 128

            gb = gatb[:, 3, :]
            if n == 0:
                ch(v.tensor_tensor(gb, gatb[:, 0, :], gatb[:, 1, :], ALU.add))
            else:
                ch(v.tensor_copy(gb, gatb[:, 2, :]))

            def evac(e, i, s, j):
                v.tensor_tensor(lg[:, bass.ds(i * U + s, 1), :].rearrange("p a e -> p (a e)"), pb[0][0:P, 0:NE], gb,
                                ALU.add).then_inc(s_eva[0], 1)
            pass_dve(dve, name, evac)
            dve.wait_ge(s_eva[0], HEAD + NEVQ(name))
            lj = lg[:, :, :].unsqueeze(2).to_broadcast([P, T, NE, NE])
            le = lg[:, :, :].unsqueeze(3).to_broadcast([P, T, NE, NE])
            ch.step(v.tensor_tensor(big, lj, le, ALU.is_gt))
            ch(v.tensor_tensor(big2, lj, le, ALU.is_equal))
            ch(v.tensor_tensor(big2, big2, ltm[:, :, :].unsqueeze(1).to_broadcast([P, T, NE, NE]), ALU.mult))
            ch(v.tensor_tensor(big, big, big2, ALU.add))
            ch(v.tensor_reduce(rk[:, :, :], big, X, ALU.add))
            for m in range(2):
                ch(v.tensor_scalar(sel[:, m], rk[:, :, :], float(m), None, ALU.is_equal))
            ch(v.tensor_tensor(sel[:, 2], sel[:, 0], sel[:, 1], ALU.add))
            for m in range(2):
                ch(v.tensor_tensor(rk[:, :, :], sel[:, m], lg[:, :, :], ALU.mult))
                ch(v.tensor_reduce(pw[:, m, :], rk[:, :, :], X, ALU.add))
            v.tensor_tensor(pw[:, 1, :], pw[:, 1, :], pw[:, 0, :], ALU.subtract).then_inc(s_v2a, 1)
            dve.wait_ge(s_a2v, 3 + n)
            ch(v.tensor_scalar(pw[:, 0, :], pw[:, 1, :], 1.0, None, ALU.add))
            ch(v.reciprocal(pw[:, 0, :], pw[:, 0, :]))
            ch(v.tensor_tensor(pw[:, 1, :], pw[:, 1, :], pw[:, 0, :], ALU.mult))
            for e in range(NE):
                ch(v.tensor_tensor_scan(scn[:, :, e], ones[0:P, 0:T], sel[:, 2, :, e], 0.0, ALU.mult, ALU.add))
            ch(v.tensor_copy(tot[:, 0:NE], scn[:, T - 1, :]))
            prefix(dve, ch, NE, SLOT, 8, (7, 16)[n])
            ch(v.tensor_tensor(scn[:, :, :], scn[:, :, :], off[:, 0:NE].unsqueeze(1).to_broadcast([P, T, NE]), ALU.add))
            ch(v.tensor_scalar(scn[:, :, :], scn[:, :, :], -1.0, None, ALU.add))
            for m in range(2):
                ch(v.tensor_tensor(rk[:, :, :], sel[:, m], scn[:, :, :], ALU.mult))
                ch(v.tensor_reduce(mu, rk[:, :, :], X, ALU.add))
                ch(v.tensor_copy(pwi[:, m, :], mu))
            sl = sel[0:1, 0, 0:8, :].rearrange("p a b -> p (a b)")[:, 0:SLOTS]
            s2 = sel[0:1, 1, 0:8, :].rearrange("p a b -> p (a b)")[:, 0:SLOTS]
            ch(v.memset(sl, 0.0))
            for e in range(1, NE):
                ch(v.tensor_scalar(s2, iota[0:1, 0:SLOTS], bs[0:1, e:e + 1], None, ALU.is_ge))
                ch(v.tensor_tensor(sl, sl, s2, ALU.add))
            ch(v.tensor_copy(eidr[:, n, :], sl))
            dve.sem_inc(s_rt, 1)
            def operands(i, z):
                t = n * SLOTS + 2 * i + z
                dve.wait_ge(s_mt, t + 1)
                np_ = HC + (4 if n else 0)
                v.tensor_copy(parT[:, z, 0:np_], pb[6][:, 0:np_]).then_inc(s_mp, 1)
                dve.wait_ge(s_mp, t + 1)
                for k in range(KC):
                    tp = pb[7][:, SLOT * k:SLOT * (k + 1)]
                    if n:
                        last = v.tensor_scalar(xsT[z][:, k, :], tp, parT[:, z, HC + k:HC + k + 1],
                                               parT[:, z, HC + 2 + k:HC + 3 + k], ALU.mult, ALU.add)
                    else:
                        last = v.tensor_copy(xsT[z][:, k, :], tp)
                last.then_inc(s_mx, 1)

            def outputs(i, z):
                dve.wait_ge(s_my[z], HEAD + n * SLOTS // 2 + i + 1)
                dve.wait_ge(s_ys[z], HEAD_DMA + 16 * (n * SLOTS // 2 + i))
                v.tensor_tensor(ysb[z], pb[4 + z][:, :].rearrange("p (a d) -> p a d", d=D),
                                b2c[:, z, :].unsqueeze(1).to_broadcast([128, 2, D]), ALU.add).then_inc(s_mo[z], 1)

            operands(0, 0)
            with dve.Fori(0, SLOTS // 2 - 1) as i:
                operands(i, 1)
                outputs(i, 0)
                operands(i + 1, 0)
                outputs(i, 1)
            operands(SLOTS // 2 - 1, 1)
            for z in range(2):
                outputs(SLOTS // 2 - 1, z)
            with dve.Fori(0, TI) as i:
                for s in range(U):
                    t = i * U + s
                    per = (3, 2)[s % 2]
                    dve.wait_ge(s_cg[s % 2], 32 * (n * TI * per + per * i + s // 2 + 1))
                    xt = x[:, bass.ds(t, 1), :].rearrange("p a d -> p (a d)")
                    v.scalar_tensor_tensor(xt, yg[:, s % 2, 0, :], pw[:, 0, bass.ds(t, 1)], xt, ALU.mult, ALU.add)\
                        .then_inc(s_cm1, 1)
                    dve.wait_ge(s_cm1, n * T + t + 1)
                    v.scalar_tensor_tensor(xt, yg[:, s % 2, 1, :], pw[:, 1, bass.ds(t, 1)], xt, ALU.mult, ALU.add)\
                        .then_inc(s_cmbd, 1)
            dve.wait_ge(s_cmbd, HEAD + (n + 1) * T)



        block = ctx.enter_context(nc.Block())

        @block.sync
        def _(sp):
            for m in s_hst + s_ys:
                sp.sem_inc(m, HEAD_DMA)
            for n, a in enumerate((src, dst, etype)):
                sp.dma_start(SA[n].bitcast(I32), a.rearrange("(p c) -> p c", p=P)).then_inc(s_edge, 16)
            sp.dma_start(x[:, :, :], x_v).then_inc(s_xin, 16)
            sp.wait_ge(s_zero, 2)
            sp.dma_start(rec_v, unused).then_inc(s_zr, 16)
            for k in range(KC):
                sp.dma_start(wcat[:, k, 0:R * D].rearrange("p (r n) -> p r n", r=R),
                             w0.rearrange("r (k p) n -> k p r n", p=128)[k]).then_inc(s_w0, 16)
                sp.dma_start(wcat[:, k, R * D:], wl0.rearrange("(k p) n -> k p n", p=128)[k]).then_inc(s_w0, 16)
                sp.dma_start(wq0[:, k, :], wqkv0.rearrange("(k p) n -> k p n", p=128)[k]).then_inc(s_w0, 16)
                sp.dma_start(wg[:, 0, k, :], f0_wg.rearrange("(k p) n -> k p n", p=128)[k]).then_inc(s_par, 16)
                sp.dma_start(wg[:, 1, k, :], f1_wr.rearrange("(k p) n -> k p n", p=128)[k]).then_inc(s_par, 16)
            sp.dma_start(gpre[:, :], gpre0.rearrange("(k p) -> p k", p=128), allow_slow_non_contiguous=True).then_inc(s_par, 16)
            for h in range(4):
                sp.dma_start(memk[:, 32 * h:32 * h + 32], memkv[0, h].rearrange("d m -> m d"), allow_slow_non_contiguous=True).then_inc(s_par, 16)
                sp.dma_start(memv[:, 32 * h:32 * h + 32], memkv[1, h].rearrange("d m -> m d"), allow_slow_non_contiguous=True).then_inc(s_par, 16)
            sp.dma_start(wo0[:, :], wout0).then_inc(s_par, 16)
            for n, a in enumerate((hb0, bout0, gout0, biases[0], biases[1], bout1)):
                sp.dma_start(bc[:, n, :], row(a)).then_inc(s_par, 16)
            for n in range(2):
                sp.dma_start(compb[:, n, :], row(comps[n].rearrange("r b -> (r b)"))).then_inc(s_par, 16)
            for n, a in enumerate((f0_bg, f0_bias, f1_br)):
                sp.dma_start(gatb[:, n, :], row(a, P)).then_inc(s_par, 16)
            for n in range(SLOTS // 4):
                sp.dma_start(xs_z[n], zeros).then_inc(s_zd, 16)

            hx_store(sp, "gnn0")
            for z in range(2):
                sp.wait_ge(s_sct[z], 16 * SCU * (EC // (2 * SCU)))
            sp.dma_start(recs[:, :, :], rec_v).then_inc(s_recl, 16)
            moe_sp(sp, 0)
            sp.wait_ge(s_ln, 3)
            gnn_weights_sp(sp, 0)
            for k in range(KC):
                sp.dma_start(wq1[:, k, :], wqkv1.rearrange("(k p) n -> k p n", p=128)[k][:, 0:512]).then_inc(s_wm, 16)
            sp.dma_start(wo1, wout1.rearrange("(j p) n -> p j n", p=128)).then_inc(s_wm, 16)
            hx_store(sp, "gnn1")
            sp.wait_ge(s_blk, HEAD + PASSES["gnn2"]["blk"])
            for k in range(KC):
                sp.dma_start(wkv[:, k, :], wqkv1.rearrange("(k p) n -> k p n", p=128)[k][:, 512:1536]).then_inc(s_wm, 16)
            sp.wait_ge(s_v2p, 9)
            gnn_weights_sp(sp, 1)
            hx_store(sp, "gnn2")
            moe_sp(sp, 1)
            for n in range(TI):
                sp.wait_ge(s_cmbd, HEAD + T + U * (n + 1))
                sp.dma_start(out_v[:, U * n:U * (n + 1), :], x[:, U * n:U * (n + 1), :]).then_inc(s_out, 16)
            sp.wait_ge(s_out, 16 * TI)


        @block.gpsimd
        def _(pool):
            ch = Chain(pool, s_pool)
            g = nc.gpsimd
            pool.sem_inc(s_dfr, HEAD)
            ch.step(g.memset(zeros, 0.0))
            ch.step(g.memset(unused, 0))
            ch.wait()
            ch.step(g.memset(unused[:, :, 1:2].bitcast(F32), -1.0))
            ch.step(g.memset(unused[:, :, 3:4].bitcast(F32), -1.0))
            ch.wait()
            g.memset(ident[:, :], 0.0).then_inc(s_zero, 2)
            ch.step(g.memset(ones[:, :], 1.0))
            ch.step(g.memset(tri[:, :], 1.0))
            ch.step(g.memset(bmask[:, :], 32 ** -0.5))
            ch.step(g.memset(bmask1[:, :], 1.0 / NODES))
            ch.step(g.memset(ltm[:, :, :], 1.0))
            ch.step(g.memset(memv[:, 128:129], 1.0))
            ch.wait()
            pool.wait_ge(s_zero, 2)
            ch.step(g.affine_select(out=ident[:, :], in_=ident[:, :], compare_op=ALU.not_equal, fill=1.0,
                                    base=0, pattern=[[-1, 128]], channel_multiplier=1))
            ch.step(g.affine_select(out=tri[:, :], in_=tri[:, :], compare_op=ALU.is_gt, fill=0.0,
                                    base=0, pattern=[[1, 128]], channel_multiplier=-1))
            ch.step(g.affine_select(out=ltm[:, :, :], in_=ltm[:, :, :], compare_op=ALU.is_gt, fill=0.0,
                                    base=0, pattern=[[1, NE], [-1, NE]], channel_multiplier=0))
            for m, b in ((bmask, 32), (bmask1, 64)):
                v = m[:, :].rearrange("p (a c) -> p a c", c=b)
                ch(g.affine_select(out=v, in_=v, compare_op=ALU.is_ge, fill=0.0, base=0,
                                   pattern=[[-b, 128 // b], [0, b]], channel_multiplier=1))
                ch(g.affine_select(out=v, in_=v, compare_op=ALU.is_ge, fill=0.0, base=b - 1,
                                   pattern=[[b, 128 // b], [0, b]], channel_multiplier=-1))
            ch.step(g.iota(iota[:, :], [[1, GROUPS + GU]], base=0, channel_multiplier=0,
                           allow_small_or_imprecise_dtypes=True))
            ch.wait()
            g.memset(dstl[:, COLS:], -1.0).then_inc(s_const, 1)
            ch(g.memset(typ[:, COLS:], -1.0))
            g.memset(inv[:, COLS:], 0.0).then_inc(s_const, 1)
            pool.wait_ge(s_pos, 1)
            pool.wait_ge(s_zr, 16)
            def scatter(i, first):
                for z in range(2):
                    c = i * 2 * SCU + z * SCU
                    if not first:
                        pool.wait_ge(s_sct[z], 16 * SCU * i)
                    g.tensor_copy(scix[:, z, :], posi[:, bass.ds(c, SCU)]).then_inc(s_cst, 1)
                    g.tensor_copy(scrc[:, z, :, :], rec[:, bass.ds(c, SCU), :]).then_inc(s_cst, 1)
                    pool.wait_ge(s_cst, 4 * i + 2 * z + 2)
                    pool.sem_inc(s_turn, 1)
                    for m in range(SCU):
                        g.indirect_dma_start(rec_d, bass.IndirectOffsetOnAxis(scix[:, z, m:m + 1], axis=0),
                                             scrc[:, z, m, :], None).then_inc(s_sct[z], 16)

            scatter(0, True)
            with pool.Fori(1, EC // (2 * SCU)) as i:
                scatter(i, False)
            pool.wait_ge(s_srt, 1)
            hx_done(pool, "gnn0")
            gather_pool(pool, 0)
            dispatch_pool(pool, 0)
            combine_pool(pool, 0)
            hx_done(pool, "gnn1")
            gather_pool(pool, 1)
            hx_done(pool, "gnn2")
            gather_pool(pool, 2)
            dispatch_pool(pool, 1)
            combine_pool(pool, 1)


        @block.tensor
        def _(pe):
            for m in [s_trn, s_blk, s_sg, s_dt, s_iP, s_ktr, s_kmm, s_mh] + s_my:
                pe.sem_inc(m, HEAD)
            pe.wait_ge(s_const, 2)

            def done(ins):
                ins.then_inc(s_q, 1)

            prefix_pe(pe, T, 1)
            pe.wait_ge(s_w0, 16 * 3 * KC)
            pe.wait_ge(s_v2p, 2)
            pass_pe(pe, "gnn0")
            pe.wait_ge(s_v2p, 3)
            nc.tensor.transpose(pb[7][:, 0:P], kmx, ident[0:P, 0:P])
            done(nc.tensor.transpose(pb[7][:, P:P + 4], memk[:, :], ident[0:4, 0:4]))
            pe.wait_ge(s_v2p, 4)
            done(nc.tensor.matmul(pb[6][:, 0:128], ones[:, :], dg, start=True, stop=True))
            pe.wait_ge(s_a2v, 2)
            for t in range(T):
                nc.tensor.matmul(pb[7][:, 0:129], tmp[:, t, 128:256], vv[:, t, :], start=(t == 0), stop=False)
            done(nc.tensor.matmul(pb[7][:, 0:129], memk[:, :], memv[:, :], start=False, stop=True))
            pe.wait_ge(s_v2p, 5)
            done(nc.tensor.transpose(pb[6][:, 0:128], ctxs, ident[:, :]))
            pe.wait_ge(s_v2p, 6)
            done(nc.tensor.matmul(pb[6][:, 0:D], ctxT, wo0[:, :], start=True, stop=True))
            pe.wait_ge(s_v2p, 7)
            pass_pe(pe, "mix0")
            gather_pe(pe, 0)
            pe.wait_ge(s_ln, 2)
            pass_pe(pe, "gate0")
            prefix_pe(pe, NE, 8)
            moe_pe(pe, 0)
            pe.wait_ge(s_cmb, 1)
            pass_pe(pe, "gnn1")
            pe.wait_ge(s_v2p, 9)
            nc.tensor.matmul(pb[6][:, :], zer[:, 0:128], zer[:, :], start=True, stop=True, skip_group_check=True)\
                .then_inc(s_dot, 1)
            gather_pe(pe, 1)
            nc.tensor.matmul(pb[5][:, 0:8], zer[:, 0:128], zer[:, 0:8], start=True, stop=True).then_inc(s_dot, 1)
            pe.wait_ge(s_cmb, 2)
            pass_pe(pe, "gnn2")
            pe.wait_ge(s_v2p, 10)
            for j in range(4):
                pe.wait_ge(s_eva[j], HEAD + NEVQ("gnn2", j))
            for j in range(4):
                done(nc.tensor.matmul(pb[j // 2][:, D * (j % 2):D * (j % 2 + 1)], dT[:, j, :], wo1[:, j, :],
                                      start=True, stop=True))
            for k in range(KC):
                for j in range(4):
                    last = nc.tensor.transpose(pb[2 + k][:, 128 * j:128 * (j + 1)],
                                               wq1[:, k, 128 * j:128 * (j + 1)], ident[:, :])
                done(last)
            pe.wait_ge(s_v2p, 11)
            for k in range(KC):
                for j in range(4):
                    last = nc.tensor.matmul(pb[4][:, D * k:D * (k + 1)], wqT[:, k, j, :], M1[:, j, :],
                                            start=(j == 0), stop=(j == 3))
                done(last)
            pe.wait_ge(s_v2p, 12)
            gather_pe(pe, 2)
            pe.wait_ge(s_ln, 4)
            pass_pe(pe, "gate1")
            prefix_pe(pe, NE, 13)
            moe_pe(pe, 1)


        @block.scalar
        def _(act):
            ac = nc.scalar

            def square(src_, dst_):
                ac.activation(dst_, src_, ACT.Square).then_inc(s_sq, 1)

            for m in (s_xT, s_eva[1], s_eva[3], s_ma, s_kev):
                act.sem_inc(m, HEAD)
            RA = [0]

            def root(o, count=None):
                act.wait_ge(s_rsv, (RA[0] if count is None else count) + 1)
                ac.activation(o, o, ACT.Sqrt).then_inc(s_rsa, 1)
                if count is None:
                    RA[0] += 1

            def ln_act(n):
                act.wait_ge(s_lnc, n + 1)
                square(tmp, xn[:, :, :])
                root(va)

            def tsrc(a):
                return lambda t: a[:, bass.ds(t, 1), :].rearrange("p a d -> p (a d)")

            ln_act(0)
            act.wait_ge(s_ln, 1)
            square(xn[:, :, :], tmp)
            root(r0)
            pass_act(act, "gnn0", tsrc(xn), hx_copy(act, "gnn0", lambda o, i: ac.activation(o, i, ACT.Copy)))
            act.wait_ge(s_v2a, 1)
            ac.activation(tmp[:, :, 0:128], tmp[:, :, 0:128], ACT.Exp).then_inc(s_a2v, 1)
            act.wait_ge(s_v2a, 2)
            ac.activation(memk[:, :], memk[:, :], ACT.Exp)
            ac.activation(tmp[:, :, 128:256], tmp[:, :, 128:256], ACT.Exp).then_inc(s_a2v, 1)
            act.wait_ge(s_v2p, 7)
            act.wait_ge(s_v2a, 3)
            pass_act(act, "mix0", lambda t: tmp[:, bass.ds(t, 1), 0:128].rearrange("p a d -> p (a d)"))
            act.wait_ge(s_v2a, 4)
            square(tmp, xn[:, :, :])
            root(va)
            ln_act(1)
            act.wait_ge(s_ln, 2)
            pass_act(act, "gate0", tsrc(xn))
            moe_act(act, 0)
            ln_act(2)
            act.wait_ge(s_ln, 3)
            pass_act(act, "gnn1", tsrc(xn), hx_copy(act, "gnn1", lambda o, i: ac.activation(o, i, ACT.Copy)))

            hx_done(act, "gnn1")
            act.wait_ge(s_v2p, 9)
            gather_act(act, 1)
            act.wait_ge(s_cmb, 2)
            pass_act(act, "gnn2", tsrc(acc), hx_copy(act, "gnn2", lambda o, i: ac.activation(o, i, ACT.Copy)),
                     ACT.Relu)
            gather_act(act, 2)
            ln_act(3)
            act.wait_ge(s_ln, 4)
            pass_act(act, "gate1", tsrc(xn))
            moe_act(act, 1)


        @block.vector
        def _(dve):
            ch = Chain(dve, s_vec)
            v = nc.vector
            AX = X

            def bt(a, n):
                return a.unsqueeze(2).to_broadcast([a.shape[0], a.shape[1], n])

            def btm(a, n):
                return a.unsqueeze(1).to_broadcast([a.shape[0], n, a.shape[1]])

            RS = [0]

            def rsq(o, scale, eps, lo=None, mul=1.0, count=None):
                k = RS[0] if count is None else count
                if lo is None:
                    v.tensor_scalar(o, o, scale, eps, ALU.mult, ALU.add).then_inc(s_rsv, 1)
                else:
                    v.tensor_scalar(o, o, lo, None, ALU.max).then_inc(s_rsv, 1)
                dve.wait_ge(s_rsa, k + 1)
                ch(v.reciprocal(o, o))
                if mul != 1.0:
                    ch(v.tensor_scalar(o, o, mul, None, ALU.mult))
                if count is None:
                    RS[0] += 1

            def ln(n):
                ch(v.tensor_reduce(mu, x[:, :, :], AX, ALU.add))
                ch(v.tensor_scalar(mu, mu, 1.0 / D, None, ALU.mult))
                v.tensor_tensor(tmp, x[:, :, :], bt(mu, D), ALU.subtract).then_inc(s_lnc, 1)
                dve.wait_ge(s_sq, SQ[n])
                ch(v.tensor_reduce(va, xn[:, :, :], AX, ALU.add))
                rsq(va, 1.0 / D, EPS)
                v.tensor_tensor(xn[:, :, :], tmp, bt(va, D), ALU.mult).then_inc(s_ln, 1)
                dve.wait_ge(s_ln, n + 1)

            SQ = [1, 4, 5, 6]
            for m in [s_eva[0], s_eva[2], s_eva[4], s_eva[5], s_acc, s_mx, s_cmbd, s_kss, s_kkk] + s_mo:
                dve.sem_inc(m, HEAD)
            dve.wait_ge(s_edge, 48)
            dve.wait_ge(s_const, 2)
            dst_f, typ_f, bin_f, posf, t1, t2, gof = SA[3], SA[4], SA[5], SA[6], SA[7], SA[8], SA[1]
            ch.step(v.tensor_copy(dst_f, SA[1].bitcast(I32)))
            ch.step(v.tensor_copy(typ_f, SA[2].bitcast(I32)))
            ch(v.tensor_copy(t2, SA[0].bitcast(I32)))
            ch(v.tensor_scalar(t1.bitcast(I32), dst_f, 4195.0, None, ALU.mult))
            ch(v.tensor_scalar(t1.bitcast(I32), t1.bitcast(I32), 19, None, ALU.arith_shift_right))
            ch(v.tensor_copy(bin_f, t1.bitcast(I32)))
            ch.step(v.scalar_tensor_tensor(rec[:, :, 0], typ_f, float(NODES), t2, ALU.mult, ALU.add))
            ch.step(v.scalar_tensor_tensor(rec[:, :, 1].bitcast(F32), bin_f, -float(P), dst_f, ALU.mult, ALU.add))
            ch.step(v.tensor_copy(rec[:, :, 2].bitcast(F32), typ_f))
            ch.step(v.tensor_copy(rec[:, :, 3].bitcast(F32), typ_f))
            one_c = t2
            ch.wait()
            ch(v.memset(one_c, 1.0))
            S0, S1, mask = SA[0], SA[1], SA[2].bitcast(I32)
            with dve.Fori(0, T) as b:
                ch.loop(b, 1)
                ch(v.tensor_scalar(S0, bin_f, iota[0:P, bass.ds(b, 1)], 0.0, ALU.is_equal, ALU.add,
                                   accum_out=tot[:, bass.ds(b, 1)]))
            ch.end(T, 1)
            prefix(dve, ch, T, GROUP, 8, 1)
            with dve.Fori(0, T) as b:
                ch.loop(b, 3)
                ch(v.tensor_scalar(mask, bin_f, iota[0:P, bass.ds(b, 1)], None, ALU.is_equal))
                ch(v.tensor_tensor_scan(S1, one_c, mask, off[:, bass.ds(b, 1)], ALU.mult, ALU.add))
                dve.sem_inc(s_turn_dve, 1)
                ch(v.copy_predicated(posf, mask, S1))
            ch.end(T, 3)
            ch(v.tensor_scalar(posf, posf, -1.0, None, ALU.add))
            ch(v.tensor_copy(posi, posf))
            ch(v.tensor_scalar(S0.bitcast(I32), posi, 7, None, ALU.arith_shift_right))
            ch(v.tensor_copy(S1, S0.bitcast(I32)))
            ch(v.scalar_tensor_tensor(posf, S1, -128.0, posf, ALU.mult, ALU.add))
            ch(v.scalar_tensor_tensor(posf, posf, float(COLS), S1, ALU.mult, ALU.add))
            ch(v.tensor_copy(posi, posf))
            g0, g1 = S0[0:1, 0:GROUPS + GU], S1[0:1, 0:GROUPS + GU]
            ch(v.memset(g0, 0.0))
            for b in range(1, T):
                ch(v.tensor_scalar(g1, iota[0:1, 0:GROUPS + GU], bs[0:1, b:b + 1], None, ALU.is_ge))
                ch(v.tensor_tensor(g0, g0, g1, ALU.add))
            ch(v.tensor_copy(binr[:, :], g0))
            dve.sem_inc(s_pos, 1)

            dve.wait_ge(s_xin, 16)
            dve.wait_ge(s_zr, 16)
            ln(0)
            dve.wait_ge(s_par, 16 * 25)
            dve.wait_ge(s_w0, 16 * 3 * KC)
            for k in range(KC):
                last = v.tensor_scalar(wq0[:, k, :], wq0[:, k, :], gpre[:, k:k + 1], None, ALU.mult)
                last.then_inc(s_vw, 1)
            dve.wait_ge(s_sq, 2)
            ch(v.tensor_reduce(r0, tmp, AX, ALU.add))
            rsq(r0, 1.0, 0.0, 1e-24, D ** 0.5)
            dve.wait_ge(s_vw, KC)

            dve.wait_ge(s_zd, 16 * (SLOTS // 4))
            v.memset(vv[:, :, 128:129], 1.0).then_inc(s_v2p, 1)

            def gnn_evac(name, bias=None, qkv=False):
                hx = hx_copy(dve, name, v.tensor_copy)
                n = HSTN[name]

                def evac(e, i, s, j):
                    t = i * U + s
                    if j < 4:
                        return hx(e, i, s, j)
                    at = acc[:, bass.ds(t, 1), :].rearrange("p a d -> p (a d)")
                    if j == 4:
                        b = bc[0:P, bias, :] if bias is not None else None
                        if b is None:
                            v.tensor_scalar(at, pb[4][0:P, 0:D], 1.0, None, ALU.mult).then_inc(s_eva[4], 1)
                        else:
                            v.tensor_tensor(at, pb[4][0:P, 0:D], b, ALU.add).then_inc(s_eva[4], 1)
                        return
                    v.tensor_scalar(tmp[:, bass.ds(t, 1), :].rearrange("p a d -> p (a d)"), pb[5][0:P, 0:D],
                                    r0[:, bass.ds(t, 1)], None, ALU.mult)
                    v.tensor_scalar(vv[:, bass.ds(t, 1), 0:128].rearrange("p a d -> p (a d)"), pb[5][0:P, D:384],
                                    r0[:, bass.ds(t, 1)], None, ALU.mult).then_inc(s_eva[5], 1)
                return evac

            pass_dve(dve, "gnn0", gnn_evac("gnn0"))
            dve.wait_ge(s_eva[5], HEAD + T)
            qv = tmp[:, :, 0:128].rearrange("p t (h d) -> p t h d", d=32)
            kv = tmp[:, :, 128:256]
            q4 = qs.rearrange("p (t h) -> p t h", h=4)
            q4b = q4.unsqueeze(3).to_broadcast([P, T, 4, 32])
            v.tensor_reduce(kmx, kv.rearrange("p t c -> p c t"), AX, ALU.max).then_inc(s_v2p, 1)
            ch(v.tensor_reduce(q4, qv, AX, ALU.max))
            v.tensor_tensor(qv, qv, q4b, ALU.subtract).then_inc(s_v2a, 1)
            dve.wait_ge(s_q, 2)
            ch(v.tensor_reduce(mcol, pb[7][:, 0:P + 4], AX, ALU.max))
            v.tensor_scalar(dg, ident[:, :], mcol, None, ALU.mult).then_inc(s_v2p, 1)
            dve.wait_ge(s_q, 3)
            v.tensor_tensor(memk[:, :], memk[:, :], pb[6][0:4, 0:128], ALU.subtract)
            v.tensor_tensor(kv, kv, btm(pb[6][0:P, 0:128], T), ALU.subtract).then_inc(s_v2a, 1)
            dve.wait_ge(s_a2v, 1)
            ch(v.tensor_reduce(q4, qv, AX, ALU.add))
            ch(v.reciprocal(qs, qs))
            v.tensor_tensor(qv, qv, q4b, ALU.mult).then_inc(s_v2a, 1)
            dve.wait_ge(s_q, 4)
            ch(v.reciprocal(rden, pb[7][:, 128:129]))
            v.scalar_tensor_tensor(ctxs, pb[7][:, 0:128], rden, bmask[:, :], ALU.mult, ALU.mult).then_inc(s_v2p, 1)
            dve.wait_ge(s_q, 5)
            v.tensor_copy(ctxT, pb[6][:, 0:128]).then_inc(s_v2p, 1)
            dve.wait_ge(s_q, 6)
            v.tensor_copy(M0, pb[6][:, 0:D]).then_inc(s_v2p, 1)

            def mix0_evac(e, i, s, j):
                v.tensor_tensor(tmp[:, bass.ds(i * U + s, 1), :].rearrange("p a d -> p (a d)"), pb[0][0:P, 0:D],
                                bc[0:P, 1, :], ALU.add).then_inc(s_eva[0], 1)
            ch(v.tensor_tensor(x[:, :, :], x[:, :, :], xn[:, :, :], ALU.add))
            pass_dve(dve, "mix0", mix0_evac)
            dve.wait_ge(s_eva[0], HEAD + NEVQ("mix0"))
            dve.sem_inc(s_v2a, 1)
            dve.wait_ge(s_sq, 3)
            ch(v.tensor_reduce(va, xn[:, :, :], AX, ALU.add))
            rsq(va, 1.0, 0.0, 1e-24, D ** 0.5)
            ch(v.tensor_tensor(tmp, tmp, bt(va, D), ALU.mult))
            ch(v.tensor_tensor(tmp, tmp, btm(bc[0:P, 2, :], T), ALU.mult))
            ch(v.tensor_tensor(x[:, :, :], x[:, :, :], tmp, ALU.add))
            dve.wait_ge(s_recl, 16)
            ch.step(v.tensor_copy(gid[:, :], recs[:, :, 0]))
            ch.step(v.tensor_copy(typ[:, 0:COLS], recs[:, :, 2].bitcast(F32)))
            ch.step(v.tensor_copy(dstl[:, 0:COLS], recs[:, :, 1].bitcast(F32)))
            ch.step(v.tensor_tensor(toh, recs[:, :, 3:4].bitcast(F32).to_broadcast([128, COLS, R]),
                                    btm(iota[:, 0:R], COLS), ALU.is_equal))
            ch.wait()
            v.memset(cnt[:, :, :], 0.0).then_inc(s_srt, 1)
            gather_dve(dve, 0)
            dve.wait_ge(s_acc, HEAD + GROUPS)
            ch(v.scalar_tensor_tensor(x[:, :, :], acc, 0.5 ** 0.5, x[:, :, :], ALU.mult, ALU.add))
            ch(v.tensor_tensor(x[:, :, :], x[:, :, :], btm(bc[0:P, 0, :], T), ALU.add))
            ch(v.tensor_scalar(cnt[:, :, :], cnt[:, :, :], 1.0, None, ALU.max))
            ch(v.reciprocal(cnt[:, :, :], cnt[:, :, :]))
            ln(1)
            moe_dve(dve, ch, 0)
            ln(2)
            relation_weights(dve, ch, 0)
            pass_dve(dve, "gnn1", gnn_evac("gnn1", bias=3))
            dve.wait_ge(s_eva[4], HEAD + PASSES["gnn2"]["ev"][4])
            dve.wait_ge(s_wm, 16 * (2 * KC + 1))
            ch(v.memset(zer, 0.0))
            wv = wkv.rearrange("p k (h d) -> p k h d", d=64)
            mh = sm[:, 256:256 + 32].rearrange("p (k h) -> p k h", k=KC)
            for k in range(KC):
                ch(v.tensor_reduce(mh[:, k, :], wv[:, k], AX, ALU.add))
                ch(v.tensor_scalar(mh[:, k, :], mh[:, k, :], 1.0 / 64, None, ALU.mult))
                ch(v.tensor_tensor(wv[:, k], wv[:, k], mh[:, k, :].unsqueeze(2).to_broadcast([128, 16, 64]), ALU.subtract))
            dve.sem_inc(s_v2p, 1)
            ch(v.tensor_tensor(x[:, :, :], x[:, :, :], btm(bc[0:P, 5, :], T), ALU.add))
            dve.wait_ge(s_dot, 1)
            gather_dve(dve, 1)
            dve.wait_ge(s_acc, HEAD + 2 * GROUPS)
            dve.wait_ge(s_dot, 2)
            v.tensor_tensor(dT[:, :, :], pb[6][:, :].rearrange("p (j c) -> p j c", j=4), btm(bmask1[:, :], 4), ALU.mult)\
                .then_inc(s_v2p, 1)
            relation_weights(dve, ch, 1)
            pass_dve(dve, "gnn2", gnn_evac("gnn2", bias=4))
            dve.wait_ge(s_eva[4], HEAD + NEV[4])
            dve.wait_ge(s_q, 7 + 6)
            for j in range(2):
                ch.step(v.tensor_copy(M1[:, 2 * j:2 * j + 2, :], pb[j][:, :].rearrange("p (a d) -> p a d", d=D)))
            ch.step(v.tensor_copy(wqT[:, 0], pb[2][:, :].rearrange("p (j c) -> p j c", j=4)))
            ch.wait()
            v.tensor_copy(wqT[:, 1], pb[3][:, :].rearrange("p (j c) -> p j c", j=4)).then_inc(s_v2p, 1)
            dve.wait_ge(s_q, 7 + 8)
            v.tensor_copy(P1v, pb[4][:, :].rearrange("p (k d) -> p k d", d=D)).then_inc(s_v2p, 1)
            gather_dve(dve, 2)
            dve.wait_ge(s_acc, HEAD + 3 * GROUPS)
            ch(v.tensor_tensor(x[:, :, :], x[:, :, :], acc, ALU.add))
            ln(3)
            moe_dve(dve, ch, 1)


_INS = ['x', 'src', 'dst', 'edge_type_8', 'L0_gnn_weight', 'L0_gnn_h_bias', 'L0_gnn_loop_weight', 'L0_mix_t',
        'L0_mix_w_qkv', 'L0_mix_mem_kv', 'L0_mix_w_out', 'L0_mix_b_out', 'L0_mix_g_out', 'L0_mix_g_pre',
        'L0_ffn_Wg', 'L0_ffn_bg', 'L0_ffn_bias', 'L0_ffn_W1', 'L0_ffn_b1', 'L0_ffn_W2', 'L0_ffn_b2',
        'L1_gnn_comps', 'L1_gnn_bases', 'L1_gnn_roots', 'L1_gnn_biases', 'L1_mix_w_qkv', 'L1_mix_w_out',
        'L1_mix_b_out', 'L1_ffn_Wr', 'L1_ffn_br', 'L1_ffn_ln_g', 'L1_ffn_ln_b', 'L1_ffn_W1', 'L1_ffn_b1',
        'L1_ffn_W2', 'L1_ffn_b2']


def kernel(**inputs):
    import numpy as _np
    import concourse.bacc as _bacc
    from concourse import mybir as _mybir
    from concourse.bass_utils import run_bass_kernel_spmd as _run

    nc = _bacc.Bacc("TRN2", target_bir_lowering=False, num_devices=1)
    arrays, args = {}, []
    for name in _INS:
        a = _np.ascontiguousarray(inputs[name])
        arrays[f"in_{name}_dram"] = a
        args.append(nc.dram_tensor(f"in_{name}_dram", a.shape, _mybir.dt.from_np(a.dtype), kind="ExternalInput").ap())
    args.append(nc.dram_tensor("out_dram", (3125, 256), _mybir.dt.float32, kind="ExternalOutput").ap())
    gps_block(nc, *args)
    r = _run(nc, [arrays], core_ids=[0])
    return r.results[0]["out_dram"]
```

```python
import concourse.bass as bass
from concourse import mybir
from contextlib import ExitStack

F32 = mybir.dt.float32
I32 = mybir.dt.int32
ALU = mybir.AluOpType
ACT = mybir.ActivationFunctionType
X = mybir.AxisListType.X

NODES, D = 3125, 256
P = 125
T = NODES // P
U = 5
TI = T // U
KC = D // 128
R = 8
EDGES = 50000
EC = EDGES // P
GROUP = 256
GROUPS = (EDGES + T * (GROUP - 1)) // GROUP
GS = 4
GROUPS = -(-GROUPS // GS) * GS
GU = 8
GR = GROUPS // GU
CH = GROUP // 128
COLS = GROUPS * CH
OS = 8
OL = 7
PADC = 3 * OS * CH
NE = 8
SLOT = 256
SLOTS = (2 * NODES + NE * (SLOT - 1)) // SLOT
SLOTS += SLOTS % 2
EPS = 1e-5
SCU = 8
HEAD = 8
HEAD_DMA = 16


class Chain:

    def __init__(self, eng, sem):
        self.eng, self.sem, self.n, self.base = eng, sem, 0, 0

    def __call__(self, ins):
        self.step(ins)
        self.wait()

    def step(self, ins):
        ins.then_inc(self.sem, 1)
        self.n += 1

    def wait(self):
        self.eng.wait_ge(self.sem, self.n)

    def loop(self, i, steps):
        self.base = self.n
        self.n = self.base + i * steps

    def end(self, rounds, steps):
        self.n = self.base + rounds * steps


def gps_block(nc, x_in, src, dst, etype, w0, hb0, wl0, t0, wqkv0, memkv, wout0, bout0, gout0, gpre0,
              f0_wg, f0_bg, f0_bias, f0_w1, f0_b1, f0_w2, f0_b2, comps, bases, roots, biases,
              wqkv1, wout1, bout1, f1_wr, f1_br, f1_g, f1_b, f1_w1, f1_b1, f1_w2, f1_b2, out):
    ctx = ExitStack()
    with ctx:
        def sb(name, shape, dt=F32):
            return ctx.enter_context(nc.sbuf_tensor(name, shape, dt))

        def sem(name):
            return ctx.enter_context(nc.semaphore(name))

        def dram(name, shape, dt=F32):
            return nc.dram_tensor(name, shape, dt, kind="Internal").ap()

        hx_d = dram("hx_d", [R * NODES, D])
        rec_d = dram("rec_d", [128 * COLS, 4], I32)
        xs_d = dram("xs_d", [SLOTS * SLOT, D])
        ys_d = dram("ys_d", [SLOTS * SLOT, D])

        x = sb("x", [P, T, D])
        xn = sb("xn", [P, T, D])
        accb = sb("accb", [128, T * D])
        tmpb = sb("tmpb", [128, T * D])
        acc = accb[0:P, :].rearrange("p (t d) -> p t d", d=D)
        tmp = tmpb[0:P, :].rearrange("p (t d) -> p t d", d=D)
        wcat = sb("wcat", [128, KC, (R + 1) * D])
        hst = sb("hst", [P, 2, R, D])
        stage = sb("stage", [P, U, D])
        xT = sb("xT", [128, U, KC, P])
        G = sb("G", [128, GS, CH, D])
        wq0 = G[:, 0:KC, :, :].rearrange("p k c d -> p k (c d)")[:, :, 0:384]
        oh = sb("oh", [128, GS, CH, P])
        ohs = [oh[:, q, :, :] for q in range(GS)] + [xT[:, 1 + q, :, :] for q in range(OS - GS)]
        ohb = [0, GROUPS + GS, GROUPS + GS + OL]
        moe = sb("moe", [128, 5 * EC + T * 129])
        hT = moe[:, 0:2048].rearrange("p (j s) -> p j s", s=SLOT)
        xsr = [moe[:, 2048 + 512 * a:2560 + 512 * a].rearrange("p (a d) -> p a d", d=D) for a in range(2)]
        xsT = [moe[:, 3072 + 512 * a:3584 + 512 * a].rearrange("p (k s) -> p k s", s=SLOT) for a in range(2)]
        ysb = [moe[:, 4096 + 512 * a:4608 + 512 * a].rearrange("p (a d) -> p a d", d=D) for a in range(2)]
        ohT = moe[0:P, 4096:4608].rearrange("p (z c n) -> p z c n", z=2, n=128)
        b2c = sb("b2c", [128, 2, D])
        par = sb("par", [12, 2, 128])
        parT = sb("parT", [128, 2, 12])
        vv = moe[0:P, 5 * EC:5 * EC + T * 129].rearrange("p (t n) -> p t n", n=129)
        rec = moe[0:P, 0:4 * EC].bitcast(I32).rearrange("p (c f) -> p c f", f=4)
        posi = moe[0:P, 4 * EC:5 * EC].bitcast(I32)
        edge_col = [accb[0:P, EC * n:EC * (n + 1)] for n in range(9)]
        recs = moe[:, 0:4 * COLS].bitcast(I32).rearrange("p (c f) -> p c f", f=4)
        zeros = moe[:, 5 * EC:5 * EC + 8 * D]
        wq1 = tmpb[:, 2048:3072].rearrange("p (k n) -> p k n", k=KC)
        wo1 = tmpb[:, 3072:4096].rearrange("p (j n) -> p j n", j=4)
        unused = tmpb[:, 8 * D:8 * D + 4 * COLS].bitcast(I32).rearrange("p (c f) -> p c f", f=4)
        gid = sb("gid", [128, COLS], I32)
        typ = sb("typ", [128, COLS + PADC])
        dstl = sb("dstl", [128, COLS + PADC])
        inv = sb("inv", [128, COLS + PADC])
        toh = tmpb[:, 0:COLS * R].rearrange("p (c r) -> p c r", r=R)
        cnt = sb("cnt", [P, T, R])
        gixs = sb("gixs", [128, 2, GS, CH], I32)
        scix = sb("scix", [P, 2, SCU], I32)
        scrc = sb("scrc", [P, 2, SCU, 4], I32)
        mix = sb("mix", [P, 2, 2, U], I32)
        binr = sb("binr", [1, GROUPS + GU], I32)
        eidr = sb("eidr", [1, 2, SLOTS], I32)
        ident = sb("ident", [128, 128])
        ones = sb("ones", [128, 128])
        tri = sb("tri", [128, 128])
        iota = sb("iota", [128, GROUPS + GU])
        bmask = sb("bmask", [128, 128])
        bmask1 = sb("bmask1", [128, 128])
        ltm = sb("ltm", [P, NE, NE])
        bc = sb("bc", [128, 6, D])
        compb = sb("compb", [128, 2, 32])
        gatb = sb("gatb", [P, 4, NE])
        gpre = sb("gpre", [128, KC])
        memk = sb("memk", [4, 128])
        memv = sb("memv", [4, 129])
        wo0 = sb("wo0", [128, D])
        wg = sb("wg", [128, 2, KC, NE])
        sm = sb("sm", [128, 1160])
        stf = stage[:, :, :].rearrange("p u d -> p (u d)")
        rk = stf[:, 0:T * NE].rearrange("p (t e) -> p t e", e=NE)
        scn = stf[:, T * NE:2 * T * NE].rearrange("p (t e) -> p t e", e=NE)
        sel = stf[:, 2 * T * NE:5 * T * NE].rearrange("p (m t e) -> p m t e", e=NE, t=T)
        pw = sb("pw", [P, 2, T])
        pwi = sb("pwi", [P, 2, T], I32)
        yg = hst[:, :, :, :].rearrange("p z (a b) d -> p (z a) b d", b=2)
        big = tmpb[0:P, 0:T * NE * NE].rearrange("p (t e j) -> p t e j", e=NE, j=NE)
        big2 = tmpb[0:P, T * NE * NE:2 * T * NE * NE].rearrange("p (t e j) -> p t e j", e=NE, j=NE)
        lg = tmpb[0:P, 2 * T * NE * NE:2 * T * NE * NE + T * NE].rearrange("p (t e) -> p t e", e=NE)
        mu = sm[0:P, 0:T]
        va = sm[0:P, 32:32 + T]
        r0 = sm[0:P, 64:64 + T]
        tot = sm[0:P, 96:96 + T]
        off = sm[0:P, 128:128 + T]
        tt = sm[0:P, 160:160 + T]
        tti = sm[0:P, 192:192 + T].bitcast(I32)
        bs = sm[0:P, 224:224 + T]
        var = sm[0:P, 356:372]
        rkv = sm[0:P, 372:380]
        qs = sm[0:P, 256:356]
        kmx = sm[0:P, 384:512]
        mcol = sm[:, 512:513]
        bst = tmpb[0:P, 4096:4096 + 6 * T].rearrange("p (t n) -> p t n", n=6)
        mv = tmpb[0:P, 4096 + 6 * T:4096 + 8 * T].rearrange("p (t n) -> p t n", n=2)
        rden = sm[:, 513:514]
        dg = sm[:, 520:648]
        ctxs = sm[:, 648:776]
        ctxT = sm[:, 776:904]
        M0 = sm[:, 904:1160]

        tq = sb("tq", [128, CH, R])
        dsts = sb("dsts", [128, GU * CH])
        typs = sb("typs", [128, GU * CH])
        invs = sb("invs", [128, GU * CH])
        dT = moe[:, 3584:4096].rearrange("p (j c) -> p j c", j=4)
        zer = moe[:, 5 * EC:5 * EC + 512]
        kt = hst[:, 0, 0:2, :].rearrange("p a d -> p (a d)")
        vt = hst[:, 0, 2:4, :].rearrange("p a d -> p (a d)")
        sqv = hst[:, 1, 0:4, :].rearrange("p a d -> p (a d)")
        M1 = moe[:, 0:1024].rearrange("p (j d) -> p j d", d=D)
        wqT = moe[:, 1024:2048].rearrange("p (k j c) -> p k j c", k=KC, j=4)

        pb = [ctx.enter_context(nc.psum_tensor(f"pb{i}", [128, 512], F32)) for i in range(8)]

        s_vec = sem("s_vec")
        s_pool = sem("s_pool")
        s_xin = sem("s_xin")
        s_edge = sem("s_edge")
        s_par = sem("s_par")
        s_w0 = sem("s_w0")
        s_const = sem("s_const")
        s_zero = sem("s_zero")
        s_zr = sem("s_zr")
        s_zd = sem("s_zd")
        s_bn = sem("s_bn")
        s_sq = sem("s_sq")
        s_ln = sem("s_ln")
        s_stg = sem("s_stg")
        s_trn = sem("s_trn")
        s_xT = sem("s_xT")
        s_blk = sem("s_blk")
        s_eva = [sem(f"s_ev{j}") for j in range(6)]
        s_hst = [sem(f"s_hst{j}") for j in range(2)]
        s_pos = sem("s_pos")
        s_cst = sem("s_cst")
        s_sct = [sem(f"s_sct{j}") for j in range(2)]
        s_recl = sem("s_recl")
        s_srt = sem("s_srt")
        s_gix = sem("s_gix")
        s_G = [sem(f"s_G{j}") for j in range(GS)]
        s_oh = sem("s_oh")
        s_oT = sem("s_oT")
        s_oC = sem("s_oC")
        s_iP = sem("s_iP")
        s_iv = sem("s_iv")
        s_col = sem("s_col")
        s_sg = sem("s_sg")
        s_acc = sem("s_acc")
        s_kst = sem("s_kst")
        s_ktr = sem("s_ktr")
        s_kxT = sem("s_kxT")
        s_kmm = sem("s_kmm")
        s_kev = sem("s_kev")
        s_kss = sem("s_kss")
        s_krt = sem("s_krt")
        s_krc = sem("s_krc")
        s_kkk = sem("s_kkk")
        s_q = sem("s_q")
        s_v2p = sem("s_v2p")
        s_v2a = sem("s_v2a")
        s_a2v = sem("s_a2v")
        s_dot = sem("s_dot")
        s_w1l = sem("s_w1l")
        s_wm = sem("s_wm")
        s_cmb = sem("s_cmb")
        s_rt = sem("s_rt")
        s_dsp = sem("s_dsp")
        s_dix = sem("s_dix")
        s_dst = [sem(f"s_dst{j}") for j in range(U)]
        s_ml = [sem(f"s_ml{j}") for j in range(2)]
        s_mw1 = [sem(f"s_mw1{j}") for j in range(2)]
        s_mw2 = [sem(f"s_mw2{j}") for j in range(2)]
        s_mt = sem("s_mt")
        s_mx = sem("s_mx")
        s_mh = sem("s_mh")
        s_ma = sem("s_ma")
        s_my = [sem(f"s_my{j}") for j in range(2)]
        s_mo = [sem(f"s_mo{j}") for j in range(2)]
        s_ys = [sem(f"s_ys{j}") for j in range(2)]
        s_cix = sem("s_cix")
        s_cg = [sem(f"s_cg{j}") for j in range(U)]
        s_cmbd = sem("s_cmbd")
        s_out = sem("s_out")
        s_rsv = sem("s_rsv")
        s_rsa = sem("s_rsa")
        s_turn = sem("s_turn")
        s_turn_sp = sem("s_turn_sp")
        s_turn_dve = sem("s_turn_dve")
        s_dt = sem("s_dt")
        s_sqk = sem("s_sqk")
        s_vw = sem("s_vw")
        s_mp = sem("s_mp")
        s_cm1 = sem("s_cm1")

        def row(ap, n=128):
            return ap.partition_broadcast(n)

        hx_v = hx_d.rearrange("(r t p) d -> t p r d", r=R, p=P)
        rec_v = rec_d.rearrange("(p c) f -> p c f", p=128)
        xs_z = xs_d.rearrange("(n p a) d -> n p (a d)", n=SLOTS // 4, p=128)
        x_v = x_in.rearrange("(t p) d -> p t d", p=P)
        out_v = out.rearrange("(t p) d -> p t d", p=P)
        NEV = [0, 0, 0, 0, 0, 0]

        w_hx = [(wcat[:, :, 512 * j:512 * (j + 1)], "av"[j % 2]) for j in range(4)]
        w_loop = [(wcat[:, :, R * D:(R + 1) * D], "v")]
        wkv = tmpb[:, 4352:6400].rearrange("p (k n) -> p k n", k=KC)
        PASSES = {}

        def tile_pass(name, nk, blocks, narrow=False):
            k = len(PASSES)
            inst = dict(k=k, nk=nk, blocks=blocks, narrow=narrow, outs=TI if narrow else T, ev=[NEV[j] for j in range(len(blocks))],
                        blk=sum(len(q["blocks"]) * T for q in PASSES.values()))
            for j in range(len(blocks)):
                NEV[j] += inst["outs"]
            PASSES[name] = inst

        M0v = M0.rearrange("p (k n) -> p k n", k=1)
        P1v = moe[:, 3072:3584].rearrange("p (k d) -> p k d", d=D)
        tile_pass("gnn0", KC, w_hx + w_loop + [(wq0[:, :, :], "v")])
        tile_pass("mix0", 1, [(M0v, "v")])
        tile_pass("gate0", KC, [(wg[:, 0, :, :], "v")], narrow=True)
        tile_pass("gnn1", KC, w_hx + w_loop)
        tile_pass("gnn2", KC, w_hx + w_loop)
        tile_pass("gate1", KC, [(wg[:, 1, :, :], "v")], narrow=True)
        HSTN = {"gnn0": 0, "gnn1": 1, "gnn2": 2}

        def xT_copy(copy, name, s):
            nk = PASSES[name]["nk"]
            copy(xT[:, s, 0:nk, :], pb[6 + s % 2][:, 0:nk * P].rearrange("p (k n) -> p k n", n=P)).then_inc(s_xT, 1)

        def xT_free(eng, name, i, s):
            q = PASSES[name]
            eng.wait_ge(s_trn, HEAD + q["k"] * T + i * U + s + 1)
            eng.wait_ge(s_blk, HEAD + q["blk"] + len(q["blocks"]) * U * i)

        def pass_act(act, name, source, evac=None, func=ACT.Copy, ready=None):
            q = PASSES[name]
            k0, nk, nb = q["k"] * T, q["nk"], len(q["blocks"])
            with act.Fori(0, TI) as i:
                act.wait_ge(s_trn, HEAD + k0 + i * U)
                if ready:
                    ready(i)
                for s in range(U):
                    nc.scalar.activation(stage[:, s, 0:nk * 128], source(i * U + s), func).then_inc(s_stg, 1)
                for s in range(U):
                    t = i * U + s
                    if nb > 1:
                        xT_free(act, name, i, s)
                        xT_copy(lambda o, a: nc.scalar.activation(o, a, ACT.Copy), name, s)
                    for j, (_, e) in enumerate(q["blocks"]):
                        if e == "a":
                            act.wait_ge(s_blk, HEAD + q["blk"] + nb * t + j + 1)
                            evac(act, i, s, j)

        def pass_pe(pe, name, weights=None):
            q = PASSES[name]
            k0, nk, nb = q["k"] * T, q["nk"], len(q["blocks"])

            def transposes(i, s):
                t = i * U + s
                pe.wait_ge(s_stg, k0 + t + 1)
                if s >= 2:
                    pe.wait_ge(s_xT, HEAD + k0 + t - 1)
                else:
                    pe.wait_ge(s_xT, HEAD + k0 + i * U)
                for k in range(nk):
                    last = nc.tensor.transpose(pb[6 + s % 2][:, P * k:P * (k + 1)],
                                               stage[:, s, 128 * k:128 * (k + 1)], ident[0:P, 0:P])
                last.then_inc(s_trn, 1)

            with pe.Fori(0, TI) as i:
                transposes(i, 0)
                for s in range(U):
                    if s + 1 < U:
                        transposes(i, s + 1)
                    t = i * U + s
                    pe.wait_ge(s_xT, HEAD + k0 + t + 1)
                    for j, (w, _) in enumerate(q["blocks"]):
                        if weights is not None and s == 0 and j < 4:
                            pe.wait_ge(s_cmb, weights + j + 1)
                        if not q["narrow"]:
                            pe.wait_ge(s_eva[j], HEAD + q["ev"][j] + t)
                        elif s == 0:
                            pe.wait_ge(s_eva[j], HEAD + q["ev"][j] + i)
                        n = w.shape[2]
                        at = n * s if q["narrow"] else 0
                        for k in range(nk):
                            last = nc.tensor.matmul(pb[j][0:P, at:at + n], xT[:, s, k, :], w[:, k, :],
                                                    start=(k == 0), stop=(k == nk - 1))
                        last.then_inc(s_blk, 1)

        def pass_dve(dve, name, evac, ahead=None):
            q = PASSES[name]
            nb = len(q["blocks"])

            def blocks(i, s):
                for j, (_, e) in enumerate(q["blocks"]):
                    if e == "v":
                        dve.wait_ge(s_blk, HEAD + q["blk"] + nb * (i * U + s) + j + 1)
                        evac(dve, i, s, j)

            def round_(i):
                for s in range(U):
                    if nb > 1:
                        blocks(i, s)
                        continue
                    xT_free(dve, name, i, s)
                    xT_copy(nc.vector.tensor_copy, name, s)
                    if s and not q["narrow"]:
                        blocks(i, s - 1)
                if nb == 1:
                    blocks(i, U - 1)

            with dve.Fori(0, TI - 1 if ahead else TI) as i:
                if ahead:
                    ahead(i + 1)
                round_(i)
            if ahead:
                round_(TI - 1)

        def hx_free(eng, name, i, s):
            n = HSTN[name]
            per = (3, 2)[s % 2]
            eng.wait_ge(s_hst[s % 2], HEAD_DMA + 16 * (n * per * TI + per * i + s // 2))

        def hx_copy(eng, name, copy):
            def evac(e, i, s, j):
                hx_free(e, name, i, s)
                copy(hst[:, s % 2, 2 * j:2 * j + 2, :], pb[j][0:P, :].rearrange("p (a d) -> p a d", d=D))\
                    .then_inc(s_eva[j], 1)
            return evac

        def hx_store(sp, name):
            q = PASSES[name]
            with sp.Fori(0, TI) as i:
                for s in range(U):
                    for j in range(4):
                        sp.wait_ge(s_eva[j], HEAD + q["ev"][j] + i * U + s + 1)
                        sp.sem_inc(s_turn_sp, 1)
                    sp.dma_start(hx_v[bass.ds(i * U + s, 1), :, :, :].rearrange("a p r d -> (a p) r d"),
                                 hst[:, s % 2, :, :]).then_inc(s_hst[s % 2], 16)

        def hx_done(eng, name):
            n = HSTN[name] + 1
            for z, per in enumerate((3, 2)):
                eng.wait_ge(s_hst[z], HEAD_DMA + 16 * n * per * TI)

        H = [f0_w1.shape[2], f1_w1.shape[2]]
        MW = [(f0_w1, f0_b1, f0_w2, f0_b2, None, None), (f1_w1, f1_b1, f1_w2, f1_b2, f1_g, f1_b)]
        wreg = [tmpb, accb]
        NLOAD = [2, 4]

        gnnb = [accb[:, 4096:6144], tmpb[:, 0:2048]]

        def gnn_weights_sp(sp, n):
            for k in range(KC):
                sp.dma_start(gnnb[n][:, 1024 * k:1024 * (k + 1)].rearrange("p (b n) -> p b n", b=4),
                             bases[n].rearrange("b (k p) n -> k p b n", p=128)[k]).then_inc(s_w1l, 16)
                sp.dma_start(wcat[:, k, R * D:], roots[n].rearrange("(k p) n -> k p n", p=128)[k]).then_inc(s_w1l, 16)

        def mw1(n, z):
            return wreg[z][:, 0:2 * H[n]].rearrange("p (k h) -> p k h", k=KC)

        def mw2(n, z):
            return wreg[z][:, 2048:2048 + 2 * H[n]].rearrange("p (j d) -> p j d", d=D)

        def moe_sp(sp, n):
            w1, b1, w2, b2, g, b = MW[n]
            HC = H[n] // 128
            sp.wait_ge(s_rt, 2 * n + 2)

            def store(i, z):
                sp.wait_ge(s_mo[z], HEAD + n * SLOTS // 2 + i + 1)
                sp.dma_start(ys_d.rearrange("(m a p) d -> m p a d", p=128, a=2)[bass.ds(2 * i + z, 1)]
                             .rearrange("m p a d -> (m p) a d"), ysb[z]).then_inc(s_ys[z], 16)

            def load_rows(i, z):
                sp.dma_start(xsr[z], xs_d.rearrange("(m a p) d -> m p a d", p=128, a=2)[bass.ds(2 * i + z, 1)]
                             .rearrange("m p a d -> (m p) a d")).then_inc(s_ml[z], 16)

            def load_first(i, z, rows=True):
                e = sp.value_load(eidr[0:1, n, bass.ds(2 * i + z, 1)], min_val=0, max_val=NE - 1)
                sp.dma_start(mw1(n, z), w1[bass.ds(e, 1)].rearrange("a (k p) h -> (a p) k h", p=128)).then_inc(s_mw1[z], 16)
                if rows:
                    load_rows(i, z)
                sp.dma_start(par[0:HC, z, :], b1[bass.ds(e, 1)].rearrange("a (j p) -> (a j) p", p=128)).then_inc(s_ml[z], 16)
                if g is not None:
                    for m, v in enumerate((g, b)):
                        sp.dma_start(par[HC + 2 * m:HC + 2 * m + 2, z, :],
                                     v[bass.ds(e, 1)].rearrange("a (j p) -> (a j) p", p=128)).then_inc(s_ml[z], 16)

            def load_second(i, z):
                e = sp.value_load(eidr[0:1, n, bass.ds(2 * i + z, 1)], min_val=0, max_val=NE - 1)
                sp.dma_start(mw2(n, z), w2[bass.ds(e, 1)].rearrange("a (j p) d -> (a p) j d", p=128)).then_inc(s_mw2[z], 16)
                sp.dma_start(b2c[:, z, :], b2[bass.ds(e, 1)].rearrange("a d -> (a d)").partition_broadcast(128))\
                    .then_inc(s_mw2[z], 16)

            for z in range(2):
                load_first(0, z, rows=False)
                load_second(0, z)
            for s in range(U):
                sp.wait_ge(s_dst[s], 32 * TI * (n + 1))
            for z in range(2):
                load_rows(0, z)
            with sp.Fori(0, SLOTS // 2 - 1) as i:
                for z in range(2):
                    sp.wait_ge(s_mh, HEAD + (0, SLOTS * (H[0] // 128))[n] + HC * (2 * i + z + 1))
                    load_first(i + 1, z)
                    store(i, z)
                    load_second(i + 1, z)
            for z in range(2):
                store(SLOTS // 2 - 1, z)

        def bins(engine, first):
            return nc.values_load_multi_w_load_instructions(binr[0:1, bass.ds(first, GU)], [engine],
                                                            min_val=0, max_val=T - 1,
                                                            skip_runtime_bounds_check_because="a count of the T - 1 "
                                                            "tiles after the first")[1]

        def groups(eng, body, first=0):
            with eng.Fori(first, GR) as i:
                for u in range(GU):
                    body(i, u)
            for u in range(GROUPS % GU):
                body(GR, u)

        def groups_beside(eng, n, body, beside):
            for u in range(GU):
                body(0, u)
                beside(0, u, True, False)
            with eng.Fori(1, T) as i:
                for u in range(GU):
                    body(i, u)
                    beside(i, u, True, n == 1)
            if n == 1:
                for u in range(GU):
                    beside(T, u, False, True)
            groups(eng, body, T)

        def gather_pool(pool, n):
            g = nc.gpsimd

            def rows(i, u):
                q, half = u % GS, u // GS
                at = n * GROUPS + i * GU + u
                if q == 0:
                    pool.wait_ge(s_sg, HEAD + at - GS)
                    g.tensor_copy(gixs[:, half, :, :], gid[:, bass.ds((i * GU + u) * CH, GS * CH)]
                                  .rearrange("p (a b) -> p a b", b=CH)).then_inc(s_gix, 1)
                    pool.wait_ge(s_gix, n * (GROUPS // GS) + i * 2 + half + 1)
                pool.wait_ge(s_sg, HEAD + at - GS + 1)
                pool.sem_inc(s_turn, 1)
                for c in range(CH):
                    g.indirect_dma_start(G[:, q, c, :], None, hx_d,
                                         bass.IndirectOffsetOnAxis(gixs[:, half, q, c:c + 1], axis=0)).then_inc(s_G[q], 16)
            groups(pool, rows)

        def rounds(eng, body):
            body(0, 0, True)
            with eng.Fori(0, (TI - 1) // 2) as i:
                body(2 * i + 1, 1, False)
                body(2 * i + 2, 0, False)

        def dispatch_pool(pool, n):
            g = nc.gpsimd
            pool.wait_ge(s_rt, 2 * n + 1)

            def body(i, z, first):
                for m in range(2):
                    g.tensor_copy(mix[:, z, m, :], pwi[:, m, bass.ds(i * U, U)]).then_inc(s_dix, 1)
                pool.wait_ge(s_dix, 2 * (n * TI + i) + 2)
                for s in range(U):
                    pool.wait_ge(s_dsp, n * T + i * U + s + 1)
                    if not first:
                        pool.sem_inc(s_turn, 1)
                        pool.wait_ge(s_dst[s], 32 * (n * TI + i))
                        pool.sem_inc(s_turn, 1)
                    for m in range(2):
                        g.indirect_dma_start(xs_d, bass.IndirectOffsetOnAxis(mix[:, z, m, s:s + 1], axis=0),
                                             stage[:, s, :], None).then_inc(s_dst[s], 16)
            rounds(pool, body)

        def combine_pool(pool, n):
            g = nc.gpsimd
            for z in range(2):
                pool.wait_ge(s_ys[z], HEAD_DMA + 16 * SLOTS // 2 * (n + 1))

            def body(i, z, first):
                for m in range(2):
                    g.tensor_copy(mix[:, z, m, :], pwi[:, m, bass.ds(i * U, U)]).then_inc(s_cix, 1)
                pool.wait_ge(s_cix, 2 * (n * TI + i) + 2)
                for s in range(U):
                    if not first:
                        pool.wait_ge(s_cmbd, HEAD + n * T + (i - 1) * U + s + 1)
                        pool.sem_inc(s_turn, 1)
                    for m in range(2):
                        g.indirect_dma_start(yg[:, s, m, :], None, ys_d,
                                             bass.IndirectOffsetOnAxis(mix[:, z, m, s:s + 1], axis=0))\
                            .then_inc(s_cg[s], 16)
            rounds(pool, body)

        def prefix_pe(pe, n, operand):
            pe.wait_ge(s_v2p, operand)
            nc.tensor.matmul(pb[7][0:P, 0:n], tri[0:P, 0:P], tot[:, 0:n], start=True, stop=True)
            nc.tensor.matmul(pb[6][0:P, 0:n], ones[0:P, 0:P], tot[:, 0:n], start=True, stop=True).then_inc(s_q, 1)

        def gather_pe(pe, n):
            banks = 4 if n == 0 else 2

            def invert_t(g, q):
                if not isinstance(g, int) or g > 0:
                    pe.wait_ge(s_oC, g)
                for c in range(CH):
                    last = nc.tensor.transpose(pb[2][0:P, 128 * c:128 * (c + 1)], ohs[q][:, c, :], ident[:, :])
                last.then_inc(s_oT, 1)

            tiles = []

            def invert_m(g, z, b, first=False):
                if not first:
                    pe.wait_ge(s_iv, g)
                for c in range(CH):
                    last = nc.tensor.matmul(pb[3][:, R * c:R * (c + 1)], ohT[:, z, c, :],
                                            cnt[:, bass.ds(b, 1), :].rearrange("p a r -> p (a r)"), start=True, stop=True)
                last.then_inc(s_iP, 1)

            def sums(i, u):
                g = i * GU + u
                at = n * GROUPS + g
                q = u % GS
                if n == 1:
                    if u == 0:
                        tiles[:] = bins(mybir.EngineType.PE, g + 3)
                    invert_m(g + 3, (u + 3) % 2, tiles[u])
                else:
                    pe.wait_ge(s_oh, ohb[n] + g + 1)
                pe.wait_ge(s_G[q], 16 * CH * (n * (GROUPS // GS) + i * 2 + u // GS + 1))
                pe.wait_ge(s_acc, HEAD + at - banks + 1)
                for c in range(CH):
                    last = nc.tensor.matmul(pb[u % banks][0:P, 0:D], ohs[u if n == 1 else q][:, c, :], G[:, q, c, :],
                                            start=(c == 0), stop=(c == CH - 1))
                if n == 0:
                    for c in range(CH):
                        last = nc.tensor.matmul(pb[4 + u % banks][0:P, 0:R], oh[:, q, c, :],
                                                toh[:, bass.ds(g * CH + c, 1), :].rearrange("p a r -> p (a r)"),
                                                start=(c == 0), stop=(c == CH - 1))
                last.then_inc(s_sg, 1)
                if n == 1:
                    invert_t(g + 5, (u + 5) % OS)

            if n == 1:
                tiles[:] = bins(mybir.EngineType.PE, 0)
                pe.wait_ge(s_oh, ohb[1] + OL)
                invert_t(0, 0)
                invert_t(1, 1)
                for q in range(3):
                    invert_m(q, q % 2, tiles[q], q == 0)
                    invert_t(q + 2, q + 2)
            if n == 0:
                groups(pe, sums)
                return

            def beside(i, u, now, late):
                k = (n - 1) * T + i
                if now and u == 1:
                    pe.wait_ge(s_kst, k + 1)
                    for c in range(KC):
                        last = nc.tensor.transpose(pb[7][:, P * c:P * (c + 1)], stage[:, 0, 128 * c:128 * (c + 1)],
                                                   ident[0:P, 0:P])
                    last.then_inc(s_ktr, 1)
                if late and u in (3, 4):
                    pe.wait_ge(s_kkk, HEAD + i)
                    pe.wait_ge(s_kev, HEAD + i)
                    for h in (2 * (u - 3), 2 * (u - 3) + 1):
                        last = nc.tensor.matmul(pb[6][:, 128 * h:128 * (h + 1)], vt[:, 128 * h:128 * (h + 1)],
                                                kt[:, 128 * h:128 * (h + 1)], start=False, stop=False,
                                                skip_group_check=True)
                    if u == 4:
                        last.then_inc(s_dt, 1)
                if now and n == 1 and u in (3, 4, 5, 6):
                    if u == 3:
                        pe.wait_ge(s_kxT, k + 1)
                    pe.wait_ge((s_kkk, s_kev)[(u - 3) // 2], HEAD + i)
                    c, kv = (u - 3) % 2, (u - 3) // 2
                    last = nc.tensor.matmul(pb[4 + kv][0:P, :], xT[:, 0, c, :], wkv[:, c, 512 * kv:512 * (kv + 1)],
                                            start=(c == 0), stop=(c == KC - 1))
                    if c == KC - 1:
                        last.then_inc(s_kmm, 1)
                if now and n == 2 and u == 3:
                    pe.wait_ge(s_kxT, k + 1)
                    pe.wait_ge(s_kev, HEAD + k)
                    for c in range(KC):
                        last = nc.tensor.matmul(pb[3][0:P, 0:D], xT[:, 0, c, :], P1v[:, c, :],
                                                start=(c == 0), stop=(c == KC - 1))
                    last.then_inc(s_kmm, 1)

            groups_beside(pe, n, sums, beside)

        def moe_pe(pe, n):
            HC = H[n] // 128
            NL = 16 * NLOAD[n]
            b0 = (0, 16 * NLOAD[0] * (SLOTS // 2))[n]
            hb = (0, SLOTS * (H[0] // 128))[n]
            np_ = HC + (4 if n else 0)

            def transposes(i, z):
                pe.wait_ge(s_ml[z], b0 + NL * (i + 1))
                pe.wait_ge(s_mx, HEAD + n * SLOTS + 2 * i + z)
                for k in range(KC):
                    for a in range(2):
                        nc.tensor.transpose(pb[7][:, 256 * k + 128 * a:256 * k + 128 * (a + 1)],
                                            xsr[z][:, a, 128 * k:128 * (k + 1)], ident[:, :])
                nc.tensor.transpose(pb[6][:, 0:np_], par[0:np_, z, :], ident[0:np_, 0:np_]).then_inc(s_mt, 1)

            def tile(i, z, ahead):
                pe.wait_ge(s_mx, HEAD + n * SLOTS + 2 * i + z + 1)
                pe.wait_ge(s_mw1[z], 16 * (n * SLOTS // 2 + i + 1))
                for j in range(HC):
                    h0 = hb + HC * (2 * i + z) + j
                    pe.wait_ge(s_ma, HEAD + (h0 - 3 if j >= 4 else h0 - j))
                    for k in range(KC):
                        last = nc.tensor.matmul(pb[j % 4][:, 0:SLOT], mw1(n, z)[:, k, 128 * j:128 * (j + 1)],
                                                xsT[z][:, k, :], start=(k == 0), stop=(k == KC - 1))
                    last.then_inc(s_mh, 1)
                if ahead:
                    transposes(*ahead)
                pe.wait_ge(s_mo[z], HEAD + n * SLOTS // 2 + i)
                pe.wait_ge(s_mw2[z], 32 * (n * SLOTS // 2 + i + 1))
                for a in range(2):
                    for j in range(HC):
                        if a == 0:
                            pe.wait_ge(s_ma, HEAD + hb + HC * (2 * i + z) + j + 1)
                        last = nc.tensor.matmul(pb[4 + z][:, D * a:D * (a + 1)],
                                                hT[:, j, 128 * a:128 * (a + 1)], mw2(n, z)[:, j, :],
                                                start=(j == 0), stop=(j == HC - 1))
                last.then_inc(s_my[z], 1)

            transposes(0, 0)
            with pe.Fori(0, SLOTS // 2 - 1) as i:
                tile(i, 0, (i, 1))
                tile(i, 1, (i + 1, 0))
            tile(SLOTS // 2 - 1, 0, (SLOTS // 2 - 1, 1))
            tile(SLOTS // 2 - 1, 1, None)

        def moe_act(act, n):
            HC = H[n] // 128
            hb = (0, SLOTS * (H[0] // 128))[n]
            ac = nc.scalar
            act.wait_ge(s_v2a, (5, 6)[n])
            ac.activation(pw[:, 1, :], pw[:, 1, :], ACT.Exp).then_inc(s_a2v, 1)
            act.wait_ge(s_rt, 2 * n + 1)

            def body(i, z, first):
                for s in range(U):
                    if not first:
                        act.wait_ge(s_dst[s], 32 * (n * TI + i))
                    ac.activation(stage[:, s, :], xn[:, bass.ds(i * U + s, 1), :].rearrange("p a d -> p (a d)"),
                                  ACT.Copy).then_inc(s_dsp, 1)
            rounds(act, body)
            with act.Fori(0, SLOTS // 2) as i:
                for z in range(2):
                    for j in range(HC):
                        h0 = hb + HC * (2 * i + z) + j
                        act.wait_ge(s_mh, HEAD + h0 + 1)
                        act.wait_ge(s_my[1 - z], HEAD + n * SLOTS // 2 + i + z)
                        ac.activation(hT[:, j, :], pb[j % 4][:, 0:SLOT], (ACT.Relu, ACT.Gelu)[n],
                                      bias=parT[:, z, j:j + 1]).then_inc(s_ma, 1)

        def NEVQ(name, j=0):
            return PASSES[name]["ev"][j] + PASSES[name]["outs"]

        def relation_weights(dve, ch, n):
            v = nc.vector
            dve.wait_ge(s_w1l, 32 * KC * (n + 1))
            for r in range(R):
                for b in range(4):
                    c = compb[:, n, 4 * r + b:4 * r + b + 1]
                    o = wcat[:, :, D * r:D * (r + 1)]
                    i = gnnb[n].rearrange("p (k b n) -> p k b n", k=KC, b=4)[:, :, b, :]
                    if b == 0:
                        ch(v.tensor_scalar(o, i, c, None, ALU.mult))
                    else:
                        ch(v.scalar_tensor_tensor(o, i, c, o, ALU.mult, ALU.add))
                if r % 2:
                    dve.sem_inc(s_cmb, 1)

        def prefix(dve, ch, n, size, shift, q):
            v = nc.vector
            dve.sem_inc(s_v2p, 1)
            dve.wait_ge(s_q, q)
            ch(v.tensor_scalar(tti[:, 0:n], pb[6][0:P, 0:n], float(size - 1), None, ALU.add))
            ch(v.tensor_scalar(tti[:, 0:n], tti[:, 0:n], shift, None, ALU.arith_shift_right))
            ch(v.tensor_copy(tt[:, 0:n], tti[:, 0:n]))
            ch(v.tensor_tensor_scan(bs[:, 0:n], ones[0:P, 0:n], tt[:, 0:n], 0.0, ALU.mult, ALU.add))
            ch(v.tensor_tensor(bs[:, 0:n], bs[:, 0:n], tt[:, 0:n], ALU.subtract))
            ch(v.scalar_tensor_tensor(off[:, 0:n], bs[:, 0:n], float(size), pb[7][0:P, 0:n], ALU.mult, ALU.add))

        def gather_dve(dve, n):
            v = nc.vector
            banks = 4 if n == 0 else 2

            def onehots(g, q, sem_=None):
                for c in range(CH):
                    if n == 1:
                        last = v.tensor_scalar(ohs[q][:, c, :], iota[:, 0:P], dsts[:, q * CH + c:q * CH + c + 1], None,
                                               ALU.is_equal)
                        continue
                    col = g * CH + c
                    if n == 2:
                        last = v.tensor_scalar(oh[:, q, c, :], iota[:, 0:P], dstl[:, bass.ds(col, 1)],
                                               inv[:, bass.ds(col, 1)], ALU.is_equal, ALU.mult)
                    else:
                        last = v.tensor_scalar(oh[:, q, c, :], iota[:, 0:P], dstl[:, bass.ds(col, 1)], None, ALU.is_equal)
                last.then_inc(sem_ or s_oh, 1)

            def stage_round(to, array, i, count):
                v.tensor_copy(to[:, :], array[:, bass.ds(i * GU * CH, GU * CH)]).then_inc(s_col, 1)
                dve.wait_ge(s_col, count)

            def invert(g, q):
                dve.wait_ge(s_iP, HEAD + g + 1)
                for c in range(CH):
                    k = q * CH + c
                    last = v.scalar_tensor_tensor(tq[:, c, :], iota[:, 0:R], typs[:, k:k + 1], pb[3][:, R * c:R * (c + 1)],
                                                  ALU.is_equal, ALU.mult, accum_out=invs[:, k:k + 1])
                last.then_inc(s_iv, 1)

            def keep(i):
                v.tensor_copy(inv[:, bass.ds(i * GU * CH, GU * CH)], invs[:, :])

            tiles = []

            def add(i, u):
                g = i * GU + u
                if n == 1:
                    if u == 5:
                        stage_round(typs, typ, i + 1, 2 + 2 * i + 2)
                    invert(g + 3, (u + 3) % GU)
                    if u == 4:
                        dve.wait_ge(s_iv, g + 4)
                        keep(i)
                if u == 0:
                    tiles[:] = bins(mybir.EngineType.DVE, g)
                b = tiles[u]
                dve.wait_ge(s_acc, HEAD + n * GROUPS + g)
                dve.wait_ge(s_sg, HEAD + n * GROUPS + g + 1)
                at = acc[:, bass.ds(b, 1), :].rearrange("p a d -> p (a d)")
                if n == 0:
                    ct = cnt[:, bass.ds(b, 1), :].rearrange("p a d -> p (a d)")
                    v.tensor_tensor(ct, ct, pb[4 + u % banks][0:P, 0:R], ALU.add)
                last = v.tensor_tensor(at, at, pb[u % banks][0:P, 0:D], ALU.add)
                if n == 1:
                    if u == GU - OL:
                        stage_round(dsts, dstl, i + 1, 2 + 2 * i + 1)
                    onehots(g + OL, (u + OL) % OS, s_acc)
                else:
                    last.then_inc(s_acc, 1)
                    onehots(g + GS, u % GS)

            if n == 1:
                stage_round(dsts, dstl, 0, 1)
                stage_round(typs, typ, 0, 2)
            for q in range(OL if n == 1 else GS):
                onehots(q, q)
            if n == 1:
                for q in range(3):
                    invert(q, q)
            if n == 0:
                groups(dve, add)
                return

            def beside(i, u, now, late):
                k = (n - 1) * T + i
                if now and n == 2 and u == 4:
                    dve.wait_ge(s_kmm, HEAD + 2 * T + i + 1)
                    xt = x[:, bass.ds(i, 1), :].rearrange("p a d -> p (a d)")
                    v.tensor_tensor(xt, pb[3][0:P, 0:D], xt, ALU.add).then_inc(s_kev, 1)
                if late and u == 0:
                    dve.wait_ge(s_sqk, 2 * i)
                    v.tensor_reduce(var[:, 8:16], sqv[:, 512:1024].rearrange("p (h d) -> p h d", d=64), X, ALU.add)\
                        .then_inc(s_kss, 1)
                    dve.wait_ge(s_kss, HEAD + 3 * i - 1)
                    v.tensor_scalar(var, var, 1.0 / 64, EPS, ALU.mult, ALU.add).then_inc(s_kss, 1)
                if late and u == 1:
                    dve.wait_ge(s_krt, i)
                    v.reciprocal(var, var).then_inc(s_krc, 1)
                    dve.wait_ge(s_krc, 2 * i - 1)
                    v.tensor_tensor(rkv, var[:, 0:8], var[:, 8:16], ALU.mult).then_inc(s_krc, 1)
                    dve.wait_ge(s_krc, 2 * i)
                    dve.wait_ge(s_dt, HEAD + i - 1)
                    v.tensor_tensor(kt.rearrange("p (h d) -> p h d", d=64),
                                    pb[4][0:P, :].rearrange("p (h d) -> p h d", d=64),
                                    rkv.unsqueeze(2).to_broadcast([P, 8, 64]), ALU.mult).then_inc(s_kkk, 1)
                if now and n == 1 and u == 6:
                    dve.wait_ge(s_sqk, 2 * i + 1)
                    v.tensor_reduce(var[:, 0:8], sqv[:, 0:512].rearrange("p (h d) -> p h d", d=64), X, ALU.add)\
                        .then_inc(s_kss, 1)

            groups_beside(dve, n, add, beside)
            if n == 1 and GROUPS % GU:
                dve.wait_ge(s_iv, GROUPS + 3)
                keep(GR)

        def gather_act(act, n):
            ac = nc.scalar

            def ahead(g, u):
                act.wait_ge(s_oT, g + 6)
                last = ac.activation(ohT[:, (u + 1) % 2, :, :], pb[2][0:P, 0:CH * 128].rearrange("p (c e) -> p c e", e=128),
                                     ACT.Copy)
                if not isinstance(g, int) or -2 <= g < GROUPS - 2:
                    q = (u + 2) % OS
                    for c in range(CH):
                        last = ac.activation(ohs[q][:, c, :], ohs[q][:, c, :], ACT.Copy,
                                             scale=invs[:, q * CH + c:q * CH + c + 1])
                last.then_inc(s_oC, 1)

            def beside(i, u, now, late):
                k = (n - 1) * T + i
                if late and u == 0:
                    act.wait_ge(s_kmm, HEAD + 2 * i)
                    act.wait_ge(s_dt, HEAD + i - 1)
                    ac.activation(vt, pb[5][0:P, :], ACT.Copy).then_inc(s_kev, 1)
                if now and u == 0:
                    act.wait_ge(s_ktr, HEAD + k)
                    ac.activation(stage[:, 0, :], xn[:, bass.ds(i, 1), :].rearrange("p a d -> p (a d)"), ACT.Copy)\
                        .then_inc(s_kst, 1)
                if late and u == 1:
                    act.wait_ge(s_kss, HEAD + 3 * i)
                    ac.activation(var, var, ACT.Sqrt).then_inc(s_krt, 1)
                if now and u == 2:
                    act.wait_ge(s_ktr, HEAD + k + 1)
                    act.wait_ge(s_kmm, HEAD + (2 * i if n == 1 else 2 * T + i))
                    ac.activation(xT[:, 0, :, :], pb[7][:, 0:KC * P].rearrange("p (k n) -> p k n", n=P), ACT.Copy)\
                        .then_inc(s_kxT, 1)
                if now and n == 1 and u in (5, 7):
                    kv = (u - 5) // 2
                    act.wait_ge(s_kmm, HEAD + 2 * i + kv + 1)
                    act.wait_ge(s_kss, HEAD + 3 * i)
                    ac.activation(sqv[:, 512 * kv:512 * (kv + 1)], pb[4 + kv][0:P, :], ACT.Square).then_inc(s_sqk, 1)

            if n == 1:
                for g in range(-5, 0):
                    ahead(g, g)
                groups_beside(act, n, lambda i, u: ahead(i * GU + u, u), beside)
            else:
                with act.Fori(0, T) as i:
                    for u in range(GU):
                        beside(i, u, True, False)

        def normalise(dve, n):
            def body(i):
                for s in range(U):
                    t = i * U + s
                    nc.vector.tensor_scalar(xn[:, bass.ds(t, 1), :].rearrange("p a d -> p (a d)"),
                                            x[:, bass.ds(t, 1), :].rearrange("p a d -> p (a d)"),
                                            mv[:, bass.ds(t, 1), 0:1].rearrange("p a c -> p (a c)"), va[:, bass.ds(t, 1)],
                                            ALU.subtract, ALU.mult).then_inc(s_ln, 1)
            return body

        def statistics(dve, i):
            for s in range(U):
                t = i * U + s
                last = nc.vector.bn_stats(bst[:, bass.ds(t, 1), :].rearrange("p a n -> p (a n)"),
                                          x[:, bass.ds(t, 1), :].rearrange("p a d -> p (a d)"))
            last.then_inc(s_bn, 1)

        def moe_dve(dve, ch, n):
            v = nc.vector
            name = ("gate0", "gate1")[n]
            HC = H[n] // 128

            gb = gatb[:, 3, :]
            if n == 0:
                ch(v.tensor_tensor(gb, gatb[:, 0, :], gatb[:, 1, :], ALU.add))
            else:
                ch(v.tensor_copy(gb, gatb[:, 2, :]))

            def evac(e, i, s, j):
                v.tensor_tensor(lg[:, bass.ds(i * U, U), :], pb[0][0:P, 0:U * NE].rearrange("p (s e) -> p s e", e=NE),
                                gb.unsqueeze(1).to_broadcast([P, U, NE]), ALU.add).then_inc(s_eva[0], 1)
            pass_dve(dve, name, evac, normalise(dve, n * 2 + 1))
            dve.wait_ge(s_eva[0], HEAD + NEVQ(name))
            lj = lg[:, :, :].unsqueeze(2).to_broadcast([P, T, NE, NE])
            le = lg[:, :, :].unsqueeze(3).to_broadcast([P, T, NE, NE])
            ch.step(v.tensor_tensor(big, lj, le, ALU.is_gt))
            ch(v.tensor_tensor(big2, lj, le, ALU.is_equal))
            ch(v.tensor_tensor(big2, big2, ltm[:, :, :].unsqueeze(1).to_broadcast([P, T, NE, NE]), ALU.mult))
            ch(v.tensor_tensor(big, big, big2, ALU.add))
            ch(v.tensor_reduce(rk[:, :, :], big, X, ALU.add))
            for m in range(2):
                ch(v.tensor_scalar(sel[:, m], rk[:, :, :], float(m), None, ALU.is_equal))
            ch(v.tensor_tensor(sel[:, 2], sel[:, 0], sel[:, 1], ALU.add))
            for m in range(2):
                ch(v.tensor_tensor(rk[:, :, :], sel[:, m], lg[:, :, :], ALU.mult))
                ch(v.tensor_reduce(pw[:, m, :], rk[:, :, :], X, ALU.add))
            v.tensor_tensor(pw[:, 1, :], pw[:, 1, :], pw[:, 0, :], ALU.subtract).then_inc(s_v2a, 1)
            dve.wait_ge(s_a2v, 3 + n)
            ch(v.tensor_scalar(pw[:, 0, :], pw[:, 1, :], 1.0, None, ALU.add))
            ch(v.reciprocal(pw[:, 0, :], pw[:, 0, :]))
            ch(v.tensor_tensor(pw[:, 1, :], pw[:, 1, :], pw[:, 0, :], ALU.mult))
            for e in range(NE):
                ch(v.tensor_tensor_scan(scn[:, :, e], ones[0:P, 0:T], sel[:, 2, :, e], 0.0, ALU.mult, ALU.add))
            ch(v.tensor_copy(tot[:, 0:NE], scn[:, T - 1, :]))
            prefix(dve, ch, NE, SLOT, 8, (7, 16)[n])
            ch(v.tensor_tensor(scn[:, :, :], scn[:, :, :], off[:, 0:NE].unsqueeze(1).to_broadcast([P, T, NE]), ALU.add))
            ch(v.tensor_scalar(scn[:, :, :], scn[:, :, :], -1.0, None, ALU.add))
            for m in range(2):
                ch(v.tensor_tensor(rk[:, :, :], sel[:, m], scn[:, :, :], ALU.mult))
                ch(v.tensor_reduce(mu, rk[:, :, :], X, ALU.add))
                ch(v.tensor_copy(pwi[:, m, :], mu))
            dve.sem_inc(s_rt, 1)
            sl, s2 = tmpb[0:1, 0:SLOTS], tmpb[0:1, SLOTS:2 * SLOTS]
            ch(v.memset(sl, 0.0))
            for e in range(1, NE):
                ch(v.tensor_scalar(s2, iota[0:1, 0:SLOTS], bs[0:1, e:e + 1], None, ALU.is_ge))
                ch(v.tensor_tensor(sl, sl, s2, ALU.add))
            ch(v.tensor_copy(eidr[:, n, :], sl))
            dve.sem_inc(s_rt, 1)
            if n == 0:
                relation_weights(dve, ch, 0)
                dve.wait_ge(s_wm, 16 * KC)
                wv = wkv.rearrange("p k (h d) -> p k h d", d=64)
                mh = sm[:, 256:256 + 32].rearrange("p (k h) -> p k h", k=KC)
                for k in range(KC):
                    ch(v.tensor_reduce(mh[:, k, :], wv[:, k], X, ALU.add))
                    ch(v.tensor_scalar(mh[:, k, :], mh[:, k, :], 1.0 / 64, None, ALU.mult))
                    ch(v.tensor_tensor(wv[:, k], wv[:, k], mh[:, k, :].unsqueeze(2).to_broadcast([128, 16, 64]),
                                       ALU.subtract))

            def operands(i, z):
                t = n * SLOTS + 2 * i + z
                dve.wait_ge(s_mt, t + 1)
                np_ = HC + (4 if n else 0)
                v.tensor_copy(parT[:, z, 0:np_], pb[6][:, 0:np_]).then_inc(s_mp, 1)
                dve.wait_ge(s_mp, t + 1)
                for k in range(KC):
                    tp = pb[7][:, SLOT * k:SLOT * (k + 1)]
                    if n:
                        last = v.tensor_scalar(xsT[z][:, k, :], tp, parT[:, z, HC + k:HC + k + 1],
                                               parT[:, z, HC + 2 + k:HC + 3 + k], ALU.mult, ALU.add)
                    else:
                        last = v.tensor_copy(xsT[z][:, k, :], tp)
                last.then_inc(s_mx, 1)

            def outputs(i, z):
                dve.wait_ge(s_my[z], HEAD + n * SLOTS // 2 + i + 1)
                dve.wait_ge(s_ys[z], HEAD_DMA + 16 * (n * SLOTS // 2 + i))
                v.tensor_tensor(ysb[z], pb[4 + z][:, :].rearrange("p (a d) -> p a d", d=D),
                                b2c[:, z, :].unsqueeze(1).to_broadcast([128, 2, D]), ALU.add).then_inc(s_mo[z], 1)

            operands(0, 0)
            with dve.Fori(0, SLOTS // 2 - 1) as i:
                operands(i, 1)
                outputs(i, 0)
                operands(i + 1, 0)
                outputs(i, 1)
            operands(SLOTS // 2 - 1, 1)
            for z in range(2):
                outputs(SLOTS // 2 - 1, z)
            with dve.Fori(0, TI) as i:
                for s in range(U):
                    t = i * U + s
                    dve.wait_ge(s_cg[s], 32 * (n * TI + i + 1))
                    xt = x[:, bass.ds(t, 1), :].rearrange("p a d -> p (a d)")
                    v.scalar_tensor_tensor(xt, yg[:, s, 0, :], pw[:, 0, bass.ds(t, 1)], xt, ALU.mult, ALU.add)\
                        .then_inc(s_cm1, 1)
                    dve.wait_ge(s_cm1, n * T + t + 1)
                    v.scalar_tensor_tensor(xt, yg[:, s, 1, :], pw[:, 1, bass.ds(t, 1)], xt, ALU.mult, ALU.add)\
                        .then_inc(s_cmbd, 1)
                if n == 0:
                    dve.wait_ge(s_cmbd, HEAD + (i + 1) * U)
                    dve.sem_inc(s_turn_dve, 1)
                    statistics(dve, i)
            dve.wait_ge(s_cmbd, HEAD + (n + 1) * T)

        block = ctx.enter_context(nc.Block())

        @block.sync
        def _(sp):
            for m in s_hst + s_ys:
                sp.sem_inc(m, HEAD_DMA)
            for n, a in enumerate((src, dst, etype)):
                sp.dma_start(edge_col[n].bitcast(I32), a.rearrange("(p c) -> p c", p=P)).then_inc(s_edge, 16)
            sp.dma_start(x[:, :, :], x_v).then_inc(s_xin, 16)
            sp.wait_ge(s_zero, 2)
            sp.dma_start(rec_v, unused).then_inc(s_zr, 16)
            for k in range(KC):
                sp.dma_start(wcat[:, k, 0:R * D].rearrange("p (r n) -> p r n", r=R),
                             w0.rearrange("r (k p) n -> k p r n", p=128)[k]).then_inc(s_w0, 16)
                sp.dma_start(wcat[:, k, R * D:], wl0.rearrange("(k p) n -> k p n", p=128)[k]).then_inc(s_w0, 16)
                sp.dma_start(wq0[:, k, :], wqkv0.rearrange("(k p) n -> k p n", p=128)[k]).then_inc(s_w0, 16)
                sp.dma_start(wg[:, 0, k, :], f0_wg.rearrange("(k p) n -> k p n", p=128)[k]).then_inc(s_par, 16)
                sp.dma_start(wg[:, 1, k, :], f1_wr.rearrange("(k p) n -> k p n", p=128)[k]).then_inc(s_par, 16)
            sp.dma_start(gpre[:, :], gpre0.rearrange("(k p) -> p k", p=128), allow_slow_non_contiguous=True).then_inc(s_par, 16)
            for h in range(4):
                sp.dma_start(memk[:, 32 * h:32 * h + 32], memkv[0, h].rearrange("d m -> m d"), allow_slow_non_contiguous=True).then_inc(s_par, 16)
                sp.dma_start(memv[:, 32 * h:32 * h + 32], memkv[1, h].rearrange("d m -> m d"), allow_slow_non_contiguous=True).then_inc(s_par, 16)
            sp.dma_start(wo0[:, :], wout0).then_inc(s_par, 16)
            for n, a in enumerate((hb0, bout0, gout0, biases[0], biases[1], bout1)):
                sp.dma_start(bc[:, n, :], row(a)).then_inc(s_par, 16)
            for n in range(2):
                sp.dma_start(compb[:, n, :], row(comps[n].rearrange("r b -> (r b)"))).then_inc(s_par, 16)
            for n, a in enumerate((f0_bg, f0_bias, f1_br)):
                sp.dma_start(gatb[:, n, :], row(a, P)).then_inc(s_par, 16)
            for n in range(SLOTS // 4):
                sp.dma_start(xs_z[n], zeros).then_inc(s_zd, 16)

            hx_store(sp, "gnn0")
            for z in range(2):
                sp.wait_ge(s_sct[z], 16 * SCU * (EC // (2 * SCU)))
            sp.dma_start(recs[:, :, :], rec_v).then_inc(s_recl, 16)
            sp.wait_ge(s_bn, 2 * TI + 1)
            gnn_weights_sp(sp, 0)
            for k in range(KC):
                sp.dma_start(wkv[:, k, :], wqkv1.rearrange("(k p) n -> k p n", p=128)[k][:, 512:1536]).then_inc(s_wm, 16)
            moe_sp(sp, 0)
            sp.wait_ge(s_cmbd, HEAD + T)
            for k in range(KC):
                sp.dma_start(wq1[:, k, :], wqkv1.rearrange("(k p) n -> k p n", p=128)[k][:, 0:512]).then_inc(s_wm, 16)
            sp.dma_start(wo1, wout1.rearrange("(j p) n -> p j n", p=128)).then_inc(s_wm, 16)
            hx_store(sp, "gnn1")
            sp.wait_ge(s_v2p, 9)
            gnn_weights_sp(sp, 1)
            hx_store(sp, "gnn2")
            moe_sp(sp, 1)
            for n in range(TI):
                sp.wait_ge(s_cmbd, HEAD + T + U * (n + 1))
                sp.dma_start(out_v[:, U * n:U * (n + 1), :], x[:, U * n:U * (n + 1), :]).then_inc(s_out, 16)
            sp.wait_ge(s_out, 16 * TI)


        @block.gpsimd
        def _(pool):
            ch = Chain(pool, s_pool)
            g = nc.gpsimd
            ch.step(g.memset(zeros, 0.0))
            ch.step(g.memset(unused, 0))
            ch.wait()
            ch.step(g.memset(unused[:, :, 1:2].bitcast(F32), -1.0))
            ch.step(g.memset(unused[:, :, 3:4].bitcast(F32), -1.0))
            ch.wait()
            g.memset(ident[:, :], 0.0).then_inc(s_zero, 2)
            ch.step(g.memset(ones[:, :], 1.0))
            ch.step(g.memset(tri[:, :], 1.0))
            ch.step(g.memset(bmask[:, :], 32 ** -0.5))
            ch.step(g.memset(bmask1[:, :], 1.0 / NODES))
            ch.step(g.memset(ltm[:, :, :], 1.0))
            ch.step(g.memset(memv[:, 128:129], 1.0))
            ch.wait()
            pool.wait_ge(s_zero, 2)
            ch.step(g.affine_select(out=ident[:, :], in_=ident[:, :], compare_op=ALU.not_equal, fill=1.0,
                                    base=0, pattern=[[-1, 128]], channel_multiplier=1))
            ch.step(g.affine_select(out=tri[:, :], in_=tri[:, :], compare_op=ALU.is_gt, fill=0.0,
                                    base=0, pattern=[[1, 128]], channel_multiplier=-1))
            ch.step(g.affine_select(out=ltm[:, :, :], in_=ltm[:, :, :], compare_op=ALU.is_gt, fill=0.0,
                                    base=0, pattern=[[1, NE], [-1, NE]], channel_multiplier=0))
            for m, b in ((bmask, 32), (bmask1, 64)):
                v = m[:, :].rearrange("p (a c) -> p a c", c=b)
                ch(g.affine_select(out=v, in_=v, compare_op=ALU.is_ge, fill=0.0, base=0,
                                   pattern=[[-b, 128 // b], [0, b]], channel_multiplier=1))
                ch(g.affine_select(out=v, in_=v, compare_op=ALU.is_ge, fill=0.0, base=b - 1,
                                   pattern=[[b, 128 // b], [0, b]], channel_multiplier=-1))
            ch.step(g.iota(iota[:, :], [[1, GROUPS + GU]], base=0, channel_multiplier=0,
                           allow_small_or_imprecise_dtypes=True))
            ch.wait()
            g.memset(dstl[:, COLS:], -1.0).then_inc(s_const, 1)
            ch(g.memset(typ[:, COLS:], -1.0))
            g.memset(inv[:, COLS:], 0.0).then_inc(s_const, 1)
            pool.wait_ge(s_pos, 1)
            pool.wait_ge(s_zr, 16)
            def scatter(i, first):
                for z in range(2):
                    c = i * 2 * SCU + z * SCU
                    if not first:
                        pool.wait_ge(s_sct[z], 16 * SCU * i)
                    g.tensor_copy(scix[:, z, :], posi[:, bass.ds(c, SCU)]).then_inc(s_cst, 1)
                    g.tensor_copy(scrc[:, z, :, :], rec[:, bass.ds(c, SCU), :]).then_inc(s_cst, 1)
                    pool.wait_ge(s_cst, 4 * i + 2 * z + 2)
                    pool.sem_inc(s_turn, 1)
                    for m in range(SCU):
                        g.indirect_dma_start(rec_d, bass.IndirectOffsetOnAxis(scix[:, z, m:m + 1], axis=0),
                                             scrc[:, z, m, :], None).then_inc(s_sct[z], 16)

            scatter(0, True)
            with pool.Fori(1, EC // (2 * SCU)) as i:
                scatter(i, False)
            pool.wait_ge(s_srt, 1)
            hx_done(pool, "gnn0")
            gather_pool(pool, 0)
            dispatch_pool(pool, 0)
            combine_pool(pool, 0)
            hx_done(pool, "gnn1")
            gather_pool(pool, 1)
            hx_done(pool, "gnn2")
            gather_pool(pool, 2)
            dispatch_pool(pool, 1)
            combine_pool(pool, 1)


        @block.tensor
        def _(pe):
            for m in [s_trn, s_blk, s_sg, s_dt, s_iP, s_ktr, s_kmm, s_mh] + s_my:
                pe.sem_inc(m, HEAD)
            pe.wait_ge(s_const, 2)

            def done(ins):
                ins.then_inc(s_q, 1)

            prefix_pe(pe, T, 1)
            pe.wait_ge(s_w0, 16 * 3 * KC)
            pe.wait_ge(s_v2p, 2)
            pass_pe(pe, "gnn0")
            pe.wait_ge(s_v2p, 3)
            nc.tensor.transpose(pb[7][:, 0:P], kmx, ident[0:P, 0:P])
            done(nc.tensor.transpose(pb[7][:, P:P + 4], memk[:, :], ident[0:4, 0:4]))
            pe.wait_ge(s_v2p, 4)
            done(nc.tensor.matmul(pb[6][:, 0:128], ones[:, :], dg, start=True, stop=True))
            pe.wait_ge(s_a2v, 2)
            for t in range(T):
                nc.tensor.matmul(pb[7][:, 0:129], tmp[:, t, 128:256], vv[:, t, :], start=(t == 0), stop=False)
            done(nc.tensor.matmul(pb[7][:, 0:129], memk[:, :], memv[:, :], start=False, stop=True))
            pe.wait_ge(s_v2p, 5)
            done(nc.tensor.transpose(pb[6][:, 0:128], ctxs, ident[:, :]))
            pe.wait_ge(s_v2p, 6)
            done(nc.tensor.matmul(pb[6][:, 0:D], ctxT, wo0[:, :], start=True, stop=True))
            pe.wait_ge(s_v2p, 7)
            pass_pe(pe, "mix0")
            gather_pe(pe, 0)
            pass_pe(pe, "gate0")
            prefix_pe(pe, NE, 8)
            moe_pe(pe, 0)
            pass_pe(pe, "gnn1", weights=0)
            pe.wait_ge(s_v2p, 9)
            for j in range(4):
                pe.wait_ge(s_eva[j], HEAD + NEVQ("gnn1", j))
            nc.tensor.matmul(pb[6][:, :], zer[:, 0:128], zer[:, :], start=True, stop=True, skip_group_check=True)\
                .then_inc(s_dot, 1)
            gather_pe(pe, 1)
            nc.tensor.matmul(pb[5][:, 0:8], zer[:, 0:128], zer[:, 0:8], start=True, stop=True).then_inc(s_dot, 1)
            pe.wait_ge(s_v2p, 10)
            pass_pe(pe, "gnn2", weights=4)
            for j in range(4):
                pe.wait_ge(s_eva[j], HEAD + NEVQ("gnn2", j))
            for j in range(4):
                done(nc.tensor.matmul(pb[j // 2][:, D * (j % 2):D * (j % 2 + 1)], dT[:, j, :], wo1[:, j, :],
                                      start=True, stop=True))
            for k in range(KC):
                for j in range(4):
                    last = nc.tensor.transpose(pb[2 + k][:, 128 * j:128 * (j + 1)],
                                               wq1[:, k, 128 * j:128 * (j + 1)], ident[:, :])
                done(last)
            pe.wait_ge(s_v2p, 11)
            for k in range(KC):
                for j in range(4):
                    last = nc.tensor.matmul(pb[4][:, D * k:D * (k + 1)], wqT[:, k, j, :], M1[:, j, :],
                                            start=(j == 0), stop=(j == 3))
                done(last)
            pe.wait_ge(s_v2p, 12)
            gather_pe(pe, 2)
            pass_pe(pe, "gate1")
            prefix_pe(pe, NE, 13)
            moe_pe(pe, 1)


        @block.scalar
        def _(act):
            ac = nc.scalar

            def square(src_, dst_):
                ac.activation(dst_, src_, ACT.Square).then_inc(s_sq, 1)

            for m in (s_xT, s_eva[1], s_eva[3], s_ma, s_kev):
                act.sem_inc(m, HEAD)
            RA = [0]

            def root(o, count=None):
                act.wait_ge(s_rsv, (RA[0] if count is None else count) + 1)
                ac.activation(o, o, ACT.Sqrt).then_inc(s_rsa, 1)
                if count is None:
                    RA[0] += 1

            def normed(n):
                return lambda i: act.wait_ge(s_ln, n * T + (i + 1) * U)

            def tsrc(a):
                return lambda t: a[:, bass.ds(t, 1), :].rearrange("p a d -> p (a d)")

            root(va)
            act.wait_ge(s_ln, T)
            square(xn[:, :, :], tmp)
            root(r0)
            pass_act(act, "gnn0", tsrc(xn), hx_copy(act, "gnn0", lambda o, i: ac.activation(o, i, ACT.Copy)))
            act.wait_ge(s_v2a, 1)
            ac.activation(tmp[:, :, 0:128], tmp[:, :, 0:128], ACT.Exp).then_inc(s_a2v, 1)
            act.wait_ge(s_v2a, 2)
            ac.activation(memk[:, :], memk[:, :], ACT.Exp)
            ac.activation(tmp[:, :, 128:256], tmp[:, :, 128:256], ACT.Exp).then_inc(s_a2v, 1)
            act.wait_ge(s_v2p, 7)
            act.wait_ge(s_v2a, 3)
            pass_act(act, "mix0", lambda t: tmp[:, bass.ds(t, 1), 0:128].rearrange("p a d -> p (a d)"))
            act.wait_ge(s_v2a, 4)
            square(tmp, xn[:, :, :])
            root(va)
            root(va)
            pass_act(act, "gate0", tsrc(xn), ready=normed(1))
            moe_act(act, 0)
            root(va)
            pass_act(act, "gnn1", tsrc(xn), hx_copy(act, "gnn1", lambda o, i: ac.activation(o, i, ACT.Copy)),
                     ready=normed(2))

            hx_done(act, "gnn1")
            act.wait_ge(s_v2p, 9)
            gather_act(act, 1)
            act.wait_ge(s_acc, HEAD + 2 * GROUPS)
            pass_act(act, "gnn2", tsrc(acc), hx_copy(act, "gnn2", lambda o, i: ac.activation(o, i, ACT.Copy)),
                     ACT.Relu)
            gather_act(act, 2)
            root(va)
            pass_act(act, "gate1", tsrc(xn), ready=normed(3))
            moe_act(act, 1)


        @block.vector
        def _(dve):
            ch = Chain(dve, s_vec)
            v = nc.vector

            def bt(a, n):
                return a.unsqueeze(2).to_broadcast([a.shape[0], a.shape[1], n])

            def btm(a, n):
                return a.unsqueeze(1).to_broadcast([a.shape[0], n, a.shape[1]])

            RS = [0]

            def rsq(o, scale, eps, lo=None, mul=1.0, count=None):
                k = RS[0] if count is None else count
                if lo is None:
                    v.tensor_scalar(o, o, scale, eps, ALU.mult, ALU.add).then_inc(s_rsv, 1)
                else:
                    v.tensor_scalar(o, o, lo, None, ALU.max).then_inc(s_rsv, 1)
                dve.wait_ge(s_rsa, k + 1)
                ch(v.reciprocal(o, o))
                if mul != 1.0:
                    ch(v.tensor_scalar(o, o, mul, None, ALU.mult))
                if count is None:
                    RS[0] += 1

            def ln(n, counted=False):
                if not counted:
                    with dve.Fori(0, TI) as i:
                        statistics(dve, i)
                dve.wait_ge(s_bn, (TI + 1) * n + TI)
                for t in range(T):
                    last = v.bn_aggr(mv[:, t, :], bst[:, t, :])
                last.then_inc(s_bn, 1)
                dve.wait_ge(s_bn, (TI + 1) * (n + 1))
                ch(v.tensor_copy(va, mv[:, :, 1]))
                rsq(va, 1.0, EPS)
                normalise(dve, n)(0)
                if n == 0:
                    with dve.Fori(1, TI) as i:
                        normalise(dve, n)(i)
                    dve.wait_ge(s_ln, T)

            for m in [s_eva[0], s_eva[2], s_eva[4], s_eva[5], s_acc, s_mx, s_cmbd, s_kss, s_kkk] + s_mo:
                dve.sem_inc(m, HEAD)
            dve.wait_ge(s_edge, 48)
            dve.wait_ge(s_const, 2)
            dst_f, typ_f, bin_f, posf, t1, t2, gof = edge_col[3], edge_col[4], edge_col[5], edge_col[6], edge_col[7], edge_col[8], edge_col[1]
            ch.step(v.tensor_copy(dst_f, edge_col[1].bitcast(I32)))
            ch.step(v.tensor_copy(typ_f, edge_col[2].bitcast(I32)))
            ch(v.tensor_copy(t2, edge_col[0].bitcast(I32)))
            ch(v.tensor_scalar(t1.bitcast(I32), dst_f, 4195.0, None, ALU.mult))
            ch(v.tensor_scalar(t1.bitcast(I32), t1.bitcast(I32), 19, None, ALU.arith_shift_right))
            ch(v.tensor_copy(bin_f, t1.bitcast(I32)))
            ch.step(v.scalar_tensor_tensor(rec[:, :, 0], typ_f, float(NODES), t2, ALU.mult, ALU.add))
            ch.step(v.scalar_tensor_tensor(rec[:, :, 1].bitcast(F32), bin_f, -float(P), dst_f, ALU.mult, ALU.add))
            ch.step(v.tensor_copy(rec[:, :, 2].bitcast(F32), typ_f))
            ch.step(v.tensor_copy(rec[:, :, 3].bitcast(F32), typ_f))
            one_c = t2
            ch.wait()
            ch(v.memset(one_c, 1.0))
            S0, S1 = edge_col[0], edge_col[1]
            spare = [edge_col[0], edge_col[1], edge_col[2], edge_col[7], edge_col[6]]
            with dve.Fori(0, TI) as i:
                ch.loop(i, U)
                for s in range(U):
                    b = i * U + s
                    if s == 0:
                        ch.wait()
                    ch.step(v.tensor_scalar(spare[s], bin_f, iota[0:P, bass.ds(b, 1)], 0.0, ALU.is_equal, ALU.add,
                                            accum_out=tot[:, bass.ds(b, 1)]))
            ch.end(TI, U)
            ch.wait()
            prefix(dve, ch, T, GROUP, 8, 1)
            masks, counts = [edge_col[2].bitcast(I32), edge_col[7].bitcast(I32)], [edge_col[1], edge_col[0]]
            with dve.Fori(0, TI) as i:
                ch.loop(i, 3 * U)
                done = ch.n

                def mask(s, need):
                    if need is not None:
                        dve.wait_ge(s_vec, done + need)
                    ch.step(v.tensor_scalar(masks[s % 2], bin_f, iota[0:P, bass.ds(i * U + s, 1)], None, ALU.is_equal))

                def count(s, need):
                    dve.wait_ge(s_vec, done + need)
                    ch.step(v.tensor_tensor_scan(counts[s % 2], one_c, masks[s % 2], off[:, bass.ds(i * U + s, 1)],
                                                 ALU.mult, ALU.add))

                def place(s, need):
                    dve.wait_ge(s_vec, done + need)
                    dve.sem_inc(s_turn_dve, 1)
                    ch.step(v.copy_predicated(posf, masks[s % 2], counts[s % 2]))

                for s in (0, 2):
                    mask(s, 3 * s)
                    mask(s + 1, 3 * s)
                    count(s, 3 * s + 1)
                    count(s + 1, 3 * s + 2)
                    place(s, 3 * s + 3)
                    place(s + 1, 3 * s + 5)
                mask(4, 12)
                count(4, 13)
                place(4, 14)
            ch.end(TI, 3 * U)
            ch.wait()
            ch(v.tensor_scalar(posf, posf, -1.0, None, ALU.add))
            ch(v.tensor_copy(posi, posf))
            ch(v.tensor_scalar(S0.bitcast(I32), posi, 7, None, ALU.arith_shift_right))
            ch(v.tensor_copy(S1, S0.bitcast(I32)))
            ch(v.scalar_tensor_tensor(posf, S1, -128.0, posf, ALU.mult, ALU.add))
            ch(v.scalar_tensor_tensor(posf, posf, float(COLS), S1, ALU.mult, ALU.add))
            ch(v.tensor_copy(posi, posf))
            dve.sem_inc(s_pos, 1)
            g0, g1 = S0[0:1, 0:GROUPS + GU], S1[0:1, 0:GROUPS + GU]
            ch(v.memset(g0, 0.0))
            for b in range(1, T):
                ch(v.tensor_scalar(g1, iota[0:1, 0:GROUPS + GU], bs[0:1, b:b + 1], None, ALU.is_ge))
                ch(v.tensor_tensor(g0, g0, g1, ALU.add))
            ch(v.tensor_copy(binr[:, :], g0))

            dve.wait_ge(s_xin, 16)
            dve.wait_ge(s_zr, 16)
            ln(0)
            dve.wait_ge(s_par, 16 * 25)
            dve.wait_ge(s_w0, 16 * 3 * KC)
            for k in range(KC):
                last = v.tensor_scalar(wq0[:, k, :], wq0[:, k, :], gpre[:, k:k + 1], None, ALU.mult)
                last.then_inc(s_vw, 1)
            dve.wait_ge(s_sq, 1)
            ch(v.tensor_reduce(r0, tmp, X, ALU.add))
            rsq(r0, 1.0, 0.0, 1e-24, D ** 0.5)
            dve.wait_ge(s_vw, KC)

            dve.wait_ge(s_zd, 16 * (SLOTS // 4))
            v.memset(vv[:, :, 128:129], 1.0).then_inc(s_v2p, 1)

            def gnn_evac(name, bias=None, qkv=False):
                hx = hx_copy(dve, name, v.tensor_copy)
                n = HSTN[name]

                def evac(e, i, s, j):
                    t = i * U + s
                    if j < 4:
                        return hx(e, i, s, j)
                    at = acc[:, bass.ds(t, 1), :].rearrange("p a d -> p (a d)")
                    if j == 4:
                        b = bc[0:P, bias, :] if bias is not None else None
                        if b is None:
                            v.tensor_scalar(at, pb[4][0:P, 0:D], 1.0, None, ALU.mult).then_inc(s_eva[4], 1)
                        else:
                            v.tensor_tensor(at, pb[4][0:P, 0:D], b, ALU.add).then_inc(s_eva[4], 1)
                        return
                    v.tensor_scalar(tmp[:, bass.ds(t, 1), :].rearrange("p a d -> p (a d)"), pb[5][0:P, 0:D],
                                    r0[:, bass.ds(t, 1)], None, ALU.mult)
                    v.tensor_scalar(vv[:, bass.ds(t, 1), 0:128].rearrange("p a d -> p (a d)"), pb[5][0:P, D:384],
                                    r0[:, bass.ds(t, 1)], None, ALU.mult).then_inc(s_eva[5], 1)
                return evac

            pass_dve(dve, "gnn0", gnn_evac("gnn0"))
            dve.wait_ge(s_eva[5], HEAD + T)
            qv = tmp[:, :, 0:128].rearrange("p t (h d) -> p t h d", d=32)
            kv = tmp[:, :, 128:256]
            q4 = qs.rearrange("p (t h) -> p t h", h=4)
            q4b = q4.unsqueeze(3).to_broadcast([P, T, 4, 32])
            v.tensor_reduce(kmx, kv.rearrange("p t c -> p c t"), X, ALU.max).then_inc(s_v2p, 1)
            ch(v.tensor_reduce(q4, qv, X, ALU.max))
            v.tensor_tensor(qv, qv, q4b, ALU.subtract).then_inc(s_v2a, 1)
            dve.wait_ge(s_q, 2)
            ch(v.tensor_reduce(mcol, pb[7][:, 0:P + 4], X, ALU.max))
            v.tensor_scalar(dg, ident[:, :], mcol, None, ALU.mult).then_inc(s_v2p, 1)
            dve.wait_ge(s_q, 3)
            v.tensor_tensor(memk[:, :], memk[:, :], pb[6][0:4, 0:128], ALU.subtract)
            v.tensor_tensor(kv, kv, btm(pb[6][0:P, 0:128], T), ALU.subtract).then_inc(s_v2a, 1)
            dve.wait_ge(s_a2v, 1)
            ch(v.tensor_reduce(q4, qv, X, ALU.add))
            ch(v.reciprocal(qs, qs))
            v.tensor_tensor(qv, qv, q4b, ALU.mult).then_inc(s_v2a, 1)
            dve.wait_ge(s_q, 4)
            ch(v.reciprocal(rden, pb[7][:, 128:129]))
            v.scalar_tensor_tensor(ctxs, pb[7][:, 0:128], rden, bmask[:, :], ALU.mult, ALU.mult).then_inc(s_v2p, 1)
            dve.wait_ge(s_q, 5)
            v.tensor_copy(ctxT, pb[6][:, 0:128]).then_inc(s_v2p, 1)
            dve.wait_ge(s_q, 6)
            v.tensor_copy(M0, pb[6][:, 0:D]).then_inc(s_v2p, 1)

            def mix0_evac(e, i, s, j):
                v.tensor_tensor(tmp[:, bass.ds(i * U + s, 1), :].rearrange("p a d -> p (a d)"), pb[0][0:P, 0:D],
                                bc[0:P, 1, :], ALU.add).then_inc(s_eva[0], 1)
            ch(v.tensor_tensor(x[:, :, :], x[:, :, :], xn[:, :, :], ALU.add))
            pass_dve(dve, "mix0", mix0_evac)
            dve.wait_ge(s_eva[0], HEAD + NEVQ("mix0"))
            dve.sem_inc(s_v2a, 1)
            dve.wait_ge(s_sq, 2)
            ch(v.tensor_reduce(va, xn[:, :, :], X, ALU.add))
            rsq(va, 1.0, 0.0, 1e-24, D ** 0.5)
            ch(v.tensor_tensor(tmp, tmp, bt(va, D), ALU.mult))
            ch(v.tensor_tensor(tmp, tmp, btm(bc[0:P, 2, :], T), ALU.mult))
            ch(v.tensor_tensor(x[:, :, :], x[:, :, :], tmp, ALU.add))
            ch(v.tensor_tensor(x[:, :, :], x[:, :, :], btm(bc[0:P, 0, :], T), ALU.add))
            dve.wait_ge(s_recl, 16)
            ch.step(v.tensor_copy(gid[:, :], recs[:, :, 0]))
            ch.step(v.tensor_copy(typ[:, 0:COLS], recs[:, :, 2].bitcast(F32)))
            ch.step(v.tensor_copy(dstl[:, 0:COLS], recs[:, :, 1].bitcast(F32)))
            ch.step(v.tensor_tensor(toh, recs[:, :, 3:4].bitcast(F32).to_broadcast([128, COLS, R]),
                                    btm(iota[:, 0:R], COLS), ALU.is_equal))
            ch.wait()
            v.memset(cnt[:, :, :], 0.0).then_inc(s_srt, 1)
            gather_dve(dve, 0)
            dve.wait_ge(s_acc, HEAD + GROUPS)
            ch(v.scalar_tensor_tensor(x[:, :, :], acc, 0.5 ** 0.5, x[:, :, :], ALU.mult, ALU.add))
            ch(v.tensor_scalar(cnt[:, :, :], cnt[:, :, :], 1.0, None, ALU.max))
            ch(v.reciprocal(cnt[:, :, :], cnt[:, :, :]))
            ln(1)
            moe_dve(dve, ch, 0)
            ln(2, counted=True)
            pass_dve(dve, "gnn1", gnn_evac("gnn1", bias=3), normalise(dve, 2))
            dve.wait_ge(s_eva[4], HEAD + PASSES["gnn2"]["ev"][4])
            dve.wait_ge(s_wm, 16 * (2 * KC + 1))
            ch(v.memset(zer, 0.0))
            dve.sem_inc(s_v2p, 1)
            ch(v.tensor_tensor(bc[0:P, 4, :], bc[0:P, 4, :], bc[0:P, 5, :], ALU.add))
            dve.wait_ge(s_dot, 1)
            gather_dve(dve, 1)
            dve.wait_ge(s_acc, HEAD + 2 * GROUPS)
            dve.wait_ge(s_dot, 2)
            v.tensor_tensor(dT[:, :, :], pb[6][:, :].rearrange("p (j c) -> p j c", j=4), btm(bmask1[:, :], 4), ALU.mult)\
                .then_inc(s_v2p, 1)
            relation_weights(dve, ch, 1)
            pass_dve(dve, "gnn2", gnn_evac("gnn2", bias=4))
            dve.wait_ge(s_eva[4], HEAD + NEV[4])
            dve.wait_ge(s_q, 7 + 6)
            for j in range(2):
                ch.step(v.tensor_copy(M1[:, 2 * j:2 * j + 2, :], pb[j][:, :].rearrange("p (a d) -> p a d", d=D)))
            ch.step(v.tensor_copy(wqT[:, 0], pb[2][:, :].rearrange("p (j c) -> p j c", j=4)))
            ch.wait()
            v.tensor_copy(wqT[:, 1], pb[3][:, :].rearrange("p (j c) -> p j c", j=4)).then_inc(s_v2p, 1)
            dve.wait_ge(s_q, 7 + 8)
            v.tensor_copy(P1v, pb[4][:, :].rearrange("p (k d) -> p k d", d=D)).then_inc(s_v2p, 1)
            gather_dve(dve, 2)
            dve.wait_ge(s_acc, HEAD + 3 * GROUPS)
            ch(v.tensor_tensor(x[:, :, :], x[:, :, :], acc, ALU.add))
            ln(3)
            moe_dve(dve, ch, 1)


_INS = ['x', 'src', 'dst', 'edge_type_8', 'L0_gnn_weight', 'L0_gnn_h_bias', 'L0_gnn_loop_weight', 'L0_mix_t',
        'L0_mix_w_qkv', 'L0_mix_mem_kv', 'L0_mix_w_out', 'L0_mix_b_out', 'L0_mix_g_out', 'L0_mix_g_pre',
        'L0_ffn_Wg', 'L0_ffn_bg', 'L0_ffn_bias', 'L0_ffn_W1', 'L0_ffn_b1', 'L0_ffn_W2', 'L0_ffn_b2',
        'L1_gnn_comps', 'L1_gnn_bases', 'L1_gnn_roots', 'L1_gnn_biases', 'L1_mix_w_qkv', 'L1_mix_w_out',
        'L1_mix_b_out', 'L1_ffn_Wr', 'L1_ffn_br', 'L1_ffn_ln_g', 'L1_ffn_ln_b', 'L1_ffn_W1', 'L1_ffn_b1',
        'L1_ffn_W2', 'L1_ffn_b2']


def kernel(**inputs):
    import numpy as _np
    import concourse.bacc as _bacc
    from concourse import mybir as _mybir
    from concourse.bass_utils import run_bass_kernel_spmd as _run

    nc = _bacc.Bacc("TRN2", target_bir_lowering=False, num_devices=1)
    arrays, args = {}, []
    for name in _INS:
        a = _np.ascontiguousarray(inputs[name])
        arrays[f"in_{name}_dram"] = a
        args.append(nc.dram_tensor(f"in_{name}_dram", a.shape, _mybir.dt.from_np(a.dtype), kind="ExternalInput").ap())
    args.append(nc.dram_tensor("out_dram", (3125, 256), _mybir.dt.float32, kind="ExternalOutput").ap())
    gps_block(nc, *args)
    r = _run(nc, [arrays], core_ids=[0])
    return r.results[0]["out_dram"]
```
